# Optimizing a Trainium2 kernel written in Bass

```python
import numpy as np
import jax
import jax.numpy as jnp

def _softmax(x, axis=-1):
    return jax.nn.softmax(x, axis=axis)

def _gelu(x):
    return jax.nn.gelu(x, approximate=True)

def _silu(x):
    return jax.nn.silu(x)

def _sigmoid(x):
    return jax.nn.sigmoid(x)

def _layernorm(x, axis=-1, eps=1e-05):
    m = jnp.mean(x, axis=axis, keepdims=True)
    v = jnp.var(x, axis=axis, keepdims=True)
    return (x - m) / jnp.sqrt(v + eps)

def _scatter_add(tgt, idx, src, axis=0):
    return tgt.at[idx].add(src)

def _segment_sum(src, seg, n):
    return jax.ops.segment_sum(src, seg, n)
kernel_name = 'mk_seq_postln_d4_jaxref_r8_7d17a3'

def setup_inputs(seed: int=0):
    np.random.seed(seed)
    _w = jnp.asarray

    def _L0_attn_setup():
        import jax, jax.numpy as jnp
        import numpy as np
        D_MODEL = 128
        N_HEADS = 16
        D_LATENT = 32
        HEAD_DIM = D_MODEL // N_HEADS

        def apply_rope(x):
            B, T, H, D = x.shape
            inv_freq = 1.0 / 10000.0 ** (jnp.arange(0, D, 2, dtype=jnp.float32) / D)
            t = jnp.arange(T, dtype=jnp.float32)
            freqs = t[:, None] * inv_freq[None, :]
            sin_f = jnp.sin(freqs)[None, :, None, :]
            cos_f = jnp.cos(freqs)[None, :, None, :]
            x1, x2 = jnp.split(x, 2, axis=-1)
            return jnp.concatenate([x1 * cos_f - x2 * sin_f, x1 * sin_f + x2 * cos_f], axis=-1)
        key = jax.random.key(seed)
        ks = jax.random.split(key, 10)
        B, T = (4, 512)
        s = lambda fan_in: 1.0 / np.sqrt(fan_in)
        return {'x': jax.random.normal(ks[0], (B, T, D_MODEL), dtype=jnp.float32), 'Wq': jax.random.normal(ks[1], (D_MODEL, D_MODEL), dtype=jnp.float32) * s(D_MODEL), 'bq': jnp.zeros((D_MODEL,), jnp.float32), 'Wdown': jax.random.normal(ks[2], (D_MODEL, D_LATENT), dtype=jnp.float32) * s(D_MODEL), 'bdown': jnp.zeros((D_LATENT,), jnp.float32), 'Wup': jax.random.normal(ks[3], (D_LATENT, 2 * D_MODEL), dtype=jnp.float32) * s(D_LATENT), 'bup': jnp.zeros((2 * D_MODEL,), jnp.float32), 'Wout': jax.random.normal(ks[4], (D_MODEL, D_MODEL), dtype=jnp.float32) * s(D_MODEL), 'bout': jnp.zeros((D_MODEL,), jnp.float32)}
    _L0_attn_in = _L0_attn_setup()

    def _L0_ffn_setup():
        import jax, jax.numpy as jnp
        import numpy as np
        B, S, D = (2, 128, 128)
        E, H, K, G = (8, 256, 2, 32)
        key = jax.random.key(seed)
        ks = jax.random.split(key, 5)
        return {'x': jax.random.normal(ks[0], (B, S, D), jnp.float32), 'wg1': jax.random.normal(ks[1], (D, G), jnp.float32) * 0.02, 'bg1': jnp.zeros((G,), jnp.float32), 'wg2': jax.random.normal(ks[2], (G, E), jnp.float32) * 0.02, 'w_in': jax.random.uniform(ks[3], (E, D, H), jnp.float32, -1.0 / D, 1.0 / D), 'w_out': jax.random.uniform(ks[4], (E, H, D), jnp.float32, -1.0 / H, 1.0 / H)}
    _L0_ffn_in = _L0_ffn_setup()

    def _L1_attn_setup():
        import jax, jax.numpy as jnp
        import numpy as np
        B, S, D = (2, 256, 128)
        H, DH = (16, 64)
        DQL, DKVL = (64, 64)
        DR = 64
        TOPK = 64
        LN_EPS = 1e-05
        ROPE_BASE = 10000.0

        def _rope_tables(seq_len, dim):
            inv_freq = 1.0 / ROPE_BASE ** (np.arange(0, dim, 2, dtype=np.float32) / dim)
            t = np.arange(seq_len, dtype=np.float32)
            freqs = np.outer(t, inv_freq)
            cos = np.concatenate([np.cos(freqs), np.cos(freqs)], -1)[:, ::2]
            sin = np.concatenate([np.sin(freqs), np.sin(freqs)], -1)[:, ::2]
            return (jnp.asarray(cos), jnp.asarray(sin))

        def _apply_rope_subspace(x, d_rope):
            s = x.shape[-2]
            cos, sin = _rope_tables(s, d_rope)
            xr, xp = (x[..., :d_rope], x[..., d_rope:])
            e, o = (xr[..., 0::2], xr[..., 1::2])
            rot = jnp.stack([e * cos - o * sin, e * sin + o * cos], axis=-1).reshape(xr.shape)
            return jnp.concatenate([rot, xp], axis=-1)

        def _reference_tuple_inner(x, w_down_q, w_down_kv, w_up_q, w_up_k, w_up_v, w_out, ln_scale, ln_bias):
            b, s, d = x.shape
            residual = x
            mu = jnp.mean(x, axis=-1, keepdims=True)
            var = jnp.mean((x - mu) ** 2, axis=-1, keepdims=True)
            h = (x - mu) * jax.lax.rsqrt(var + LN_EPS) * ln_scale + ln_bias
            c_q = h @ w_down_q.T
            c_kv = h @ w_down_kv.T
            q = (c_q @ w_up_q.T).reshape(b, s, H, DH).transpose(0, 2, 1, 3)
            k = (c_kv @ w_up_k.T).reshape(b, s, H, DH).transpose(0, 2, 1, 3)
            v = (c_kv @ w_up_v.T).reshape(b, s, H, DH).transpose(0, 2, 1, 3)
            q = _apply_rope_subspace(q, DR)
            k = _apply_rope_subspace(k, DR)
            scale = 1.0 / np.sqrt(DH).astype(np.float32)
            scores = jnp.einsum('bhqd,bhkd->bhqk', q, k) * scale
            _, indices = jax.lax.top_k(scores, min(TOPK, s))
            attn = jax.nn.softmax(scores, axis=-1)
            out = jnp.einsum('bhqk,bhkd->bhqd', attn, v)
            out = out.transpose(0, 2, 1, 3).reshape(b, s, H * DH)
            out = out @ w_out.T + residual
            return (out, indices.astype(jnp.int64))
        key = jax.random.key(seed)
        ks = jax.random.split(key, 7)
        init = lambda k, shape: jax.random.normal(k, shape, jnp.float32) * 0.02
        return {'x': jax.random.normal(ks[0], (B, S, D), jnp.float32), 'w_down_q': init(ks[1], (DQL, D)), 'w_down_kv': init(ks[2], (DKVL, D)), 'w_up_q': init(ks[3], (H * DH, DQL)), 'w_up_k': init(ks[4], (H * DH, DKVL)), 'w_up_v': init(ks[5], (H * DH, DKVL)), 'w_out': init(ks[6], (D, H * DH)), 'ln_scale': jnp.ones((D,), jnp.float32), 'ln_bias': jnp.zeros((D,), jnp.float32)}
    _L1_attn_in = _L1_attn_setup()

    def _L1_ffn_setup():
        import jax, jax.numpy as jnp
        import numpy as np
        B, T, C = (2, 128, 128)
        H = 512
        E_R, E_S, K = (8, 2, 2)

        def _rmsnorm(x, g):
            eps = jnp.finfo(x.dtype).eps
            return x * jax.lax.rsqrt(jnp.mean(x * x, axis=-1, keepdims=True) + eps) * g

        def _experts_mlp(x, g, W1, b1, W2, b2):
            xn = _rmsnorm(x, g)
            h = jnp.einsum('btc,ech->bteh', xn, W1) + b1
            h = jax.nn.gelu(h, approximate=False)
            return jnp.einsum('bteh,ehc->btec', h, W2) + b2
        key = jax.random.key(seed)
        ks = jax.random.split(key, 12)
        s = 0.02
        return {'u': jax.random.normal(ks[0], (B, T, C), dtype=jnp.float32), 'g_shared': jnp.ones((C,), jnp.float32), 'W1_s': jax.random.normal(ks[1], (E_S, C, H), jnp.float32) * s, 'b1_s': jax.random.normal(ks[2], (E_S, H), jnp.float32) * s, 'W2_s': jax.random.normal(ks[3], (E_S, H, C), jnp.float32) * s, 'b2_s': jax.random.normal(ks[4], (E_S, C), jnp.float32) * s, 'g_routed': jnp.ones((C,), jnp.float32), 'W1_r': jax.random.normal(ks[5], (E_R, C, H), jnp.float32) * s, 'b1_r': jax.random.normal(ks[6], (E_R, H), jnp.float32) * s, 'W2_r': jax.random.normal(ks[7], (E_R, H, C), jnp.float32) * s, 'b2_r': jax.random.normal(ks[8], (E_R, C), jnp.float32) * s, 'centroids': jax.random.normal(ks[9], (C, E_R), jnp.float32) * s}
    _L1_ffn_in = _L1_ffn_setup()

    def _L2_attn_setup():
        import jax, jax.numpy as jnp
        import numpy as np
        D_MODEL, D_STATE, D_CONV, EXPAND = (128, 16, 4, 2)
        D_INNER = EXPAND * D_MODEL
        DT_RANK = (D_MODEL + 15) // 16
        B_SZ, SEQLEN = (2, 256)

        def _mamba_fwd(hidden_states, in_proj_w, conv_w, conv_b, x_proj_w, dt_proj_w, dt_proj_b, A_log, D, out_proj_w):
            B, L, _ = hidden_states.shape
            silu = jax.nn.silu
            xz = jnp.einsum('bld,ed->bel', hidden_states, in_proj_w)
            x, z = (xz[:, :D_INNER, :], xz[:, D_INNER:, :])
            x_pad = jnp.pad(x, ((0, 0), (0, 0), (D_CONV - 1, 0)))
            xc = sum((conv_w[None, :, k, None] * x_pad[:, :, k:k + L] for k in range(D_CONV)))
            x = silu(xc + conv_b[None, :, None])
            xt = jnp.swapaxes(x, 1, 2)
            x_dbl = jnp.einsum('bld,ed->ble', xt, x_proj_w)
            dt_lo = x_dbl[..., :DT_RANK]
            Bm = x_dbl[..., DT_RANK:DT_RANK + D_STATE]
            Cm = x_dbl[..., DT_RANK + D_STATE:]
            delta = jax.nn.softplus(jnp.einsum('blr,dr->bld', dt_lo, dt_proj_w) + dt_proj_b)
            A = -jnp.exp(A_log.astype(jnp.float32))

            def step(h, inp):
                d_t, B_t, C_t, x_t = inp
                dA = jnp.exp(d_t[..., None] * A)
                h = dA * h + (d_t * x_t)[..., None] * B_t[:, None, :]
                y = jnp.einsum('bdn,bn->bd', h, C_t)
                return (h, y)
            h0 = jnp.zeros((B, D_INNER, D_STATE), dtype=jnp.float32)
            xs = (jnp.swapaxes(delta, 0, 1), jnp.swapaxes(Bm, 0, 1), jnp.swapaxes(Cm, 0, 1), jnp.swapaxes(xt, 0, 1))
            _, ys = jax.lax.scan(step, h0, xs)
            y = jnp.swapaxes(ys, 0, 1) + D * xt
            y = y * silu(jnp.swapaxes(z, 1, 2))
            return jnp.einsum('bld,md->blm', y, out_proj_w)
        key = jax.random.key(seed)
        ks = jax.random.split(key, 10)
        import math
        dt = jnp.exp(jax.random.uniform(ks[8], (D_INNER,)) * (math.log(0.1) - math.log(0.001)) + math.log(0.001))
        dt = jnp.clip(dt, 0.0001, None)
        inv_dt = dt + jnp.log(-jnp.expm1(-dt))
        A_log = jnp.log(jnp.tile(jnp.arange(1, D_STATE + 1, dtype=jnp.float32)[None, :], (D_INNER, 1)))
        s = lambda k, shp, scale: jax.random.normal(k, shp, dtype=jnp.float32) * scale
        return {'hidden_states': jax.random.normal(ks[0], (B_SZ, SEQLEN, D_MODEL), dtype=jnp.float32), 'in_proj_w': s(ks[1], (2 * D_INNER, D_MODEL), D_MODEL ** (-0.5)), 'conv_w': s(ks[2], (D_INNER, D_CONV), D_CONV ** (-0.5)), 'conv_b': s(ks[3], (D_INNER,), 0.02), 'x_proj_w': s(ks[4], (DT_RANK + 2 * D_STATE, D_INNER), D_INNER ** (-0.5)), 'dt_proj_w': jax.random.uniform(ks[5], (D_INNER, DT_RANK), minval=-DT_RANK ** (-0.5), maxval=DT_RANK ** (-0.5)), 'dt_proj_b': inv_dt, 'A_log': A_log, 'D': jnp.ones((D_INNER,), dtype=jnp.float32), 'out_proj_w': s(ks[6], (D_MODEL, D_INNER), D_INNER ** (-0.5))}
    _L2_attn_in = _L2_attn_setup()

    def _L2_ffn_setup():
        import jax, jax.numpy as jnp
        import numpy as np
        D_MODEL = 128
        N_EXPERTS = 8
        TOP_K = 2
        HIDDEN = 4 * D_MODEL
        key = jax.random.key(seed)
        ks = jax.random.split(key, 6)
        B, S = (2, 256)
        x = jax.random.normal(ks[0], (B, S, D_MODEL), dtype=jnp.float32)
        shared_w1 = jax.random.normal(ks[1], (HIDDEN, D_MODEL), dtype=jnp.float32) * 0.02
        shared_w2 = jax.random.normal(ks[2], (D_MODEL, HIDDEN), dtype=jnp.float32) * 0.02
        experts_w1 = jax.random.normal(ks[3], (N_EXPERTS, HIDDEN, D_MODEL), dtype=jnp.float32) * 0.02
        experts_w2 = jax.random.normal(ks[4], (N_EXPERTS, D_MODEL, HIDDEN), dtype=jnp.float32) * 0.02
        gate_w = jax.random.normal(ks[5], (N_EXPERTS, D_MODEL), dtype=jnp.float32) * 0.02
        return {'x': x, 'shared_w1': shared_w1, 'shared_w2': shared_w2, 'experts_w1': experts_w1, 'experts_w2': experts_w2, 'gate_w': gate_w}
    _L2_ffn_in = _L2_ffn_setup()

    def _L3_attn_setup():
        import jax, jax.numpy as jnp
        import numpy as np
        N_EMBD = 128
        N_HEAD = 16
        HEAD_SIZE = N_EMBD // N_HEAD
        WINDOW = 3

        def _shift(a, j):
            if j == 0:
                return a
            return jnp.pad(a, ((0, 0), (0, 0), (j, 0), (0, 0)))[:, :, :-j, :]
        key = jax.random.key(seed)
        ks = jax.random.split(key, 9)
        C = N_EMBD
        s = 1.0 / np.sqrt(C)
        x = jax.random.normal(ks[0], (8, 512, C), dtype=jnp.float32)
        Wq = jax.random.uniform(ks[1], (C, C), jnp.float32, -s, s)
        Wk = jax.random.uniform(ks[2], (C, C), jnp.float32, -s, s)
        Wv = jax.random.uniform(ks[3], (C, C), jnp.float32, -s, s)
        Wo = jax.random.uniform(ks[4], (C, C), jnp.float32, -s, s)
        bq = jax.random.uniform(ks[5], (C,), jnp.float32, -s, s)
        bk = jax.random.uniform(ks[6], (C,), jnp.float32, -s, s)
        bv = jax.random.uniform(ks[7], (C,), jnp.float32, -s, s)
        bo = jax.random.uniform(ks[8], (C,), jnp.float32, -s, s)
        return {'x': x, 'Wq': Wq, 'bq': bq, 'Wk': Wk, 'bk': bk, 'Wv': Wv, 'bv': bv, 'Wo': Wo, 'bo': bo}
    _L3_attn_in = _L3_attn_setup()

    def _L3_ffn_setup():
        import jax, jax.numpy as jnp
        import numpy as np
        BLOCK = 16
        _GRID = jnp.array([0.0, 0.5, 1.0, 1.5, 2.0, 3.0, 4.0, 6.0], dtype=jnp.float32)
        _MID = jnp.array([0.25, 0.75, 1.25, 1.75, 2.5, 3.5, 5.0], dtype=jnp.float32)

        def fp4_quant_dequant(x):
            shape = x.shape
            xb = x.reshape(shape[:-1] + (shape[-1] // BLOCK, BLOCK))
            scale = jnp.max(jnp.abs(xb), axis=-1, keepdims=True) / 6.0
            scale = jnp.maximum(scale, jnp.float32(1e-12))
            xn = xb / scale
            idx = jnp.searchsorted(_MID, jnp.abs(xn))
            q = _GRID[idx] * jnp.sign(xn) * scale
            return q.reshape(shape)

        def fp4_linear(x, w):
            xq = fp4_quant_dequant(x)
            wq = fp4_quant_dequant(w)
            return jnp.einsum('bsk,nk->bsn', xq, wq)
        key = jax.random.key(seed)
        k1, k2, k3, k4 = jax.random.split(key, 4)
        H, I = (128, 352)
        x = jax.random.normal(k1, (4, 512, H), dtype=jnp.float32)
        w_gate = jax.random.normal(k2, (I, H), dtype=jnp.float32) * 0.02
        w_up = jax.random.normal(k3, (I, H), dtype=jnp.float32) * 0.02
        w_down = jax.random.normal(k4, (H, I), dtype=jnp.float32) * 0.02
        return {'x': x, 'w_gate': w_gate, 'w_up': w_up, 'w_down': w_down}
    _L3_ffn_in = _L3_ffn_setup()
    _d = {'L0_attn_x': _L0_attn_in['x'], 'L0_attn_Wq': _L0_attn_in['Wq'], 'L0_attn_bq': _L0_attn_in['bq'], 'L0_attn_Wdown': _L0_attn_in['Wdown'], 'L0_attn_bdown': _L0_attn_in['bdown'], 'L0_attn_Wup': _L0_attn_in['Wup'], 'L0_attn_bup': _L0_attn_in['bup'], 'L0_attn_Wout': _L0_attn_in['Wout'], 'L0_attn_bout': _L0_attn_in['bout'], 'L0_ffn_wg1': _L0_ffn_in['wg1'], 'L0_ffn_bg1': _L0_ffn_in['bg1'], 'L0_ffn_wg2': _L0_ffn_in['wg2'], 'L0_ffn_w_in': _L0_ffn_in['w_in'], 'L0_ffn_w_out': _L0_ffn_in['w_out'], 'L1_attn_w_down_q': _L1_attn_in['w_down_q'], 'L1_attn_w_down_kv': _L1_attn_in['w_down_kv'], 'L1_attn_w_up_q': _L1_attn_in['w_up_q'], 'L1_attn_w_up_k': _L1_attn_in['w_up_k'], 'L1_attn_w_up_v': _L1_attn_in['w_up_v'], 'L1_attn_w_out': _L1_attn_in['w_out'], 'L1_attn_ln_scale': _L1_attn_in['ln_scale'], 'L1_attn_ln_bias': _L1_attn_in['ln_bias'], 'L1_ffn_g_shared': _L1_ffn_in['g_shared'], 'L1_ffn_W1_s': _L1_ffn_in['W1_s'], 'L1_ffn_b1_s': _L1_ffn_in['b1_s'], 'L1_ffn_W2_s': _L1_ffn_in['W2_s'], 'L1_ffn_b2_s': _L1_ffn_in['b2_s'], 'L1_ffn_g_routed': _L1_ffn_in['g_routed'], 'L1_ffn_W1_r': _L1_ffn_in['W1_r'], 'L1_ffn_b1_r': _L1_ffn_in['b1_r'], 'L1_ffn_W2_r': _L1_ffn_in['W2_r'], 'L1_ffn_b2_r': _L1_ffn_in['b2_r'], 'L1_ffn_centroids': _L1_ffn_in['centroids'], 'L2_attn_in_proj_w': _L2_attn_in['in_proj_w'], 'L2_attn_conv_w': _L2_attn_in['conv_w'], 'L2_attn_conv_b': _L2_attn_in['conv_b'], 'L2_attn_x_proj_w': _L2_attn_in['x_proj_w'], 'L2_attn_dt_proj_w': _L2_attn_in['dt_proj_w'], 'L2_attn_dt_proj_b': _L2_attn_in['dt_proj_b'], 'L2_attn_A_log': _L2_attn_in['A_log'], 'L2_attn_D': _L2_attn_in['D'], 'L2_attn_out_proj_w': _L2_attn_in['out_proj_w'], 'L2_ffn_shared_w1': _L2_ffn_in['shared_w1'], 'L2_ffn_shared_w2': _L2_ffn_in['shared_w2'], 'L2_ffn_experts_w1': _L2_ffn_in['experts_w1'], 'L2_ffn_experts_w2': _L2_ffn_in['experts_w2'], 'L2_ffn_gate_w': _L2_ffn_in['gate_w'], 'L3_attn_Wq': _L3_attn_in['Wq'], 'L3_attn_bq': _L3_attn_in['bq'], 'L3_attn_Wk': _L3_attn_in['Wk'], 'L3_attn_bk': _L3_attn_in['bk'], 'L3_attn_Wv': _L3_attn_in['Wv'], 'L3_attn_bv': _L3_attn_in['bv'], 'L3_attn_Wo': _L3_attn_in['Wo'], 'L3_attn_bo': _L3_attn_in['bo'], 'L3_ffn_w_gate': _L3_ffn_in['w_gate'], 'L3_ffn_w_up': _L3_ffn_in['w_up'], 'L3_ffn_w_down': _L3_ffn_in['w_down']}
    _x0 = _d['L0_attn_x']
    _d['L0_attn_x'] = jax.random.normal(jax.random.fold_in(jax.random.key(seed), 1), (16, 256, 128), dtype=_x0.dtype)
    del _x0
    return _d

def reference(L0_attn_x, L0_attn_Wq, L0_attn_bq, L0_attn_Wdown, L0_attn_bdown, L0_attn_Wup, L0_attn_bup, L0_attn_Wout, L0_attn_bout, L0_ffn_wg1, L0_ffn_bg1, L0_ffn_wg2, L0_ffn_w_in, L0_ffn_w_out, L1_attn_w_down_q, L1_attn_w_down_kv, L1_attn_w_up_q, L1_attn_w_up_k, L1_attn_w_up_v, L1_attn_w_out, L1_attn_ln_scale, L1_attn_ln_bias, L1_ffn_g_shared, L1_ffn_W1_s, L1_ffn_b1_s, L1_ffn_W2_s, L1_ffn_b2_s, L1_ffn_g_routed, L1_ffn_W1_r, L1_ffn_b1_r, L1_ffn_W2_r, L1_ffn_b2_r, L1_ffn_centroids, L2_attn_in_proj_w, L2_attn_conv_w, L2_attn_conv_b, L2_attn_x_proj_w, L2_attn_dt_proj_w, L2_attn_dt_proj_b, L2_attn_A_log, L2_attn_D, L2_attn_out_proj_w, L2_ffn_shared_w1, L2_ffn_shared_w2, L2_ffn_experts_w1, L2_ffn_experts_w2, L2_ffn_gate_w, L3_attn_Wq, L3_attn_bq, L3_attn_Wk, L3_attn_bk, L3_attn_Wv, L3_attn_bv, L3_attn_Wo, L3_attn_bo, L3_ffn_w_gate, L3_ffn_w_up, L3_ffn_w_down):

    def _L0_attn_ref(x, Wq, bq, Wdown, bdown, Wup, bup, Wout, bout):
        import jax, jax.numpy as jnp
        import numpy as np
        D_MODEL = 128
        N_HEADS = 16
        D_LATENT = 32
        HEAD_DIM = D_MODEL // N_HEADS

        def apply_rope(x):
            B, T, H, D = x.shape
            inv_freq = 1.0 / 10000.0 ** (jnp.arange(0, D, 2, dtype=jnp.float32) / D)
            t = jnp.arange(T, dtype=jnp.float32)
            freqs = t[:, None] * inv_freq[None, :]
            sin_f = jnp.sin(freqs)[None, :, None, :]
            cos_f = jnp.cos(freqs)[None, :, None, :]
            x1, x2 = jnp.split(x, 2, axis=-1)
            return jnp.concatenate([x1 * cos_f - x2 * sin_f, x1 * sin_f + x2 * cos_f], axis=-1)
        B, T, D = x.shape
        H, Dh = (N_HEADS, HEAD_DIM)
        q = x @ Wq + bq
        kv_latent = x @ Wdown + bdown
        kv = kv_latent @ Wup + bup
        q = q.reshape(B, T, H, Dh)
        kv = kv.reshape(B, T, H, 2 * Dh)
        k, v = jnp.split(kv, 2, axis=-1)
        q = apply_rope(q)
        k = apply_rope(k)
        att = jnp.einsum('bthd,btgd->bthg', q, k) / jnp.sqrt(jnp.float32(Dh))
        att = jax.nn.softmax(att, axis=-1)
        out = jnp.einsum('bthg,btgd->bthd', att, v)
        out = out.reshape(B, T, D)
        return out @ Wout + bout

    def _L0_ffn_ref(x, wg1, bg1, wg2, w_in, w_out):
        import jax, jax.numpy as jnp
        import numpy as np
        B, S, D = (2, 128, 128)
        E, H, K, G = (8, 256, 2, 32)
        b, s, d = x.shape
        xt = x.reshape(-1, d)
        n = xt.shape[0]
        g = jax.nn.gelu(xt @ wg1 + bg1, approximate=False)
        logits = g @ wg2
        probs = jax.nn.softmax(logits, axis=-1)
        top_vals, top_idx = jax.lax.top_k(probs, K)
        gates = jnp.zeros_like(probs).at[jnp.arange(n)[:, None], top_idx].set(top_vals)
        h = jax.nn.gelu(jnp.einsum('nd,edh->enh', xt, w_in), approximate=False)
        o = jnp.einsum('enh,ehd->end', h, w_out)
        y = jnp.einsum('ne,end->nd', gates, o)
        return y.reshape(b, s, d)

    def _L1_attn_ref(x, w_down_q, w_down_kv, w_up_q, w_up_k, w_up_v, w_out, ln_scale, ln_bias):
        import jax, jax.numpy as jnp
        import numpy as np
        B, S, D = (2, 256, 128)
        H, DH = (16, 64)
        DQL, DKVL = (64, 64)
        DR = 64
        TOPK = 64
        LN_EPS = 1e-05
        ROPE_BASE = 10000.0

        def _rope_tables(seq_len, dim):
            inv_freq = 1.0 / ROPE_BASE ** (np.arange(0, dim, 2, dtype=np.float32) / dim)
            t = np.arange(seq_len, dtype=np.float32)
            freqs = np.outer(t, inv_freq)
            cos = np.concatenate([np.cos(freqs), np.cos(freqs)], -1)[:, ::2]
            sin = np.concatenate([np.sin(freqs), np.sin(freqs)], -1)[:, ::2]
            return (jnp.asarray(cos), jnp.asarray(sin))

        def _apply_rope_subspace(x, d_rope):
            s = x.shape[-2]
            cos, sin = _rope_tables(s, d_rope)
            xr, xp = (x[..., :d_rope], x[..., d_rope:])
            e, o = (xr[..., 0::2], xr[..., 1::2])
            rot = jnp.stack([e * cos - o * sin, e * sin + o * cos], axis=-1).reshape(xr.shape)
            return jnp.concatenate([rot, xp], axis=-1)

        def _reference_tuple_inner(x, w_down_q, w_down_kv, w_up_q, w_up_k, w_up_v, w_out, ln_scale, ln_bias):
            b, s, d = x.shape
            residual = x
            mu = jnp.mean(x, axis=-1, keepdims=True)
            var = jnp.mean((x - mu) ** 2, axis=-1, keepdims=True)
            h = (x - mu) * jax.lax.rsqrt(var + LN_EPS) * ln_scale + ln_bias
            c_q = h @ w_down_q.T
            c_kv = h @ w_down_kv.T
            q = (c_q @ w_up_q.T).reshape(b, s, H, DH).transpose(0, 2, 1, 3)
            k = (c_kv @ w_up_k.T).reshape(b, s, H, DH).transpose(0, 2, 1, 3)
            v = (c_kv @ w_up_v.T).reshape(b, s, H, DH).transpose(0, 2, 1, 3)
            q = _apply_rope_subspace(q, DR)
            k = _apply_rope_subspace(k, DR)
            scale = 1.0 / np.sqrt(DH).astype(np.float32)
            scores = jnp.einsum('bhqd,bhkd->bhqk', q, k) * scale
            _, indices = jax.lax.top_k(scores, min(TOPK, s))
            attn = jax.nn.softmax(scores, axis=-1)
            out = jnp.einsum('bhqk,bhkd->bhqd', attn, v)
            out = out.transpose(0, 2, 1, 3).reshape(b, s, H * DH)
            out = out @ w_out.T + residual
            return (out, indices.astype(jnp.int64))
        return _reference_tuple_inner(x, w_down_q, w_down_kv, w_up_q, w_up_k, w_up_v, w_out, ln_scale, ln_bias)[0]

    def _L1_ffn_ref(u, g_shared, W1_s, b1_s, W2_s, b2_s, g_routed, W1_r, b1_r, W2_r, b2_r, centroids):
        import jax, jax.numpy as jnp
        import numpy as np
        B, T, C = (2, 128, 128)
        H = 512
        E_R, E_S, K = (8, 2, 2)

        def _rmsnorm(x, g):
            eps = jnp.finfo(x.dtype).eps
            return x * jax.lax.rsqrt(jnp.mean(x * x, axis=-1, keepdims=True) + eps) * g

        def _experts_mlp(x, g, W1, b1, W2, b2):
            xn = _rmsnorm(x, g)
            h = jnp.einsum('btc,ech->bteh', xn, W1) + b1
            h = jax.nn.gelu(h, approximate=False)
            return jnp.einsum('bteh,ehc->btec', h, W2) + b2
        h_s = _experts_mlp(u, g_shared, W1_s, b1_s, W2_s, b2_s).sum(axis=-2)
        scores = jax.nn.sigmoid(u @ centroids)
        gpk, i_topk = jax.lax.top_k(scores, K)
        gk = gpk / scores.sum(axis=-1, keepdims=True)
        routed_all = _experts_mlp(u, g_routed, W1_r, b1_r, W2_r, b2_r)
        routed_topk = jnp.take_along_axis(routed_all, i_topk[..., None], axis=2)
        h_r = (gk[..., None] * routed_topk).sum(axis=-2)
        return u + h_s + h_r

    def _L2_attn_ref(hidden_states, in_proj_w, conv_w, conv_b, x_proj_w, dt_proj_w, dt_proj_b, A_log, D, out_proj_w):
        import jax, jax.numpy as jnp
        import numpy as np
        D_MODEL, D_STATE, D_CONV, EXPAND = (128, 16, 4, 2)
        D_INNER = EXPAND * D_MODEL
        DT_RANK = (D_MODEL + 15) // 16
        B_SZ, SEQLEN = (2, 256)

        def _mamba_fwd(hidden_states, in_proj_w, conv_w, conv_b, x_proj_w, dt_proj_w, dt_proj_b, A_log, D, out_proj_w):
            B, L, _ = hidden_states.shape
            silu = jax.nn.silu
            xz = jnp.einsum('bld,ed->bel', hidden_states, in_proj_w)
            x, z = (xz[:, :D_INNER, :], xz[:, D_INNER:, :])
            x_pad = jnp.pad(x, ((0, 0), (0, 0), (D_CONV - 1, 0)))
            xc = sum((conv_w[None, :, k, None] * x_pad[:, :, k:k + L] for k in range(D_CONV)))
            x = silu(xc + conv_b[None, :, None])
            xt = jnp.swapaxes(x, 1, 2)
            x_dbl = jnp.einsum('bld,ed->ble', xt, x_proj_w)
            dt_lo = x_dbl[..., :DT_RANK]
            Bm = x_dbl[..., DT_RANK:DT_RANK + D_STATE]
            Cm = x_dbl[..., DT_RANK + D_STATE:]
            delta = jax.nn.softplus(jnp.einsum('blr,dr->bld', dt_lo, dt_proj_w) + dt_proj_b)
            A = -jnp.exp(A_log.astype(jnp.float32))

            def step(h, inp):
                d_t, B_t, C_t, x_t = inp
                dA = jnp.exp(d_t[..., None] * A)
                h = dA * h + (d_t * x_t)[..., None] * B_t[:, None, :]
                y = jnp.einsum('bdn,bn->bd', h, C_t)
                return (h, y)
            h0 = jnp.zeros((B, D_INNER, D_STATE), dtype=jnp.float32)
            xs = (jnp.swapaxes(delta, 0, 1), jnp.swapaxes(Bm, 0, 1), jnp.swapaxes(Cm, 0, 1), jnp.swapaxes(xt, 0, 1))
            _, ys = jax.lax.scan(step, h0, xs)
            y = jnp.swapaxes(ys, 0, 1) + D * xt
            y = y * silu(jnp.swapaxes(z, 1, 2))
            return jnp.einsum('bld,md->blm', y, out_proj_w)
        return _mamba_fwd(hidden_states, in_proj_w, conv_w, conv_b, x_proj_w, dt_proj_w, dt_proj_b, A_log, D, out_proj_w)

    def _L2_ffn_ref(x, shared_w1, shared_w2, experts_w1, experts_w2, gate_w):
        import jax, jax.numpy as jnp
        import numpy as np
        D_MODEL = 128
        N_EXPERTS = 8
        TOP_K = 2
        HIDDEN = 4 * D_MODEL
        B, S, D = x.shape
        T = B * S
        x_flat = x.reshape(T, D)
        shared = jnp.einsum('td,dh->th', x_flat, shared_w1.T)
        shared = jnp.einsum('th,hd->td', jax.nn.silu(shared), shared_w2.T)
        gate_logits = x_flat @ gate_w.T
        top_k_gates, top_k_idx = jax.lax.top_k(gate_logits, TOP_K)
        top_k_gates = jax.nn.softmax(top_k_gates, axis=1)
        gates = jnp.zeros((T, N_EXPERTS), dtype=x.dtype)
        gates = gates.at[jnp.arange(T)[:, None], top_k_idx].set(top_k_gates)
        h = jnp.einsum('td,ehd->teh', x_flat, experts_w1)
        expert_out = jnp.einsum('teh,edh->ted', jax.nn.silu(h), experts_w2)
        selected = jnp.einsum('ted,te->td', expert_out, gates)
        return (shared + selected).reshape(B, S, D)

    def _L3_attn_ref(x, Wq, bq, Wk, bk, Wv, bv, Wo, bo):
        import jax, jax.numpy as jnp
        import numpy as np
        N_EMBD = 128
        N_HEAD = 16
        HEAD_SIZE = N_EMBD // N_HEAD
        WINDOW = 3

        def _shift(a, j):
            if j == 0:
                return a
            return jnp.pad(a, ((0, 0), (0, 0), (j, 0), (0, 0)))[:, :, :-j, :]
        B, T, C = x.shape
        H, d = (N_HEAD, HEAD_SIZE)
        scale = 1.0 / np.sqrt(d)
        q = (x @ Wq.T + bq).reshape(B, T, H, d).transpose(0, 2, 1, 3)
        k = (x @ Wk.T + bk).reshape(B, T, H, d).transpose(0, 2, 1, 3)
        v = (x @ Wv.T + bv).reshape(B, T, H, d).transpose(0, 2, 1, 3)
        scores = jnp.stack([jnp.einsum('bhtd,bhtd->bht', q, _shift(k, j)) * scale for j in range(WINDOW)], axis=-1)
        valid = jnp.arange(T)[:, None] >= jnp.arange(WINDOW)[None, :]
        scores = jnp.where(valid[None, None], scores, -jnp.inf)
        att = jax.nn.softmax(scores, axis=-1)
        y = sum((att[..., j:j + 1] * _shift(v, j) for j in range(WINDOW)))
        y = y.transpose(0, 2, 1, 3).reshape(B, T, C)
        return y @ Wo.T + bo

    def _L3_ffn_ref(x, w_gate, w_up, w_down):
        import jax, jax.numpy as jnp
        import numpy as np
        BLOCK = 16
        _GRID = jnp.array([0.0, 0.5, 1.0, 1.5, 2.0, 3.0, 4.0, 6.0], dtype=jnp.float32)
        _MID = jnp.array([0.25, 0.75, 1.25, 1.75, 2.5, 3.5, 5.0], dtype=jnp.float32)

        def fp4_quant_dequant(x):
            shape = x.shape
            xb = x.reshape(shape[:-1] + (shape[-1] // BLOCK, BLOCK))
            scale = jnp.max(jnp.abs(xb), axis=-1, keepdims=True) / 6.0
            scale = jnp.maximum(scale, jnp.float32(1e-12))
            xn = xb / scale
            idx = jnp.searchsorted(_MID, jnp.abs(xn))
            q = _GRID[idx] * jnp.sign(xn) * scale
            return q.reshape(shape)

        def fp4_linear(x, w):
            xq = fp4_quant_dequant(x)
            wq = fp4_quant_dequant(w)
            return jnp.einsum('bsk,nk->bsn', xq, wq)
        gate = fp4_linear(x, w_gate)
        y = fp4_linear(x, w_up)
        h = jax.nn.silu(gate) * y
        return fp4_linear(h, w_down)
    x = L0_attn_x
    x = _layernorm(x + _L0_attn_ref(x, L0_attn_Wq, L0_attn_bq, L0_attn_Wdown, L0_attn_bdown, L0_attn_Wup, L0_attn_bup, L0_attn_Wout, L0_attn_bout), axis=-1)
    x = _layernorm(x + _L0_ffn_ref(x, L0_ffn_wg1, L0_ffn_bg1, L0_ffn_wg2, L0_ffn_w_in, L0_ffn_w_out), axis=-1)
    x = _layernorm(x + _L1_attn_ref(x, L1_attn_w_down_q, L1_attn_w_down_kv, L1_attn_w_up_q, L1_attn_w_up_k, L1_attn_w_up_v, L1_attn_w_out, L1_attn_ln_scale, L1_attn_ln_bias), axis=-1)
    x = _layernorm(x + _L1_ffn_ref(x, L1_ffn_g_shared, L1_ffn_W1_s, L1_ffn_b1_s, L1_ffn_W2_s, L1_ffn_b2_s, L1_ffn_g_routed, L1_ffn_W1_r, L1_ffn_b1_r, L1_ffn_W2_r, L1_ffn_b2_r, L1_ffn_centroids), axis=-1)
    x = _layernorm(x + _L2_attn_ref(x, L2_attn_in_proj_w, L2_attn_conv_w, L2_attn_conv_b, L2_attn_x_proj_w, L2_attn_dt_proj_w, L2_attn_dt_proj_b, L2_attn_A_log, L2_attn_D, L2_attn_out_proj_w), axis=-1)
    x = _layernorm(x + _L2_ffn_ref(x, L2_ffn_shared_w1, L2_ffn_shared_w2, L2_ffn_experts_w1, L2_ffn_experts_w2, L2_ffn_gate_w), axis=-1)
    x = _layernorm(x + _L3_attn_ref(x, L3_attn_Wq, L3_attn_bq, L3_attn_Wk, L3_attn_bk, L3_attn_Wv, L3_attn_bv, L3_attn_Wo, L3_attn_bo), axis=-1)
    x = _layernorm(x + _L3_ffn_ref(x, L3_ffn_w_gate, L3_ffn_w_up, L3_ffn_w_down), axis=-1)
    return x

_drawn_inputs = setup_inputs


def setup_inputs(seed=0):
    import zlib

    import numpy as np

    out = dict(_drawn_inputs(seed))
    spreads = {'L0_attn_bq': (0.0, 0.271),
     'L0_attn_bdown': (0.0, 0.1),
     'L0_attn_bup': (0.0, 0.1),
     'L0_attn_bout': (0.0, 0.1),
     'L0_ffn_bg1': (0.0, 0.8),
     'L1_attn_ln_scale': (1.0, 0.6),
     'L1_attn_ln_bias': (0.0, 0.8),
     'L1_ffn_g_shared': (1.0, 0.6),
     'L1_ffn_g_routed': (1.0, 0.6),
     'L2_attn_D': (1.0, 0.2)}
    factors = {'L0_ffn_wg1': 8.0,
     'L0_ffn_wg2': 8.0,
     'L0_ffn_w_in': 8.0,
     'L0_ffn_w_out': 8.0,
     'L1_attn_w_down_q': 8.0,
     'L1_attn_w_down_kv': 8.0,
     'L1_attn_w_up_q': 8.0,
     'L1_attn_w_up_k': 8.0,
     'L1_attn_w_up_v': 8.0,
     'L1_attn_w_out': 8.0,
     'L1_ffn_b1_s': 8.0,
     'L1_ffn_b2_s': 3.553,
     'L1_ffn_W1_r': 8.0,
     'L1_ffn_b1_r': 8.0,
     'L1_ffn_W2_r': 8.0,
     'L1_ffn_b2_r': 8.0,
     'L1_ffn_centroids': 8.0,
     'L2_attn_conv_b': 7.609,
     'L2_attn_dt_proj_w': 2.987,
     'L3_attn_bq': 8.0,
     'L3_attn_bk': 8.0,
     'L3_ffn_w_gate': 5.732,
     'L3_ffn_w_up': 5.58,
     'L3_ffn_w_down': 5.614}
    for name, (base, spread) in spreads.items():
        noise = np.random.default_rng([zlib.crc32(name.encode()), seed]).standard_normal(out[name].shape)
        drawn = base * np.exp(spread * noise) if base else spread * noise
        out[name] = jnp.asarray(drawn.astype(out[name].dtype))
    for name, factor in factors.items():
        out[name] = (out[name] * factor).astype(out[name].dtype)
    return out
```

```python
from contextlib import ExitStack

import concourse.bass as bass
from concourse import mybir

F32, F32R, BF16 = mybir.dt.float32, mybir.dt.float32r, mybir.dt.bfloat16
U32 = mybir.dt.uint32
ALU = mybir.AluOpType
ACT = mybir.ActivationFunctionType
AX = mybir.AxisListType

P = 128
B, T, D = 16, 256, 128
NTOK = B * T
NTILE = NTOK // P
LN_EPS = 1e-5
PHASES = (0, 8)


class Chain:

    def __init__(self, eng, sem, i, per):
        self.eng, self.sem, self.base, self.per, self.k = eng, sem, i * per, per, 0

    def __call__(self, ins):
        self.k += 1
        ins.then_inc(self.sem, 1)
        self.eng.wait_ge(self.sem, self.base + self.k)

    def close(self):
        assert self.k == self.per, f"this chain has {self.k} steps a turn, not {self.per}"


def mm3(nc, out, wh, wl, xh, xl, start=True, stop=True):
    nc.tensor.matmul(out, wh, xh, start=start, stop=False)
    nc.tensor.matmul(out, wl, xh, start=False, stop=False)
    return nc.tensor.matmul(out, wh, xl, start=False, stop=stop)


class Tail:

    def __init__(self, prog, c, tag, s, n, out_ps, turn_ps, gain=1.0, last=False):
        nc = self.nc = prog.nc
        self.prog, self.n, self.out_ps, self.turn_ps, self.gain, self.last = prog, n, out_ps, turn_ps, gain, last

        def sb(name, shape):
            return c.enter_context(nc.sbuf_tensor(f"{tag}_{name}{s}", shape, F32))

        def sem(name):
            return prog.semaphore(f"{tag}_{name}{s}")

        self.y, self.xn = sb("y", [P, n, D]), sb("xn", [P, n, D])
        self.st, self.mv, self.ve, self.rs = sb("st", [P, n, 6]), sb("mv", [P, n, 2]), sb("ve", [P, n]), sb("rs", [P, n])
        self.y_ps, self.ve_done, self.rs_done, self.xn_done = (sem("out_ready"), sem("var_ready"), sem("rstd_ready"),
                                                              sem("xn_ready"))
        self.xnt_ps, self.xh_kept, self.x_kept, self.done = sem("xnT_ready"), sem("xh_kept"), sem("x_kept"), sem("turn_done")
        if last:
            self.done = self.x_kept

    def dve(self, dve, link, i, seq):
        v, n, prog = self.nc.vector, self.n, self.prog
        dve.wait_ge(self.y_ps, i + 1)
        link(v.scalar_tensor_tensor(self.y[:], prog.X[:, bass.ds(seq * n, n), :], self.gain,
                                    self.out_ps.rearrange("p (c d) -> p c d", c=n), ALU.mult, ALU.add))
        prog.norm_stats(link, self.y, self.st, self.mv, self.ve[:], n, LN_EPS).then_inc(self.ve_done, 1)
        dve.wait_ge(self.rs_done, i + 1)
        for t in range(n):
            m = v.tensor_scalar(self.xn[:, t, :], self.y[:, t, :], self.mv[:, t, 0:1], self.rs[:, t:t + 1],
                                ALU.subtract, ALU.mult)
        m.then_inc(self.xn_done, 1)

    def dve_low(self, dve, i, seq):
        w = self.n * P
        dve.wait_ge(self.xh_kept, i + 1)
        dve.wait_ge(self.x_kept, i + 1)
        self.nc.vector.tensor_tensor(self.prog.XL[:, bass.ds(seq * w, w)], self.turn_ps,
                                     self.prog.XH[:, bass.ds(seq * w, w)].bitcast(F32),
                                     ALU.subtract).then_inc(self.done, 1)

    def pool(self, pool, i, seq):
        g, n = self.nc.gpsimd, self.n
        pool.wait_ge(self.ve_done, i + 1)
        g.tensor_tensor(self.rs[:], self.ve[:], self.prog.mhalf[:, 0:n], ALU.pow).then_inc(self.rs_done, 1)
        pool.wait_ge(self.xn_done, i + 1)
        g.tensor_copy(self.prog.X[:, bass.ds(seq * n, n), :], self.xn[:]).then_inc(self.x_kept, 1)

    def act(self, act, i, seq):
        w = self.n * P
        act.wait_ge(self.xnt_ps, i + 1)
        self.nc.scalar.activation(self.prog.XH[:, bass.ds(seq * w, w)], self.turn_ps, ACT.Copy).then_inc(self.xh_kept, 1)

    def pe(self, pe, i):
        pe.wait_ge(self.xn_done, i + 1)
        for t in range(self.n):
            m = self.nc.tensor.transpose(self.turn_ps[:, t * P:(t + 1) * P], self.xn[:, t, :], self.prog.idF[:])
        m.then_inc(self.xnt_ps, 1)


class Program:
    def __init__(self, nc, ins, out):
        self.nc, self.ins, self.out = nc, ins, out
        self.ctx, self.phase_sems = ExitStack(), []

    def build(self):
        nc = self.nc
        with self.ctx:
            c = self.ctx
            self.X = c.enter_context(nc.sbuf_tensor("X", [P, NTILE, D], F32))
            self.XH = c.enter_context(nc.sbuf_tensor("XH", [P, NTOK], F32R))
            self.XL = c.enter_context(nc.sbuf_tensor("XL", [P, NTOK], F32R))
            self.idF = c.enter_context(nc.sbuf_tensor("idF", [P, P], F32))
            self.idB = c.enter_context(nc.sbuf_tensor("idB", [P, P], BF16))
            self.mhalf = c.enter_context(nc.sbuf_tensor("mhalf", [P, 8], F32))
            self.pad = c.enter_context(nc.sbuf_tensor("pad", [P, 1], F32))
            self.ps = [c.enter_context(nc.psum_tensor(f"bank{i}", [P, 512], F32)) for i in range(8)]
            self.load_x()
            self.clear_semaphores()
            phases = [self.head_attention,
                      lambda: self.mixture("f0", "mlp", ACT.Gelu, 0, 2),
                      self.latent_attention,
                      lambda: self.mixture("f1", "sigmoid", ACT.Gelu, 2, 4, rms=True, biases=True),
                      self.selective_scan,
                      lambda: self.mixture("f2", "logits", ACT.Silu, 1, 4),
                      self.window_attention,
                      self.fp4_mlp]
            for f in phases[PHASES[0]:PHASES[1]]:
                f()
                self.clear_semaphores()
            self.store_x()

    def semaphore(self, name):
        self.phase_sems.append(self.nc.alloc_semaphore(name=name))
        return self.phase_sems[-1]

    def clear_semaphores(self):
        self.nc.clear_and_free_semaphores(self.phase_sems)
        self.nc.all_engine_barrier()
        self.phase_sems = []

    def load_x(self):
        nc = self.nc
        x_in, xh_done, const_in, fin0 = (self.semaphore(n) for n in ("x_in", "xh_done", "const_in", "x_low_done"))
        with nc.sbuf_tensor("xt_in", [P, NTOK], F32) as xt_in, nc.Block() as block:
            CH = NTOK // 4

            @block.sync
            def _(sp):
                for k in range(4):
                    sp.dma_start(xt_in[:, k * CH:(k + 1) * CH], self.ins["xt"][:, k * CH:(k + 1) * CH]).then_inc(x_in, 16)
                    sp.wait_ge(x_in, 16 * (k + 1))
                sp.dma_start(self.X[:], self.ins["x"].rearrange("(n p) d -> p n d", p=P)).then_inc(const_in, 16)
                sp.dma_start(self.idF[:], self.ins["ident"]).then_inc(const_in, 16)
                sp.wait_ge(const_in, 32)

            @block.scalar
            def _(act):
                for k in range(4):
                    act.wait_ge(x_in, 16 * (k + 1))
                    act.activation(self.XH[:, k * CH:(k + 1) * CH], xt_in[:, k * CH:(k + 1) * CH],
                                   ACT.Copy).then_inc(xh_done, 1)

            @block.vector
            def _(dve):
                dve.memset(self.mhalf[:], -0.5).then_inc(fin0, 1)
                for k in range(4):
                    dve.wait_ge(xh_done, k + 1)
                    s = slice(k * CH, (k + 1) * CH)
                    dve.tensor_tensor(self.XL[:, s], xt_in[:, s], self.XH[:, s].bitcast(F32), ALU.subtract).then_inc(fin0, 1)
                dve.wait_ge(const_in, 32)
                dve.tensor_copy(self.idB[:], self.idF[:]).then_inc(fin0, 1)
                dve.wait_ge(fin0, 6)

    def store_x(self):
        nc = self.nc
        out_done = self.semaphore("out_done")
        with nc.Block() as block:
            @block.sync
            def _(sp):
                sp.dma_start(self.out.rearrange("(n p) d -> p n d", p=P), self.X[:]).then_inc(out_done, 16)
                sp.wait_ge(out_done, 16)

    def norm_stats(self, link, y, st, mv, ve, n, eps):
        v = self.nc.vector
        for t in range(n):
            ins = v.bn_stats(st[:, t, :], y[:, t, :])
            if t == n - 1:
                link(ins)
        v.memset(self.pad[:], 0.0)
        for t in range(n):
            ins = v.bn_aggr(mv[:, t, :], st[:, t, :])
            if t == n - 1:
                link(ins)
        return v.tensor_scalar(ve, mv[:, :, 1], eps, None, ALU.add)

    def head_attention(self):
        nc, I, ps = self.nc, self.ins, self.ps
        H, DH, DL = 16, 8, 32
        SCALE = 1.0 / float(DH) ** 0.5
        KC = T // P
        PER_DVE = 17
        with ExitStack() as c:
            def sb(name, shape, dt=F32):
                return c.enter_context(nc.sbuf_tensor("a0_" + name, shape, dt))

            def sem(name):
                return self.semaphore("a0_" + name)

            NW = 2 * D + DL
            NU = 3 * D
            w_in, up_in = sb("w_in", [P, NW]), sb("up_in", [DL, NU])
            wh, wl = sb("wh", [P, NW], F32R), sb("wl", [P, NW], F32R)
            uh, ul = sb("uh", [DL, NU], F32R), sb("ul", [DL, NU], F32R)
            wout, bout, one_row = sb("wout", [P, D]), sb("bout", [1, D]), sb("one_row", [1, P])
            vec, cs = sb("vec", [P, 6]), sb("cs", [P, 2 * T])
            lat_h, lat_l = sb("lat_h", [DL, T], F32R), sb("lat_l", [DL, T], F32R)
            rope_t = sb("rope_t", [P, 4, T])
            qkv = sb("qkv", [P, 3, T])
            tok = sb("tok", [P, KC, 3, H, DH])
            prod, prod2 = sb("prod", [P, KC, H * H * DH]), sb("prod2", [P, KC, H * DH * H])
            s_ = sb("s", [P, KC, H, H])
            mx, pe_ = sb("mx", [P, KC, H]), sb("p", [P, KC, H, H])
            den, rec = sb("den", [P, KC, H]), sb("rec", [P, KC, H])
            o, on, ot = sb("o", [P, KC, H, DH]), sb("on", [P, KC, H, DH]), sb("ot", [P, T])
            y, xn = sb("y", [P, KC, D]), sb("xn", [P, KC, D])
            st, mv, ve, rs = sb("st", [P, KC, 6]), sb("mv", [P, KC, 2]), sb("ve", [P, KC]), sb("rs", [P, KC])

            loaded, split, low_split = sem("weights_loaded"), sem("weights_split"), sem("low_parts_ready")
            seq_done, proj_ps = sem("sequence_done"), sem("projections_ready")
            lat_split, lat_half, qkv_done = sem("latent_split"), sem("latent_high"), sem("qkv_ready")
            tok_ps, tok_kept, v_done = sem("token_major_ready"), sem("token_major_kept"), sem("v_ready")
            shifted, exp_done, prod2_done = sem("scores_shifted"), sem("exp_done"), sem("pv_products_ready")
            on_done, ont_ps, ont_kept, y_ps = sem("normalised"), sem("outT_ready"), sem("outT_kept"), sem("attn_out_ready")
            ve_done, rs_done, xn_done, xnt_ps = sem("var_ready"), sem("rstd_ready"), sem("xn_ready"), sem("xnT_ready")
            xh_kept, x_kept, dchain = sem("xh_kept"), sem("x_kept"), sem("dve_chain")
            block = c.enter_context(nc.Block())
            loads = ((w_in, "a0_w"), (up_in, "a0_up"), (wout, "a0_wout"), (bout, "a0_bout"), (vec, "a0_vec"),
                     (cs, "a0_cs"), (one_row, "one_row"))

            @block.sync
            def _(sp):
                for dst, src in loads:
                    sp.dma_start(dst[:], I[src]).then_inc(loaded, 16)

            @block.gpsimd
            def _(pool):
                with pool.Fori(0, B) as i:
                    for t in range(KC):
                        pool.wait_ge(exp_done, i * KC + t + 1)
                        nc.gpsimd.tensor_tensor(prod2[:, t, :].rearrange("p (h d g) -> p h d g", h=H, d=DH),
                                                pe_[:, t, :, :].unsqueeze(2).broadcast_to([P, H, DH, H]),
                                                tok[:, t, 2, :, :].rearrange("p g d -> p d g").unsqueeze(1)
                                                .broadcast_to([P, H, DH, H]), ALU.mult).then_inc(prod2_done, 1)
                    pool.wait_ge(ve_done, i + 1)
                    nc.gpsimd.tensor_tensor(rs[:], ve[:], self.mhalf[:, 0:KC], ALU.pow).then_inc(rs_done, 1)
                    pool.wait_ge(xn_done, i + 1)
                    nc.gpsimd.tensor_copy(self.X[:, bass.ds(i * KC, KC), :], xn[:]).then_inc(x_kept, 1)

            @block.scalar
            def _(act):
                act.wait_ge(loaded, 16 * len(loads))
                act.activation(wh[:], w_in[:], ACT.Copy).then_inc(split, 1)
                act.activation(uh[:], up_in[:], ACT.Copy).then_inc(split, 1)
                with act.Fori(0, B) as i:
                    act.wait_ge(proj_ps, i * 4 + 2)
                    act.activation(lat_h[:], ps[1][0:DL, 0:T], ACT.Identity, bias=vec[0:DL, 2:3]).then_inc(lat_half, 1)
                    act.wait_ge(proj_ps, i * 4 + 4)
                    act.activation(qkv[:, 2, :], ps[3][:, 0:T], ACT.Identity, bias=vec[:, 5:6]).then_inc(v_done, 1)
                    for t in range(KC):
                        act.wait_ge(tok_ps, i * KC + t + 1)
                        act.activation(tok[:, t, :, :, :].rearrange("p k h d -> p (k h d)"), ps[4 + t][:, 0:3 * D],
                                       ACT.Copy).then_inc(tok_kept, 1)
                    for t in range(KC):
                        act.wait_ge(shifted, i * KC + t + 1)
                        act.activation(pe_[:, t, :, :], s_[:, t, :, :], ACT.Exp, scale=SCALE).then_inc(exp_done, 1)
                    act.wait_ge(ont_ps, i + 1)
                    act.activation(ot[:], ps[6][:, 0:T], ACT.Copy).then_inc(ont_kept, 1)
                    act.wait_ge(xnt_ps, i + 1)
                    act.activation(self.XH[:, bass.ds(i * T, T)], ps[6][:, 0:T], ACT.Copy).then_inc(xh_kept, 1)

            @block.tensor
            def _(pe):
                pe.wait_ge(split, 2)
                pe.wait_ge(low_split, 2)
                with pe.Fori(0, B) as i:
                    pe.wait_ge(seq_done, i + 1)
                    xh, xl = self.XH[:, bass.ds(i * T, T)], self.XL[:, bass.ds(i * T, T)]
                    mm3(nc, ps[0][:, 0:T], wh[:, 0:D], wl[:, 0:D], xh, xl)
                    mm3(nc, ps[0][:, T:2 * T], wh[:, D:2 * D], wl[:, D:2 * D], xh, xl).then_inc(proj_ps, 1)
                    mm3(nc, ps[1][0:DL, 0:T], wh[:, 2 * D:NW], wl[:, 2 * D:NW], xh, xl).then_inc(proj_ps, 1)
                    pe.wait_ge(lat_split, i + 1)
                    for r, o_ in enumerate((ps[2][:, 0:T], ps[2][:, T:2 * T], ps[3][:, 0:T])):
                        m = mm3(nc, o_, uh[:, r * D:(r + 1) * D], ul[:, r * D:(r + 1) * D], lat_h[:], lat_l[:])
                        if r:
                            m.then_inc(proj_ps, 1)
                    pe.wait_ge(qkv_done, i + 1)
                    pe.wait_ge(v_done, i + 1)
                    for t in range(KC):
                        for k in range(3):
                            m = nc.tensor.transpose(ps[4 + t][:, k * D:(k + 1) * D], qkv[:, k, t * P:(t + 1) * P], self.idF[:])
                        m.then_inc(tok_ps, 1)
                    pe.wait_ge(on_done, i * KC + KC)
                    for t in range(KC):
                        m = nc.tensor.transpose(ps[6][:, t * P:(t + 1) * P],
                                                on[:, t, :, :].rearrange("p h d -> p (h d)"), self.idF[:])
                    m.then_inc(ont_ps, 1)
                    pe.wait_ge(ont_kept, i + 1)
                    for t in range(KC):
                        o_ = ps[7][:, t * P:(t + 1) * P]
                        nc.tensor.matmul(o_, ot[:, t * P:(t + 1) * P], wout[:], start=True, stop=False)
                        m = nc.tensor.matmul(o_, one_row[:], bout[:], start=False, stop=True)
                    m.then_inc(y_ps, 1)
                    pe.wait_ge(xn_done, i + 1)
                    for t in range(KC):
                        m = nc.tensor.transpose(ps[6][:, t * P:(t + 1) * P], xn[:, t, :], self.idF[:])
                    m.then_inc(xnt_ps, 1)

            @block.vector
            def _(dve):
                v = nc.vector
                dve.wait_ge(split, 2)
                v.tensor_tensor(wl[:], w_in[:], wh[:].bitcast(F32), ALU.subtract).then_inc(low_split, 1)
                v.tensor_tensor(ul[:], up_in[:], uh[:].bitcast(F32), ALU.subtract).then_inc(low_split, 1)
                dve.sem_inc(seq_done, 1)
                with dve.Fori(0, B) as i:
                    link = Chain(dve, dchain, i, PER_DVE)
                    cos, sin = cs[:, 0:T], cs[:, T:2 * T]
                    dve.wait_ge(proj_ps, i * 4 + 1)
                    v.scalar_tensor_tensor(rope_t[:, 0, :], ps[0][:, 0:T], vec[:, 0:1], cos, ALU.add, ALU.mult)
                    link(v.scalar_tensor_tensor(rope_t[:, 1, :], ps[0][:, T:2 * T], vec[:, 1:2], sin, ALU.add, ALU.mult))
                    dve.wait_ge(lat_half, i + 1)
                    v.scalar_tensor_tensor(lat_l[:], ps[1][0:DL, 0:T], vec[0:DL, 2:3], lat_h[:].bitcast(F32),
                                           ALU.add, ALU.subtract).then_inc(lat_split, 1)
                    v.tensor_tensor(qkv[:, 0, :], rope_t[:, 0, :], rope_t[:, 1, :], ALU.add)
                    dve.wait_ge(proj_ps, i * 4 + 3)
                    v.scalar_tensor_tensor(rope_t[:, 2, :], ps[2][:, 0:T], vec[:, 3:4], cos, ALU.add, ALU.mult)
                    link(v.scalar_tensor_tensor(rope_t[:, 3, :], ps[2][:, T:2 * T], vec[:, 4:5], sin, ALU.add, ALU.mult))
                    v.tensor_tensor(qkv[:, 1, :], rope_t[:, 2, :], rope_t[:, 3, :], ALU.add).then_inc(qkv_done, 1)
                    for t in range(KC):
                        dve.wait_ge(tok_kept, i * KC + t + 1)
                        link(v.tensor_tensor(prod[:, t, :].rearrange("p (h g d) -> p h g d", h=H, g=H),
                                             tok[:, t, 0, :, :].unsqueeze(2).broadcast_to([P, H, H, DH]),
                                             tok[:, t, 1, :, :].unsqueeze(1).broadcast_to([P, H, H, DH]), ALU.mult))
                        link(v.tensor_reduce(s_[:, t, :, :], prod[:, t, :].rearrange("p (h g d) -> p h g d", h=H, g=H),
                                             AX.X, ALU.add))
                        link(v.tensor_reduce(mx[:, t, :], s_[:, t, :, :], AX.X, ALU.max))
                        v.tensor_tensor(s_[:, t, :, :], s_[:, t, :, :], mx[:, t, :].unsqueeze(2).broadcast_to([P, H, H]),
                                        ALU.subtract).then_inc(shifted, 1)
                    for t in range(KC):
                        dve.wait_ge(exp_done, i * KC + t + 1)
                        link(v.tensor_reduce(den[:, t, :], pe_[:, t, :, :], AX.X, ALU.add))
                        link(v.reciprocal(rec[:, t, :], den[:, t, :]))
                        dve.wait_ge(prod2_done, i * KC + t + 1)
                        link(v.tensor_reduce(o[:, t, :, :], prod2[:, t, :].rearrange("p (h d g) -> p h d g", h=H, d=DH),
                                             AX.X, ALU.add))
                        v.tensor_tensor(on[:, t, :, :], o[:, t, :, :], rec[:, t, :].unsqueeze(2).broadcast_to([P, H, DH]),
                                        ALU.mult).then_inc(on_done, 1)
                    dve.wait_ge(y_ps, i + 1)
                    link(v.tensor_tensor(y[:], ps[7][:, 0:T].rearrange("p (c d) -> p c d", c=KC),
                                         self.X[:, bass.ds(i * KC, KC), :], ALU.add))
                    self.norm_stats(link, y, st, mv, ve[:], KC, LN_EPS).then_inc(ve_done, 1)
                    dve.wait_ge(rs_done, i + 1)
                    for t in range(KC):
                        m = v.tensor_scalar(xn[:, t, :], y[:, t, :], mv[:, t, 0:1], rs[:, t:t + 1], ALU.subtract, ALU.mult)
                    m.then_inc(xn_done, 1)
                    dve.wait_ge(xh_kept, i + 1)
                    dve.wait_ge(x_kept, i + 1)
                    v.tensor_tensor(self.XL[:, bass.ds(i * T, T)], ps[6][:, 0:T],
                                    self.XH[:, bass.ds(i * T, T)].bitcast(F32), ALU.subtract).then_inc(seq_done, 1)
                    link.close()


    def mixture(self, tag, router, act_fn, n_shared, ht, rms=False, biases=False):
        nc, I, ps = self.nc, self.ins, self.ps
        NR = 8
        NE = n_shared + NR
        H = ht * P
        NB = 512
        NBLK = NTOK // NB
        TB = NB // P
        R = 32 if router == "mlp" else P
        HP, HR = 3, 4
        LAG = 2
        scaled = rms
        GR = 1 if rms else 2
        gates_dram = nc.dram_tensor(tag + "_gates", (2, NE, NTOK), F32).ap()
        with ExitStack() as c:
            def sb(name, shape, dt=F32):
                return c.enter_context(nc.sbuf_tensor(f"{tag}_{name}", shape, dt))

            def sem(name):
                return self.semaphore(f"{tag}_{name}")

            acc = sb("acc", [P, NTOK])
            if rms:
                RH, RL = sb("RH", [P, NTOK], F32R), sb("RL", [P, NTOK], F32R)
            else:
                RH, RL = self.XH, self.XL
            wr_in = sb("wr_in", [P, R])
            wrh, wrl = sb("wrh", [P, R], F32R), sb("wrl", [P, R], F32R)
            wg2, bg1 = sb("wg2", [32, P]), sb("bg1", [32, 1])
            rank = sb("rank", [P, NR])
            hid_r, lt = sb("hid_r", [32, NB]), sb("lt", [P, NB])
            V = sb("V", [P, NTILE, NR])
            ta, tb_, s1, s2 = (sb(n, [P, NTILE, NR]) for n in ("ta", "tb", "s1", "s2"))
            m1, m2 = sb("m1", [P, NTILE]), sb("m2", [P, NTILE])
            G = sb("G", [P, NTILE, NE])
            gt = sb("gt", [NE, NB])
            gth, gtl = sb("gth", [NE, 2, NB], F32R), sb("gtl", [NE, 2, NB], F32R)
            b2, b1 = sb("b2", [NE, P]), sb("b1", [P, NE * ht])
            b1e, b1_kept = sb("b1e", [P, ht]), sem("biases_kept")
            gs = sb("gs", [P, NE])
            ones_in, ones2 = sb("ones_in", [2, P]), sb("ones2", [2, P], F32R)
            w1_in, w2_in = sb("w1_in", [P, H]), sb("w2_in", [P, H])
            w1h, w1l, w2h, w2l = (sb(n, [P, H], F32R) for n in ("w1h", "w1l", "w2h", "w2l"))
            grow = sb("grow", [2, GR * NTOK], F32R)
            gsb, tmp = sb("gsb", [P, 2, NB]), sb("tmp", [P, 2, NB])
            hf = sb("hf", [P, 3, NB])
            hh, hl = sb("hh", [P, HR, NB], F32R), sb("hl", [P, HR, NB], F32R)
            yt, gpad = sb("yt", [P, NB]), sb("gpad", [P, 1])
            st, mv, ve, rs = sb("st", [P, TB, 6]), sb("mv", [P, TB, 2]), sb("ve", [P, TB]), sb("rs", [P, TB])
            xn = sb("xn", [P, TB, D])
            sq, ss = sb("sq", [P, TB, D]), sb("ss", [P, TB])

            loaded, split_h, split_l, idle = sem("weights_loaded"), sem("router_high"), sem("router_low"), sem("ready")
            hid_ps, hid_kept, lt_ps, lt_kept = sem("router_hidden"), sem("router_hidden_kept"), sem("logitsT"), sem("logitsT_kept")
            v_ps, v_kept = sem("logits_ready"), sem("logits_kept")
            acc_done, acc_half = sem("acc_done"), sem("acc_started")
            ss_done, sse, rrs, rn_done, rnt_ps, rh_kept, rl_kept = (sem("squares"), sem("squares_eps"), sem("rms_rstd"),
                sem("rms_ready"), sem("rmsT_ready"), sem("rms_high"), sem("rms_low"))
            once, act_once, g_done, gt_ps, gt_kept, gth_done, gtl_done = (sem("dve_once"), sem("act_once"), sem("gates_ready"),
                sem("gatesT_ready"), sem("gatesT_kept"), sem("gates_high"), sem("gates_low"))
            bias_ps, bias_added, g_stored = sem("gate_bias_ready"), sem("gate_bias_added"), sem("gates_stored")
            w_in, grow_in, w_high, w_low = sem("expert_loaded"), sem("gate_rows_loaded"), sem("expert_high"), sem("expert_low")
            gbc_ps, gbc_kept = sem("gate_broadcast"), sem("gate_kept")
            h_ps, h_act, h_high, h_split, o_step, o_ps, o_read = (sem("hidden_ready"), sem("hidden_activated"), sem("hidden_high"),
                sem("hidden_split"), sem("out_step"), sem("out_ready"), sem("out_gated"))
            yt_kept, y_ps, ve_done, rs_done, xn_done, xnt_ps, xh_kept, xl_kept, x_kept = (sem("sumT_kept"), sem("sum_ready"),
                sem("var_ready"), sem("rstd_ready"), sem("xn_ready"), sem("xnT_ready"), sem("xh_kept"), sem("xl_kept"), sem("x_kept"))
            dchain, dchain2, pchain = sem("dve_chain"), sem("dve_chain2"), sem("pool_chain")
            block = c.enter_context(nc.Block())
            loads = [(wr_in, "wr"), (rank, "rank"), (ones_in, "ones")]
            if router == "mlp":
                loads += [(wg2, "wg2"), (bg1, "bg1")]
            if biases:
                loads += [(b1, "b1"), (b2, "b2"), (gs, "gs")]
            NLOAD = len(loads)

            @block.sync
            def _(sp):
                for dst, src in loads:
                    sp.dma_start(dst[:], I[f"{tag}_{src}"]).then_inc(loaded, 16)
                sp.dma_start(w1_in[:], I[f"{tag}_w1"][0:P, :]).then_inc(w_in, 16)
                sp.dma_start(w2_in[:], I[f"{tag}_w2"][0:P, :]).then_inc(w_in, 16)
                for b in range(NBLK):
                    sp.wait_ge(gth_done, b + 1)
                    sp.wait_ge(gtl_done, b + 1)
                    sp.dma_start(gates_dram[0, :, b * NB:(b + 1) * NB], gth[:, b % 2, :].bitcast(F32)).then_inc(g_stored, 16)
                    sp.dma_start(gates_dram[1, :, b * NB:(b + 1) * NB], gtl[:, b % 2, :].bitcast(F32)).then_inc(g_stored, 16)
                    sp.wait_ge(g_stored, 32 * (b + 1))
                sp.dma_start(grow[:, 0:NTOK].bitcast(F32), gates_dram[:, 0, :]).then_inc(grow_in, 16)
                with sp.Fori(1, NE) as e:
                    sp.wait_ge(w_high, e * 2)
                    sp.wait_ge(w_low, e * 2)
                    sp.dma_start(w1_in[:], I[f"{tag}_w1"][bass.ds(e * P, P), :]).then_inc(w_in, 16)
                    sp.dma_start(w2_in[:], I[f"{tag}_w2"][bass.ds(e * P, P), :]).then_inc(w_in, 16)
                    sp.wait_ge(grow_in, e * 16)
                    sp.wait_ge(gbc_ps, e * NBLK - (GR - 1) * NBLK + 1)
                    sp.dma_start(grow[:, bass.ds((e % GR) * NTOK, NTOK)].bitcast(F32),
                                 gates_dram[:, bass.ds(e, 1), :].rearrange("a b n -> a (b n)")).then_inc(grow_in, 16)

            @block.gpsimd
            def _(pool):
                g = nc.gpsimd
                with pool.Fori(0, NBLK) as b:
                    blk = bass.ds(b * NB, NB)
                    if rms:
                        g.tensor_tensor(acc[:, blk], self.XH[:, blk].bitcast(F32), self.XL[:, blk].bitcast(F32),
                                        ALU.add).then_inc(acc_half, 1)
                        pool.wait_ge(acc_half, b + 1)
                        g.tensor_tensor(gpad[:], self.mhalf[:, 0:1], self.mhalf[:, 0:1], ALU.mult)
                        g.tensor_tensor(acc[:, blk], acc[:, blk], acc[:, blk], ALU.add).then_inc(acc_done, 1)
                        pool.wait_ge(sse, b + 1)
                        g.tensor_tensor(rs[:], ve[:], self.mhalf[:, 0:TB], ALU.pow).then_inc(rrs, 1)
                    else:
                        g.tensor_tensor(acc[:, blk], self.XH[:, blk].bitcast(F32), self.XL[:, blk].bitcast(F32),
                                        ALU.add).then_inc(acc_done, 1)
                if biases:
                    pool.wait_ge(bias_added, NBLK)
                with pool.Fori(0, NE) as e:
                    for b in range(NBLK):
                        n = e * NBLK + b
                        pool.wait_ge(o_read, n + 1)
                        pool.wait_ge(acc_done, n + 1)
                        g.tensor_tensor(acc[:, b * NB:(b + 1) * NB], acc[:, b * NB:(b + 1) * NB], tmp[:, b % 2, :],
                                        ALU.add).then_inc(acc_done, 1)
                with pool.Fori(0, NBLK) as b:
                    pool.wait_ge(ve_done, b + 1)
                    g.tensor_tensor(rs[:], ve[:], self.mhalf[:, 0:TB], ALU.pow).then_inc(rs_done, 1)
                    pool.wait_ge(xn_done, b + 1)
                    g.tensor_copy(self.X[:, bass.ds(b * TB, TB), :], xn[:]).then_inc(x_kept, 1)

            @block.scalar
            def _(act):
                a = nc.scalar
                act.wait_ge(loaded, 16 * NLOAD)
                a.activation(wrh[:], wr_in[:], ACT.Copy).then_inc(split_h, 1)
                a.activation(ones2[:], ones_in[:], ACT.Copy).then_inc(split_h, 1)
                with act.Fori(0, NBLK) as b:
                    if rms:
                        act.wait_ge(idle, b + 1)
                        for t in range(TB):
                            a.activation(sq[:, t, :], self.X[:, bass.ds(b * TB + t, 1), :].rearrange("p a d -> p (a d)"),
                                             ACT.Square, accum_out=ss[:, t:t + 1]).then_inc(ss_done, 1)
                    if router == "mlp":
                        act.wait_ge(hid_ps, b + 1)
                        a.activation(hid_r[:], ps[0][0:32, :], ACT.Gelu, bias=bg1[:, 0:1]).then_inc(hid_kept, 1)
                    act.wait_ge(lt_ps, b + 1)
                    a.activation(lt[:], ps[1][:], ACT.Copy).then_inc(lt_kept, 1)
                    if rms:
                        act.wait_ge(rnt_ps, b + 1)
                        a.activation(RH[:, bass.ds(b * NB, NB)], ps[3][:], ACT.Copy).then_inc(rh_kept, 1)
                if router == "sigmoid":
                    act.wait_ge(v_kept, NBLK)
                    a.activation(V[:], V[:], ACT.Sigmoid).then_inc(act_once, 1)
                else:
                    act.wait_ge(once, {"mlp": 2, "logits": 8}[router])
                    a.activation(ta[:], ta[:], ACT.Exp).then_inc(act_once, 1)
                for b in range(NBLK):
                    act.wait_ge(gt_ps, b + 1)
                    if b:
                        act.wait_ge(gtl_done, b)
                        if biases:
                            act.wait_ge(bias_ps, b)
                    a.activation(gt[:], ps[4 + b % 2][0:NE, :], ACT.Copy).then_inc(gt_kept, 1)
                    act.wait_ge(gt_kept, b + 1)
                    if b >= 2:
                        act.wait_ge(g_stored, 32 * (b - 1))
                    a.activation(gth[:, b % 2, :], gt[:], ACT.Copy).then_inc(gth_done, 1)
                with act.Fori(0, NE) as e:
                    act.wait_ge(w_in, e * 32 + 32)
                    act.wait_ge(o_ps, e * NBLK + 1)
                    a.activation(w2h[:], w2_in[:], ACT.Copy).then_inc(w_high, 1)
                    if scaled:
                        a.activation(w1h[:], w1_in[:], ACT.Copy, scale=gs[:, bass.ds(e, 1)]).then_inc(w_high, 1)
                    else:
                        a.activation(w1h[:], w1_in[:], ACT.Copy).then_inc(w_high, 1)
                    if biases:
                        a.activation(b1e[:], b1[:, bass.ds(e * ht, ht)], ACT.Copy).then_inc(b1_kept, 1)
                        act.wait_ge(b1_kept, e + 1)
                    for b in range(NBLK):
                        n = e * NBLK + b
                        for j in range(ht):
                            q = n * ht + j
                            k = b * ht + j
                            act.wait_ge(h_ps, q + 1)
                            if k >= 3:
                                act.wait_ge(h_split, q - 2)
                            bias = b1e[:, j:j + 1] if biases else 0.0
                            a.activation(hf[:, k % 3, :], ps[k % HP][:], act_fn, bias=bias).then_inc(h_act, 1)
                        act.wait_ge(gbc_ps, n + 2)
                        if b >= 2:
                            act.wait_ge(o_read, n - 1)
                        a.activation(gsb[:, b % 2, :], ps[5 + b % 2][:], ACT.Copy).then_inc(gbc_kept, 1)
                with act.Fori(0, NBLK) as b:
                    act.wait_ge(xl_kept, b + 1)
                    act.wait_ge(acc_done, NBLK * NE + NBLK)
                    a.activation(yt[:], acc[:, bass.ds(b * NB, NB)], ACT.Copy).then_inc(yt_kept, 1)
                    act.wait_ge(xnt_ps, b + 1)
                    a.activation(self.XH[:, bass.ds(b * NB, NB)], ps[1][:], ACT.Copy).then_inc(xh_kept, 1)

            @block.tensor
            def _(pe):
                pe.wait_ge(split_h, 2)
                pe.wait_ge(split_l, 1)
                with pe.Fori(0, NBLK) as b:
                    pe.wait_ge(idle, b + 1)
                    xh, xl = self.XH[:, bass.ds(b * NB, NB)], self.XL[:, bass.ds(b * NB, NB)]
                    if router == "mlp":
                        mm3(nc, ps[0][0:32, :], wrh[:], wrl[:], xh, xl).then_inc(hid_ps, 1)
                        pe.wait_ge(hid_kept, b + 1)
                        nc.tensor.matmul(ps[1][:], wg2[:], hid_r[:], start=True, stop=True).then_inc(lt_ps, 1)
                    else:
                        mm3(nc, ps[1][:], wrh[:], wrl[:], xh, xl).then_inc(lt_ps, 1)
                    pe.wait_ge(lt_kept, b + 1)
                    for t in range(TB):
                        m = nc.tensor.transpose(ps[2][:, t * P:(t + 1) * P], lt[:, t * P:(t + 1) * P], self.idF[:])
                    m.then_inc(v_ps, 1)
                    if rms:
                        pe.wait_ge(rn_done, b + 1)
                        for t in range(TB):
                            m = nc.tensor.transpose(ps[3][:, t * P:(t + 1) * P], xn[:, t, :], self.idF[:])
                        m.then_inc(rnt_ps, 1)
                pe.wait_ge(g_done, 1)
                for b in range(NBLK):
                    if b >= 2:
                        pe.wait_ge(gt_kept, b - 1)
                    for t in range(TB):
                        m = nc.tensor.transpose(ps[4 + b % 2][0:NE, t * P:(t + 1) * P], G[:, b * TB + t, :], self.idF[:])
                    m.then_inc(gt_ps, 1)
                    if biases:
                        pe.wait_ge(gt_kept, b + 1)
                        if b:
                            pe.wait_ge(bias_added, b)
                        nc.tensor.matmul(ps[6][:], b2[:], gt[:], start=True, stop=True).then_inc(bias_ps, 1)
                pe.wait_ge(gt_kept, NBLK)
                if biases:
                    pe.wait_ge(bias_added, NBLK)
                pe.sem_inc(gbc_ps, 1)
                pe.sem_inc(o_ps, 1)
                with pe.Fori(0, NE) as e:
                    pe.wait_ge(w_high, e * 2 + 2)
                    pe.wait_ge(w_low, e * 2 + 2)
                    pe.wait_ge(grow_in, e * 16 + 16)

                    def gate(b):
                        if b >= 2:
                            pe.wait_ge(gbc_kept, e * NBLK + b - 1)
                        nc.tensor.matmul(ps[5 + b % 2][:], ones2[:], grow[:, bass.ds((e % GR) * NTOK + b * NB, NB)],
                                         start=True, stop=True).then_inc(gbc_ps, 1)

                    def hidden(k):
                        b, j = divmod(k, ht)
                        if k >= HP:
                            pe.wait_ge(h_act, (e * NBLK) * ht + k - HP + 1)
                        s = slice(j * P, (j + 1) * P)
                        mm3(nc, ps[k % HP][:], w1h[:, s], w1l[:, s], RH[:, b * NB:(b + 1) * NB],
                            RL[:, b * NB:(b + 1) * NB]).then_inc(h_ps, 1)

                    def outward(k):
                        b, j = divmod(k, ht)
                        pe.wait_ge(h_split, (e * NBLK) * ht + k + 1)
                        if j == 0 and b >= 2:
                            pe.wait_ge(o_read, e * NBLK + b - 1)
                        s = slice(j * P, (j + 1) * P)
                        m = mm3(nc, ps[3 + b % 2][:], w2h[:, s], w2l[:, s], hh[:, k % HR, :], hl[:, k % HR, :],
                                start=(j == 0), stop=(j == ht - 1))
                        m.then_inc(o_ps if j == ht - 1 else o_step, 1)

                    for k in range(NBLK * ht + LAG):
                        if k < NBLK * ht:
                            if k % ht == 0:
                                gate(k // ht)
                            hidden(k)
                        if k >= LAG:
                            outward(k - LAG)
                pe.wait_ge(o_read, NE * NBLK)
                with pe.Fori(0, NBLK) as b:
                    pe.wait_ge(yt_kept, b + 1)
                    for t in range(TB):
                        m = nc.tensor.transpose(ps[0][:, t * P:(t + 1) * P], yt[:, t * P:(t + 1) * P], self.idF[:])
                    m.then_inc(y_ps, 1)
                    pe.wait_ge(xn_done, b + 1)
                    for t in range(TB):
                        m = nc.tensor.transpose(ps[1][:, t * P:(t + 1) * P], xn[:, t, :], self.idF[:])
                    m.then_inc(xnt_ps, 1)

            @block.vector
            def _(dve):
                v = nc.vector
                dve.wait_ge(split_h, 1)
                v.tensor_tensor(wrl[:], wr_in[:], wrh[:].bitcast(F32), ALU.subtract).then_inc(split_l, 1)
                dve.sem_inc(idle, 1)
                with dve.Fori(0, NBLK) as b:
                    if rms:
                        dve.wait_ge(ss_done, b * TB + TB)
                        v.tensor_scalar(ve[:], ss[:], 1.0 / D, 1.1920929e-07, ALU.mult, ALU.add).then_inc(sse, 1)
                        dve.wait_ge(rrs, b + 1)
                        for t in range(TB):
                            m = v.tensor_scalar(xn[:, t, :], self.X[:, bass.ds(b * TB + t, 1), :].rearrange("p a d -> p (a d)"),
                                                rs[:, t:t + 1], None, ALU.mult)
                        m.then_inc(rn_done, 1)
                    dve.wait_ge(v_ps, b + 1)
                    v.tensor_copy(V[:, bass.ds(b * TB, TB), :], ps[2][:].rearrange("p (t r) -> p t r", t=TB)[:, :, 0:NR]).then_inc(v_kept if rms else idle, 1)
                    if rms:
                        dve.wait_ge(rh_kept, b + 1)
                        v.tensor_tensor(RL[:, bass.ds(b * NB, NB)], ps[3][:], RH[:, bass.ds(b * NB, NB)].bitcast(F32),
                                        ALU.subtract).then_inc(idle, 1)
                dve.wait_ge(*((v_kept, NBLK) if rms else (idle, NBLK + 1)))
                cnt = [0]

                def step(ins):
                    cnt[0] += 1
                    ins.then_inc(once, 1)
                    dve.wait_ge(once, cnt[0])

                def wide(m):
                    return m[:].unsqueeze(2).broadcast_to([P, NTILE, NR])

                if router == "mlp":
                    step(v.tensor_reduce(m1[:], V[:], AX.X, ALU.max))
                    step(v.tensor_tensor(ta[:], V[:], wide(m1), ALU.subtract))
                    dve.wait_ge(act_once, 1)
                    step(v.tensor_reduce(m1[:], ta[:], AX.X, ALU.add))
                    step(v.reciprocal(m2[:], m1[:]))
                    step(v.tensor_tensor(V[:], ta[:], wide(m2), ALU.mult))
                if router == "sigmoid":
                    dve.wait_ge(act_once, 1)

                def choose(vals, out):
                    step(v.tensor_reduce(m1[:], vals[:], AX.X, ALU.max))
                    step(v.tensor_tensor(tb_[:], vals[:], wide(m1), ALU.is_equal))
                    step(v.tensor_tensor(tb_[:], tb_[:], rank[:].unsqueeze(1).broadcast_to([P, NTILE, NR]), ALU.mult))
                    step(v.tensor_reduce(m2[:], tb_[:], AX.X, ALU.max))
                    step(v.tensor_tensor(out[:], tb_[:], wide(m2), ALU.is_equal))

                choose(V, s1)
                if router == "logits":
                    step(v.tensor_tensor(ta[:], V[:], wide(m1), ALU.subtract))
                    step(v.tensor_copy(m2[:], m1[:]))
                    step(v.tensor_copy(m2[:], m1[:]))
                    dve.wait_ge(act_once, 1)
                    step(v.tensor_copy(G[:, :, n_shared:], ta[:]))
                step(v.scalar_tensor_tensor(ta[:].rearrange("p t r -> p (t r)"), s1[:].rearrange("p t r -> p (t r)"), -3e38,
                                            V[:].rearrange("p t r -> p (t r)"), ALU.mult, ALU.add))
                choose(ta, s2)
                step(v.tensor_tensor(s1[:], s1[:], s2[:], ALU.add))
                if router == "mlp":
                    step(v.tensor_tensor(G[:, :, n_shared:], V[:], s1[:], ALU.mult))
                elif router == "sigmoid":
                    step(v.tensor_reduce(m1[:], V[:], AX.X, ALU.add))
                    step(v.reciprocal(m2[:], m1[:]))
                    step(v.tensor_tensor(s1[:], V[:], s1[:], ALU.mult))
                    step(v.tensor_tensor(G[:, :, n_shared:], s1[:], wide(m2), ALU.mult))
                else:
                    step(v.tensor_tensor(ta[:], G[:, :, n_shared:], s1[:], ALU.mult))
                    step(v.tensor_reduce(m1[:], ta[:], AX.X, ALU.add))
                    step(v.reciprocal(m2[:], m1[:]))
                    step(v.tensor_tensor(G[:, :, n_shared:], ta[:], wide(m2), ALU.mult))
                if n_shared:
                    step(v.memset(G[:, :, 0:n_shared], 1.0))
                v.memset(self.pad[:], 0.0).then_inc(g_done, 1)
                for b in range(NBLK):
                    s = slice(b * NB, (b + 1) * NB)
                    dve.wait_ge(gth_done, b + 1)
                    if b >= 2:
                        dve.wait_ge(g_stored, 32 * (b - 1))
                    v.tensor_tensor(gtl[:, b % 2, :], gt[:], gth[:, b % 2, :].bitcast(F32), ALU.subtract).then_inc(gtl_done, 1)
                    if biases:
                        dve.wait_ge(bias_ps, b + 1)
                        dve.wait_ge(acc_done, NBLK)
                        v.tensor_tensor(acc[:, s], ps[6][:], acc[:, s], ALU.add).then_inc(bias_added, 1)
                with dve.Fori(0, NE) as e:
                    dve.wait_ge(w_high, e * 2 + 1)
                    v.tensor_tensor(w2l[:], w2_in[:], w2h[:].bitcast(F32), ALU.subtract).then_inc(w_low, 1)
                    dve.wait_ge(w_high, e * 2 + 2)
                    if scaled:
                        v.scalar_tensor_tensor(w1l[:], w1_in[:], gs[:, bass.ds(e, 1)], w1h[:].bitcast(F32), ALU.mult,
                                               ALU.subtract).then_inc(w_low, 1)
                    else:
                        v.tensor_tensor(w1l[:], w1_in[:], w1h[:].bitcast(F32), ALU.subtract).then_inc(w_low, 1)

                    def gated(b):
                        n = e * NBLK + b
                        dve.wait_ge(gbc_kept, n + 1)
                        dve.wait_ge(o_ps, n + 2)
                        dve.wait_ge(acc_done, n + NBLK - 1)
                        v.tensor_tensor(tmp[:, b % 2, :], ps[3 + b % 2][:], gsb[:, b % 2, :], ALU.mult).then_inc(o_read, 1)

                    for k in range(NBLK * ht):
                        q = e * (NBLK * ht) + k
                        dve.wait_ge(h_act, q + 1)
                        if k >= HR:
                            kk = k - HR
                            fb, fj = divmod(kk, ht)
                            if fj == ht - 1:
                                dve.wait_ge(o_ps, e * NBLK + fb + 2)
                            else:
                                dve.wait_ge(o_step, e * (NBLK * (ht - 1)) + fb * (ht - 1) + fj + 1)
                        v.tensor_copy(hh[:, k % HR, :], hf[:, k % 3, :]).then_inc(h_high, 1)
                        dve.wait_ge(h_high, q + 1)
                        v.tensor_tensor(hl[:, k % HR, :], hf[:, k % 3, :], hh[:, k % HR, :].bitcast(F32),
                                        ALU.subtract).then_inc(h_split, 1)
                        if k >= LAG and (k - LAG) % ht == ht - 1:
                            gated((k - LAG) // ht)
                    gated(NBLK - 1)
                dve.sem_inc(xl_kept, 1)
                with dve.Fori(0, NBLK) as b:
                    link = Chain(dve, dchain2, b, 2)
                    dve.wait_ge(y_ps, b + 1)
                    y = ps[0][:].rearrange("p (t d) -> p t d", t=TB)
                    self.norm_stats(link, y, st, mv, ve[:], TB, LN_EPS).then_inc(ve_done, 1)
                    dve.wait_ge(rs_done, b + 1)
                    for t in range(TB):
                        m = v.tensor_scalar(xn[:, t, :], y[:, t, :], mv[:, t, 0:1], rs[:, t:t + 1], ALU.subtract, ALU.mult)
                    m.then_inc(xn_done, 1)
                    dve.wait_ge(xh_kept, b + 1)
                    dve.wait_ge(x_kept, b + 1)
                    v.tensor_tensor(self.XL[:, bass.ds(b * NB, NB)], ps[1][:], self.XH[:, bass.ds(b * NB, NB)].bitcast(F32),
                                    ALU.subtract).then_inc(xl_kept, 1)


    def latent_attention(self):
        nc, I, ps = self.nc, self.ins, self.ps
        H, DH, KC = 16, 64, T // P
        SCALE = 1.0 / float(DH) ** 0.5
        NC_ = H * DH // P
        HPC = P // DH
        WU = H * DH
        VA = DH + 1
        with ExitStack() as c_:
            def sb(name, shape, dt=F32):
                return c_.enter_context(nc.sbuf_tensor("a1_" + name, shape, dt))

            def sem(name):
                return self.semaphore("a1_" + name)

            wd_in, up_in = sb("wd_in", [P, P]), sb("up_in", [P, 3 * WU])
            wdh, wdl = sb("wdh", [P, P], F32R), sb("wdl", [P, P], F32R)
            uh, ul = sb("uh", [P, 3 * WU], F32R), sb("ul", [P, 3 * WU], F32R)
            wout, ln, cs = sb("wout", [P, NC_, D]), sb("ln", [P, 2]), sb("cs", [P, 2 * T])
            sel_in, sel = sb("sel_in", [32, H * P]), sb("sel", [32, H * P], BF16)
            st, mv, ve, rs, xn = sb("st_", [P, KC, 6]), sb("mv_", [P, KC, 2]), sb("ve_", [P, KC]), sb("rs_", [P, KC]), sb("xn_", [P, KC, D])
            hf, hh, hl = sb("hf", [P, T]), sb("hh", [P, T], F32R), sb("hl", [P, T], F32R)
            ch, cl = sb("ch", [P, T], F32R), sb("cl", [P, T], F32R)
            rt = sb("rt", [P, 4, 2 * T])
            qk, qkb = sb("qk", [P, NC_, 2, T]), sb("qkb", [P, NC_, 2, T], BF16)
            va = sb("va", [P, KC, H, VA])
            negm, nmt = sb("negm", [P, KC, P]), sb("nmt", [32, T], BF16)
            pt = sb("pt", [P, 3, 2 * T])
            rec, on, ot = sb("rec", [P, 2, KC, HPC]), sb("on", [P, KC, H, DH]), sb("ot", [P, NC_, T])
            bM, bV, bNM, bST, bPV = (4, 5), (6, 7), 6, (0, 1, 2), (4, 5)
            tail = Tail(self, c_, "a1", 0, KC, ps[6][:, 0:T], ps[7][:, 0:T], gain=2.0)

            loaded, w_high, w_low = sem("weights_loaded"), sem("weights_high"), sem("weights_low")
            ve_done, rs_done, xn_done, hnt_ps, hf_done, hh_done, hl_done = (sem("pre_var"), sem("pre_rstd"), sem("pre_xn"),
                sem("normedT_ready"), sem("normed_scaled"), sem("normed_high"), sem("normed_low"))
            c_ps, ch_done, cl_done = sem("latents_ready"), sem("latents_high"), sem("latents_low")
            qk_ps, rt_done, add_done, qkb_done = sem("qk_ready"), sem("rope_products"), sem("rope_done"), sem("bf16_qk_ready")
            v_ps, v_kept = sem("v_ready"), sem("v_kept")
            s_ps, max_done, nm_ps, nm_kept = sem("scores_ready"), sem("max_done"), sem("maxT_ready"), sem("maxT_kept")
            st_ps, exp_done, pv_done, on_done = sem("scoresT_ready"), sem("exp_done"), sem("pv_done"), sem("normalised")
            ont_ps, ont_kept, chain = sem("outT_ready"), sem("outT_kept"), sem("dve_chain")
            block = c_.enter_context(nc.Block())
            loads = ((wd_in, "a1_wd"), (up_in, "a1_up"), (wout, "a1_wout"), (ln, "a1_ln"), (cs, "a1_cs"), (sel_in, "a1_sel"))

            @block.sync
            def _(sp):
                for dst, src in loads:
                    sp.dma_start(dst[:], I[src]).then_inc(loaded, 16)

            @block.gpsimd
            def _(pool):
                g = nc.gpsimd
                with pool.Fori(0, B) as i:
                    pool.wait_ge(ve_done, i + 1)
                    g.tensor_tensor(rs[:], ve[:], self.mhalf[:, 0:KC], ALU.pow).then_inc(rs_done, 1)
                    for j in range(NC_):
                        for r in range(2):
                            m = 2 * j + r
                            pool.wait_ge(rt_done, i * 2 * NC_ + m + 1)
                            g.tensor_tensor(qk[:, j, r, :], rt[:, m % 4, 0:T], rt[:, m % 4, T:2 * T], ALU.add).then_inc(add_done, 1)
                    tail.pool(pool, i, i)

            @block.scalar
            def _(act):
                a = nc.scalar
                act.wait_ge(loaded, 16 * len(loads))
                a.activation(wdh[:], wd_in[:], ACT.Copy).then_inc(w_high, 1)
                a.activation(uh[:], up_in[:], ACT.Copy).then_inc(w_high, 1)
                a.activation(sel[:], sel_in[:], ACT.Copy).then_inc(w_high, 1)
                with act.Fori(0, B) as i:
                    act.wait_ge(hf_done, i + 1)
                    a.activation(hh[:], hf[:], ACT.Copy).then_inc(hh_done, 1)
                    act.wait_ge(c_ps, i + 1)
                    a.activation(ch[:], ps[1][:, 0:T], ACT.Copy).then_inc(ch_done, 1)
                    for j in range(NC_):
                        if j < 4:
                            k, half = divmod(j, 2)
                            act.wait_ge(v_ps, i * 4 + j + 1)
                            a.activation(va[:, k, half * 8:half * 8 + 8, 0:DH], ps[bV[j % 2]][:].rearrange("p (h d) -> p h d", d=DH),
                                         ACT.Copy).then_inc(v_kept, 1)
                        act.wait_ge(add_done, i * 2 * NC_ + 2 * j + 2)
                        a.activation(qkb[:, j, :, :], qk[:, j, :, :], ACT.Copy).then_inc(qkb_done, 1)
                    act.wait_ge(nm_ps, i + 1)
                    a.activation(nmt[:], ps[bNM][0:32, 0:T], ACT.Copy).then_inc(nm_kept, 1)
                    for h in range(H):
                        act.wait_ge(st_ps, i * H + h + 1)
                        if h >= 3:
                            act.wait_ge(pv_done, i * H + h - 2)
                        a.activation(pt[:, h % 3, :], ps[bST[h % 3]][:], ACT.Exp, scale=SCALE).then_inc(exp_done, 1)
                    for b in range(4):
                        act.wait_ge(ont_ps, i * 4 + b + 1)
                        a.activation(ot[:, 2 * b:2 * b + 2, :], ps[b][:].rearrange("p (c t) -> p c t", c=2), ACT.Copy).then_inc(ont_kept, 1)
                    tail.act(act, i, i)

            @block.tensor
            def _(pe):
                pe.wait_ge(w_high, 3)
                pe.wait_ge(w_low, 4)
                with pe.Fori(0, B) as i:
                    pe.wait_ge(xn_done, i + 1)
                    pe.wait_ge(tail.done, i + 1)
                    for t in range(KC):
                        m = nc.tensor.transpose(ps[0][:, t * P:(t + 1) * P], xn[:, t, :], self.idF[:])
                    m.then_inc(hnt_ps, 1)
                    pe.wait_ge(hl_done, i + 1)
                    mm3(nc, ps[1][:, 0:T], wdh[:], wdl[:], hh[:], hl[:]).then_inc(c_ps, 1)
                    pe.wait_ge(ch_done, i + 1)
                    pe.wait_ge(cl_done, i + 1)

                    def project(j):
                        if j >= 2:
                            pe.wait_ge(rt_done, i * 2 * NC_ + 2 * j - 2)
                        for r in range(2):
                            rows = slice(r * DH, (r + 1) * DH)
                            for sw in range(2):
                                col = slice(sw * WU + j * P, sw * WU + (j + 1) * P)
                                m = mm3(nc, ps[2 * (j % 2) + r][:, sw * T:(sw + 1) * T], uh[rows, col], ul[rows, col],
                                        ch[rows, :], cl[rows, :])
                            m.then_inc(qk_ps, 1)

                    def values(n):
                        if n >= 2:
                            pe.wait_ge(v_kept, i * 4 + n - 1)
                        k, half = divmod(n, 2)
                        col = slice(2 * WU + half * 512, 2 * WU + (half + 1) * 512)
                        t = slice(k * P, (k + 1) * P)
                        mm3(nc, ps[bV[n % 2]][:], ch[DH:P, t], cl[DH:P, t], uh[DH:P, col], ul[DH:P, col]).then_inc(v_ps, 1)

                    def maxima(j):
                        pe.wait_ge(qkb_done, i * NC_ + j + 1)
                        for u in range(HPC):
                            h = HPC * j + u
                            if h >= 2:
                                pe.wait_ge(max_done, i * H + h - 1)
                            rows = slice(u * DH, (u + 1) * DH)
                            for t in range(KC):
                                m = nc.tensor.matmul(ps[bM[h % 2]][:, t * T:(t + 1) * T], qkb[rows, j, 0, t * P:(t + 1) * P],
                                                     qkb[rows, j, 1, :], start=True, stop=True)
                            m.then_inc(s_ps, 1)

                    for j in range(NC_):
                        project(j)
                        if j < 4:
                            values(j)
                        if j:
                            maxima(j - 1)
                    maxima(NC_ - 1)
                    pe.wait_ge(max_done, i * H + H)
                    pe.wait_ge(v_kept, i * 4 + 4)
                    for t in range(KC):
                        m = nc.tensor.transpose(ps[bNM][:, t * P:(t + 1) * P], negm[:, t, :], self.idF[:])
                    m.then_inc(nm_ps, 1)
                    pe.wait_ge(nm_kept, i + 1)

                    def scores_t(h):
                        if h >= 3:
                            pe.wait_ge(exp_done, i * H + h - 2)
                        j, u = divmod(h, HPC)
                        rows = slice(u * DH, (u + 1) * DH)
                        out = ps[bST[h % 3]]
                        for k in range(KC):
                            nc.tensor.matmul(out[:, k * T:(k + 1) * T], qk[rows, j, 1, k * P:(k + 1) * P], qk[rows, j, 0, :],
                                             start=True, stop=False)
                            m = nc.tensor.matmul(out[:, k * T:(k + 1) * T], sel[:, h * P:(h + 1) * P], nmt[:], start=False,
                                                 stop=True)
                        m.then_inc(st_ps, 1)

                    def pv(h):
                        g, u = divmod(h, HPC)
                        pe.wait_ge(exp_done, i * H + h + 1)
                        if u == 0 and g >= 2:
                            pe.wait_ge(on_done, i * NC_ + g - 1)
                        for t in range(KC):
                            n = u * KC + t
                            for k in range(KC):
                                m = nc.tensor.matmul(ps[bPV[g % 2]][:, n * VA:(n + 1) * VA],
                                                     pt[:, h % 3, k * T + t * P:k * T + (t + 1) * P], va[:, k, h, :],
                                                     start=(k == 0), stop=(k == KC - 1))
                        m.then_inc(pv_done, 1)

                    for h in range(H):
                        scores_t(h)
                        if h:
                            pv(h - 1)
                    pv(H - 1)
                    pe.wait_ge(on_done, i * NC_ + NC_)
                    for b in range(4):
                        for k in range(2):
                            for t in range(KC):
                                j = 2 * b + k
                                m = nc.tensor.transpose(ps[b][:, k * T + t * P:k * T + (t + 1) * P],
                                                        on[:, t, HPC * j:HPC * (j + 1), :].rearrange("p h d -> p (h d)"), self.idF[:])
                        m.then_inc(ont_ps, 1)
                    pe.wait_ge(ont_kept, i * 4 + 4)
                    for t in range(KC):
                        for j in range(NC_):
                            m = nc.tensor.matmul(ps[6][:, t * P:(t + 1) * P], ot[:, j, t * P:(t + 1) * P], wout[:, j, :],
                                                 start=(j == 0), stop=(j == NC_ - 1))
                    m.then_inc(tail.y_ps, 1)
                    tail.pe(pe, i)

            @block.vector
            def _(dve):
                v = nc.vector
                v.memset(negm[:], 0.0).then_inc(w_low, 1)
                v.memset(va[:, :, :, DH:VA], 1.0).then_inc(w_low, 1)
                dve.wait_ge(w_high, 3)
                v.tensor_tensor(wdl[:], wd_in[:], wdh[:].bitcast(F32), ALU.subtract).then_inc(w_low, 1)
                v.tensor_tensor(ul[:], up_in[:], uh[:].bitcast(F32), ALU.subtract).then_inc(w_low, 1)
                dve.wait_ge(w_low, 4)
                dve.sem_inc(tail.done, 1)
                with dve.Fori(0, B) as i:
                    link = Chain(dve, chain, i, 2 + NC_ + 3)
                    self.norm_stats(link, self.X[:, bass.ds(i * KC, KC), :], st, mv, ve[:], KC, LN_EPS).then_inc(ve_done, 1)
                    dve.wait_ge(rs_done, i + 1)
                    for t in range(KC):
                        m = v.tensor_scalar(xn[:, t, :], self.X[:, bass.ds(i * KC + t, 1), :].rearrange("p a d -> p (a d)"),
                                            mv[:, t, 0:1], rs[:, t:t + 1], ALU.subtract, ALU.mult)
                    m.then_inc(xn_done, 1)
                    dve.wait_ge(hnt_ps, i + 1)
                    v.tensor_scalar(hf[:], ps[0][:, 0:T], ln[:, 0:1], ln[:, 1:2], ALU.mult, ALU.add).then_inc(hf_done, 1)
                    dve.wait_ge(hh_done, i + 1)
                    v.tensor_tensor(hl[:], hf[:], hh[:].bitcast(F32), ALU.subtract).then_inc(hl_done, 1)
                    dve.wait_ge(ch_done, i + 1)
                    v.tensor_tensor(cl[:], ps[1][:, 0:T], ch[:].bitcast(F32), ALU.subtract).then_inc(cl_done, 1)

                    def maxes(j):
                        for u in range(HPC):
                            h = HPC * j + u
                            dve.wait_ge(s_ps, i * H + h + 1)
                            v.tensor_reduce(negm[:, :, h:h + 1], ps[bM[h % 2]][:].rearrange("p (t k) -> p t k", t=KC), AX.X,
                                            ALU.max, negate=True).then_inc(max_done, 1)

                    for j in range(NC_):
                        for r in range(2):
                            m = 2 * j + r
                            dve.wait_ge(qk_ps, i * 2 * NC_ + m + 1)
                            if m >= 4:
                                dve.wait_ge(add_done, i * 2 * NC_ + m - 3)
                            v.tensor_tensor(rt[:, m % 4, :], ps[2 * (j % 2) + r][:], cs[:], ALU.mult).then_inc(rt_done, 1)
                        if j:
                            maxes(j - 1)
                    maxes(NC_ - 1)
                    for g in range(NC_):
                        dve.wait_ge(pv_done, i * H + HPC * g + HPC)
                        o = ps[bPV[g % 2]][:, 0:HPC * KC * VA].rearrange("p (u t r) -> p t u r", u=HPC, t=KC)
                        link(v.reciprocal(rec[:, g % 2, :, :], o[:, :, :, DH]))
                        v.tensor_tensor(on[:, :, HPC * g:HPC * (g + 1), :], o[:, :, :, 0:DH],
                                        rec[:, g % 2, :, :].unsqueeze(3).broadcast_to([P, KC, HPC, DH]), ALU.mult).then_inc(on_done, 1)
                    tail.dve(dve, link, i, i)
                    tail.dve_low(dve, i, i)
                    link.close()

    def selective_scan(self):
        nc, I, ps = self.nc, self.ins, self.ps
        NST, KCONV, NCH, NS = 16, 4, 2, 2
        NB = NS * T
        TB = NB // P
        NBLK = NTOK // NB
        NQ = NST * NCH
        with ExitStack() as c_:
            def sb(name, shape, dt=F32):
                return c_.enter_context(nc.sbuf_tensor("m2_" + name, shape, dt))

            def sem(name):
                return self.semaphore("m2_" + name)

            w_in, wh, wl = sb("w_in", [P, 4 * P]), sb("wh", [P, 4 * P], F32R), sb("wl", [P, 4 * P], F32R)
            xp_w, dt_w, out_w = sb("xp_w", [P, NCH, P]), sb("dt_w", [P, NCH * P]), sb("out_w", [P, NCH, D])
            sel_in, sel = sb("sel_in", [64, 2 * NST * P]), sb("sel", [64, 2 * NST * P], F32R)
            cw, cvec, a_log, am = sb("cw", [P, NCH, KCONV]), sb("cvec", [P, NCH, 3]), sb("a_log", [P, NCH, NST]), sb("a", [P, NCH, NST])
            xp = sb("xp", [P, NCH, NS, KCONV - 1 + T])
            sz, cv, xt = sb("sz", [P, NCH, NB]), sb("cv", [P, NCH, NB]), sb("xt", [P, NCH, NB])
            st, st_hi, dbl = sb("st", [64, NB], F32R), sb("st_hi", [64, NB], F32R), sb("dbl", [P, NB])
            p_, en, w1, lw, delta, dx = (sb(n, [P, NCH, NB]) for n in ("p", "en", "w1", "lw", "delta", "dx"))
            dA, dbu, h, hc, cs = sb("dA", [P, 3, NB]), sb("dbu", [P, 2, NB]), sb("h", [P, 3, NB]), sb("hc", [P, 2, NB]), sb("cs", [P, 2, NB])
            y = sb("y_", [P, NCH, NB])
            tail = Tail(self, c_, "m2", 0, TB, ps[7][:], ps[4][:])
            bXZ, bDBL, bDP, bB, bC, bY = (0, 1, 2, 3), 4, (5, 6), (0, 1), (2, 3), (5, 6)

            loaded, w_high, w_low, zeros = sem("weights_loaded"), sem("weights_high"), sem("weights_low"), sem("zeros")
            a_exp, a_neg = sem("a_exp"), sem("a_negated")
            xz_ps, xp_kept, sz_done, conv_done, xt_done = sem("xz_ready"), sem("x_padded"), sem("z_silu"), sem("conv_done"), sem("x_silu")
            dbl_ps, dbl_kept, st_low, dp_ps, p_done = sem("bcdt_ready"), sem("bcdt_kept"), sem("bc_low"), sem("dt_ready"), sem("dt_biased")
            en_done, w1_done, lw_done, dx_done = sem("exp_done"), sem("one_plus"), sem("ln_done"), sem("delta_ready")
            b_ps, c_ps, c_kept = sem("b_broadcast"), sem("c_broadcast"), sem("c_kept")
            dA_done, dbu_done, h_done, hc_done, sum_done = (sem("decay_ready"), sem("input_ready"), sem("state_ready"),
                                                           sem("readout_ready"), sem("readout_summed"))
            y_done, chain = sem("gated"), sem("dve_chain")
            block = c_.enter_context(nc.Block())
            loads = ((w_in, "m2_w"), (xp_w, "m2_xp"), (dt_w, "m2_dt"), (out_w, "m2_out"), (sel_in, "m2_sel"),
                     (cw, "m2_cw"), (cvec, "m2_cvec"), (a_log, "m2_alog"))

            @block.sync
            def _(sp):
                for dst, src in loads:
                    sp.dma_start(dst[:], I[src]).then_inc(loaded, 16)

            @block.gpsimd
            def _(pool):
                g = nc.gpsimd
                with pool.Fori(0, NBLK) as i:
                    for q in range(NQ):
                        n, c = divmod(q, NCH)
                        pool.wait_ge(h_done, i * NQ + q + 1)
                        pool.wait_ge(c_kept, i * NST + n + 1)
                        if q >= 2:
                            pool.wait_ge(sum_done, i * NQ + q - 1)
                        g.tensor_tensor(hc[:, q % 2, :], h[:, q % 3, :], cs[:, n % 2, :], ALU.mult).then_inc(hc_done, 1)
                    tail.pool(pool, i, i)

            @block.scalar
            def _(act):
                a = nc.scalar
                act.wait_ge(loaded, 16 * len(loads))
                a.activation(wh[:], w_in[:], ACT.Copy).then_inc(w_high, 1)
                a.activation(sel[:], sel_in[:], ACT.Copy).then_inc(w_high, 1)
                a.activation(am[:], a_log[:], ACT.Exp).then_inc(a_exp, 1)
                act.wait_ge(a_neg, 1)
                with act.Fori(0, NBLK) as i:
                    for c in range(NCH):
                        act.wait_ge(xz_ps, i * 4 + c + 1)
                        a.activation(xp[:, c, :, KCONV - 1:], ps[bXZ[c]][:].rearrange("p (s t) -> p s t", s=NS), ACT.Copy).then_inc(xp_kept, 1)
                    for c in range(NCH):
                        act.wait_ge(conv_done, i * NCH + c + 1)
                        a.activation(xt[:, c, :], cv[:, c, :], ACT.Silu, bias=cvec[:, c, 0:1]).then_inc(xt_done, 1)
                    act.wait_ge(xz_ps, i * 4 + 4)
                    a.activation(sz[:, 0, :], ps[bXZ[2]][:], ACT.Silu)
                    a.activation(sz[:, 1, :], ps[bXZ[3]][:], ACT.Silu).then_inc(sz_done, 1)
                    act.wait_ge(dbl_ps, i + 1)
                    a.activation(dbl[:], ps[bDBL][:], ACT.Copy)
                    a.activation(st[0:32, :], ps[bDBL][0:32, :], ACT.Copy)
                    a.activation(st_hi[32:64, :], ps[bDBL][32:64, :], ACT.Copy).then_inc(dbl_kept, 1)
                    act.wait_ge(p_done, i + 1)
                    a.activation(en[:], en[:], ACT.Exp, scale=-1.0).then_inc(en_done, 1)
                    act.wait_ge(w1_done, i + 1)
                    a.activation(lw[:], w1[:], ACT.Ln).then_inc(lw_done, 1)
                    act.wait_ge(dx_done, i + 1)

                    def keep_c(n):
                        act.wait_ge(c_ps, i * NST + n + 1)
                        if n >= 2:
                            act.wait_ge(hc_done, i * NQ + 2 * n - 2)
                        a.activation(cs[:, n % 2, :], ps[bC[n % 2]][:], ACT.Copy).then_inc(c_kept, 1)

                    for q in range(NQ):
                        n, c = divmod(q, NCH)
                        if q >= 3:
                            act.wait_ge(h_done, i * NQ + q - 2)
                        a.activation(dA[:, q % 3, :], delta[:, c, :], ACT.Exp, scale=am[:, c, n:n + 1]).then_inc(dA_done, 1)
                        if c == 0:
                            keep_c(n)
                    tail.act(act, i, i)

            @block.tensor
            def _(pe):
                pe.wait_ge(w_high, 2)
                pe.wait_ge(w_low, 1)
                with pe.Fori(0, NBLK) as i:
                    pe.wait_ge(tail.done, i + 1)
                    xh, xl = self.XH[:, bass.ds(i * NB, NB)], self.XL[:, bass.ds(i * NB, NB)]
                    for k in range(4):
                        s = slice(k * P, (k + 1) * P)
                        mm3(nc, ps[bXZ[k]][:], wh[:, s], wl[:, s], xh, xl).then_inc(xz_ps, 1)
                    for c in range(NCH):
                        pe.wait_ge(xt_done, i * NCH + c + 1)
                        m = nc.tensor.matmul(ps[bDBL][:], xp_w[:, c, :], xt[:, c, :], start=(c == 0), stop=(c == NCH - 1))
                    m.then_inc(dbl_ps, 1)
                    pe.wait_ge(dbl_kept, i + 1)
                    for c in range(NCH):
                        m = nc.tensor.matmul(ps[bDP[c]][:], dt_w[:, c * P:(c + 1) * P], dbl[:], start=True, stop=True)
                    m.then_inc(dp_ps, 1)
                    pe.wait_ge(st_low, i + 1)
                    pe.wait_ge(sz_done, i + 1)

                    def broadcast(n):
                        if n >= 2:
                            pe.wait_ge(dbu_done, i * NQ + 2 * n - 2)
                        nc.tensor.matmul(ps[bB[n % 2]][:], sel[:, n * P:(n + 1) * P], st[:], start=True, stop=True).then_inc(b_ps, 1)
                        if n >= 2:
                            pe.wait_ge(c_kept, i * NST + n - 1)
                        nc.tensor.matmul(ps[bC[n % 2]][:], sel[:, (NST + n) * P:(NST + n + 1) * P], st[:], start=True,
                                         stop=True).then_inc(c_ps, 1)

                    broadcast(0)
                    broadcast(1)
                    pe.wait_ge(p_done, i + 1)
                    for q in range(NQ):
                        n, c = divmod(q, NCH)
                        pe.wait_ge(hc_done, i * NQ + q + 1)
                        nc.tensor.matmul(ps[bY[c]][:], self.idF[:], hc[:, q % 2, :], start=(n == 0),
                                         stop=(n == NST - 1)).then_inc(sum_done, 1)
                        if c == NCH - 1 and n + 2 < NST:
                            broadcast(n + 2)
                    pe.wait_ge(y_done, i + 1)
                    for t in range(TB):
                        for c in range(NCH):
                            m = nc.tensor.matmul(ps[7][:, t * P:(t + 1) * P], y[:, c, t * P:(t + 1) * P], out_w[:, c, :],
                                                 start=(c == 0), stop=(c == NCH - 1))
                    m.then_inc(tail.y_ps, 1)
                    tail.pe(pe, i)

            @block.vector
            def _(dve):
                v = nc.vector
                v.memset(xp[:, :, :, 0:KCONV - 1], 0.0).then_inc(zeros, 1)
                dve.wait_ge(w_high, 1)
                v.tensor_tensor(wl[:], w_in[:], wh[:].bitcast(F32), ALU.subtract).then_inc(w_low, 1)
                dve.wait_ge(a_exp, 1)
                v.tensor_scalar(am[:], am[:], -1.0, None, ALU.mult).then_inc(a_neg, 1)
                dve.wait_ge(zeros, 1)
                dve.sem_inc(tail.done, 1)
                with dve.Fori(0, NBLK) as i:
                    link = Chain(dve, chain, i, 15)
                    def conv(c, k):
                        src = xp[:, c, :, k:k + T]
                        dst = cv[:, c, :].rearrange("p (s t) -> p s t", s=NS)
                        if k == 0:
                            return v.tensor_scalar(dst, src, cw[:, c, 0:1], None, ALU.mult)
                        return v.scalar_tensor_tensor(dst, src, cw[:, c, k:k + 1], dst, ALU.mult, ALU.add)

                    for c in range(NCH):
                        dve.wait_ge(xp_kept, i * NCH + c + 1)
                        for k in range(KCONV - 1):
                            link(conv(c, k))
                        conv(c, KCONV - 1).then_inc(conv_done, 1)
                    dve.wait_ge(dbl_kept, i + 1)
                    v.tensor_tensor(st[32:64, :], ps[bDBL][32:64, :], st_hi[32:64, :].bitcast(F32), ALU.subtract).then_inc(st_low, 1)
                    dve.wait_ge(dp_ps, i + 1)
                    for c in range(NCH):
                        m = v.tensor_scalar(p_[:, c, :], ps[bDP[c]][:], cvec[:, c, 1:2], None, ALU.add)
                    link(m)
                    v.tensor_scalar(w1[:], p_[:], -1.0, None, ALU.mult)
                    link(v.tensor_scalar(delta[:], p_[:], 0.0, None, ALU.max))
                    v.tensor_tensor(en[:], p_[:], w1[:], ALU.max).then_inc(p_done, 1)
                    dve.wait_ge(en_done, i + 1)
                    v.tensor_scalar(w1[:], en[:], 1.0, None, ALU.add).then_inc(w1_done, 1)
                    dve.wait_ge(w1_done, i + 1)
                    link(v.scalar_tensor_tensor(en[:], w1[:], 1.0, en[:], ALU.subtract, ALU.subtract))
                    link(v.tensor_tensor(delta[:], delta[:], en[:], ALU.subtract))
                    dve.wait_ge(lw_done, i + 1)
                    link(v.tensor_tensor(delta[:], delta[:], lw[:], ALU.add))
                    v.tensor_tensor(dx[:], delta[:], xt[:], ALU.mult).then_inc(dx_done, 1)
                    dve.wait_ge(dx_done, i + 1)
                    for q in range(NQ):
                        n, c = divmod(q, NCH)
                        dve.wait_ge(b_ps, i * NST + n + 1)
                        v.tensor_tensor(dbu[:, q % 2, :], dx[:, c, :], ps[bB[n % 2]][:], ALU.mult).then_inc(dbu_done, 1)
                        dve.wait_ge(dbu_done, i * NQ + q + 1)
                        dve.wait_ge(dA_done, i * NQ + q + 1)
                        if q >= 3:
                            dve.wait_ge(hc_done, i * NQ + q - 2)
                        for s in range(NS):
                            r = slice(s * T, (s + 1) * T)
                            m = v.tensor_tensor_scan(h[:, q % 3, r], dA[:, q % 3, r], dbu[:, q % 2, r], 0.0, ALU.mult, ALU.add)
                        m.then_inc(h_done, 1)
                    dve.wait_ge(sum_done, i * NQ + NQ)
                    for c in range(NCH):
                        m = v.scalar_tensor_tensor(y[:, c, :], xt[:, c, :], cvec[:, c, 2:3], ps[bY[c]][:], ALU.mult, ALU.add)
                    link(m)
                    v.tensor_tensor(y[:], y[:], sz[:], ALU.mult).then_inc(y_done, 1)
                    tail.dve(dve, link, i, i)
                    tail.dve_low(dve, i, i)
                    link.close()

    def window_attention(self):
        nc, I, ps = self.nc, self.ins, self.ps
        W, S, KC = 3, 2, T // P
        SCALE = 1.0 / 8.0 ** 0.5
        PAST = -1e30
        with ExitStack() as c:
            def sb(name, shape, dt=F32):
                return c.enter_context(nc.sbuf_tensor("a3_" + name, shape, dt))

            def sem(name):
                return self.semaphore("a3_" + name)

            def both(make, name, *a):
                return [make(f"{name}{s}", *a) for s in range(S)]

            w_in = sb("w_in", [P, 3 * D])
            wh, wl = sb("wh", [P, 3 * D], F32R), sb("wl", [P, 3 * D], F32R)
            wo, bo, one_row = sb("wo", [P, D]), sb("bo", [1, D]), sb("one_row", [1, P])
            vec, heads = sb("vec", [P, 3]), sb("heads", [P, P])
            q, kp, vp = both(sb, "q", [P, T]), both(sb, "kp", [P, W - 1 + T]), both(sb, "vp", [P, W - 1 + T])
            prod, e, pv = both(sb, "prod", [P, W, T]), both(sb, "e", [P, W, T]), both(sb, "pv", [P, W, T])
            m, den, rec, o, on = (both(sb, n, [P, T]) for n in ("m", "den", "rec", "o", "on"))
            bA, bB, bC = [ps[0], ps[4]], [ps[1], ps[5]], [ps[2], ps[6]]
            tail = [Tail(self, c, "a3", s, KC, bB[s][:, T:2 * T], bB[s][:, 0:T]) for s in range(S)]
            loaded, w_high, w_low = sem("weights_loaded"), sem("weights_high"), sem("weights_low")
            qk_ps, v_ps, qk_kept, v_kept = both(sem, "qk_ready"), both(sem, "v_ready"), both(sem, "qk_kept"), both(sem, "v_kept")
            prod_done, prod2_done, s_ps, shifted = (both(sem, "products"), both(sem, "products2"), both(sem, "scores_ready"),
                                                    both(sem, "shifted"))
            exp_done, pv_done, on_done = both(sem, "exp_done"), both(sem, "pv_products"), both(sem, "normalised")
            chain = both(sem, "dve_chain")
            block = c.enter_context(nc.Block())
            loads = ((w_in, "a3_w"), (wo, "a3_wo"), (bo, "a3_bo"), (vec, "a3_vec"), (heads, "a3_heads"), (one_row, "one_row"))

            @block.sync
            def _(sp):
                for dst, src in loads:
                    sp.dma_start(dst[:], I[src]).then_inc(loaded, 16)

            @block.gpsimd
            def _(pool):
                g = nc.gpsimd
                with pool.Fori(0, B // S) as i:
                    for s in range(S):
                        pool.wait_ge(qk_kept[s], i + 1)
                        g.tensor_tensor(prod[s][:, 2, :], q[s][:], kp[s][:, 0:T], ALU.mult).then_inc(prod2_done[s], 1)
                    for s in range(S):
                        pool.wait_ge(exp_done[s], i + 1)
                        pool.wait_ge(v_kept[s], i + 1)
                        g.tensor_tensor(pv[s][:, 2, :], e[s][:, 2, :], vp[s][:, 0:T], ALU.mult)
                        g.tensor_tensor(pv[s][:, 1, :], e[s][:, 1, :], vp[s][:, 1:T + 1], ALU.mult).then_inc(pv_done[s], 1)
                    for s in range(S):
                        tail[s].pool(pool, i, i * S + s)

            @block.scalar
            def _(act):
                a = nc.scalar
                act.wait_ge(loaded, 16 * len(loads))
                a.activation(wh[:], w_in[:], ACT.Copy).then_inc(w_high, 1)
                with act.Fori(0, B // S) as i:
                    for s in range(S):
                        act.wait_ge(qk_ps[s], i + 1)
                        a.activation(q[s][:], bA[s][:, 0:T], ACT.Identity, bias=vec[:, 0:1])
                        a.activation(kp[s][:, W - 1:], bA[s][:, T:2 * T], ACT.Identity, bias=vec[:, 1:2]).then_inc(qk_kept[s], 1)
                        act.wait_ge(v_ps[s], i + 1)
                        a.activation(vp[s][:, W - 1:], bB[s][:, 0:T], ACT.Identity, bias=vec[:, 2:3]).then_inc(v_kept[s], 1)
                    for s in range(S):
                        act.wait_ge(shifted[s], i + 1)
                        a.activation(e[s][:], e[s][:], ACT.Exp, scale=SCALE).then_inc(exp_done[s], 1)
                    for s in range(S):
                        tail[s].act(act, i, i * S + s)

            @block.tensor
            def _(pe):
                pe.wait_ge(w_high, 1)
                pe.wait_ge(w_low, 1 + 2 * S)
                with pe.Fori(0, B // S) as i:
                    for s in range(S):
                        seq = i * S + s
                        pe.wait_ge(tail[s].done, i + 1)
                        xh, xl = self.XH[:, bass.ds(seq * T, T)], self.XL[:, bass.ds(seq * T, T)]
                        mm3(nc, bA[s][:, 0:T], wh[:, 0:D], wl[:, 0:D], xh, xl)
                        mm3(nc, bA[s][:, T:2 * T], wh[:, D:2 * D], wl[:, D:2 * D], xh, xl).then_inc(qk_ps[s], 1)
                        mm3(nc, bB[s][:, 0:T], wh[:, 2 * D:], wl[:, 2 * D:], xh, xl).then_inc(v_ps[s], 1)
                    for s in range(S):
                        pe.wait_ge(prod_done[s], i + 1)
                        nc.tensor.matmul(bC[s][:], heads[:], prod[s][:, 0:2, :].rearrange("p j t -> p (j t)"), start=True, stop=True)
                        pe.wait_ge(prod2_done[s], i + 1)
                        nc.tensor.matmul(bA[s][:, 0:T], heads[:], prod[s][:, 2, :], start=True, stop=True).then_inc(s_ps[s], 1)
                    for s in range(S):
                        pe.wait_ge(on_done[s], i + 1)
                        for t in range(KC):
                            out = bB[s][:, T + t * P:T + (t + 1) * P]
                            nc.tensor.matmul(out, on[s][:, t * P:(t + 1) * P], wo[:], start=True, stop=False)
                            mm = nc.tensor.matmul(out, one_row[:], bo[:], start=False, stop=True)
                        mm.then_inc(tail[s].y_ps, 1)
                    for s in range(S):
                        tail[s].pe(pe, i)

            @block.vector
            def _(dve):
                v = nc.vector
                for s in range(S):
                    v.memset(kp[s][:, 0:W - 1], 0.0).then_inc(w_low, 1)
                    v.memset(vp[s][:, 0:W - 1], 0.0).then_inc(w_low, 1)
                dve.wait_ge(w_high, 1)
                v.tensor_tensor(wl[:], w_in[:], wh[:].bitcast(F32), ALU.subtract).then_inc(w_low, 1)
                for s in range(S):
                    dve.sem_inc(tail[s].done, 1)
                with dve.Fori(0, B // S) as i:
                    link = [Chain(dve, chain[s], i, 9) for s in range(S)]
                    for s in range(S):
                        dve.wait_ge(qk_kept[s], i + 1)
                        v.tensor_tensor(prod[s][:, 0, :], q[s][:], kp[s][:, 2:T + 2], ALU.mult)
                        v.tensor_tensor(prod[s][:, 1, :], q[s][:], kp[s][:, 1:T + 1], ALU.mult).then_inc(prod_done[s], 1)
                    for s in range(S):
                        dve.wait_ge(s_ps[s], i + 1)
                        v.memset(bC[s][:, T:T + 1], PAST)
                        link[s](v.memset(bA[s][:, 0:2], PAST))
                        link[s](v.tensor_reduce(m[s][:], bC[s][:].rearrange("p (j t) -> p t j", j=2), AX.X, ALU.max))
                        link[s](v.tensor_tensor(m[s][:], m[s][:], bA[s][:, 0:T], ALU.max))
                        v.tensor_tensor(e[s][:, 0:2, :], bC[s][:].rearrange("p (j t) -> p j t", j=2),
                                        m[s][:].unsqueeze(1).broadcast_to([P, 2, T]), ALU.subtract)
                        v.tensor_tensor(e[s][:, 2, :], bA[s][:, 0:T], m[s][:], ALU.subtract).then_inc(shifted[s], 1)
                    for s in range(S):
                        dve.wait_ge(exp_done[s], i + 1)
                        link[s](v.tensor_reduce(den[s][:], e[s][:].rearrange("p j t -> p t j"), AX.X, ALU.add))
                        v.reciprocal(rec[s][:], den[s][:])
                        dve.wait_ge(v_kept[s], i + 1)
                        link[s](v.tensor_tensor(pv[s][:, 0, :], e[s][:, 0, :], vp[s][:, 2:T + 2], ALU.mult))
                        dve.wait_ge(pv_done[s], i + 1)
                        link[s](v.tensor_reduce(o[s][:], pv[s][:].rearrange("p j t -> p t j"), AX.X, ALU.add))
                        v.tensor_tensor(on[s][:], o[s][:], rec[s][:], ALU.mult).then_inc(on_done[s], 1)
                    for s in range(S):
                        tail[s].dve(dve, link[s], i, i * S + s)
                    for s in range(S):
                        tail[s].dve_low(dve, i, i * S + s)
                        link[s].close()

    def fp4_mlp(self):
        nc, I, ps = self.nc, self.ins, self.ps
        S, KC, BL = 2, T // P, 16
        NI = 352
        NCH = (NI + P - 1) // P
        NIP = NCH * P
        NH = KC * NI
        NX = KC * D
        NWQ = 3 * NIP // S
        assert NWQ <= NH and NI % BL == 0
        QSTEPS = 9
        with ExitStack() as c:
            def sb(name, shape, dt=F32):
                return c.enter_context(nc.sbuf_tensor("f3_" + name, shape, dt))

            def sem(name):
                return self.semaphore("f3_" + name)

            def both(make, name, *a):
                return [make(f"{name}{s}", *a) for s in range(S)]

            w_in, wq = sb("w_in", [P, 3 * NIP]), sb("wq", [P, 3 * NIP])
            wg, wu, wd = sb("wg", [P, NIP]), sb("wu", [P, NIP]), sb("wd", [P, NCH, D])
            ab, sg, v_, t_, u_, ss_ = (both(sb, n, [P, NH]) for n in ("abs", "sign", "scaled", "code", "upper", "signscale"))
            am, sc = both(sb, "absmax", [P, NH // BL]), both(sb, "scale", [P, NH // BL])
            rsc = both(sb, "rscale", [P, NH // BL])
            u5 = both(sb, "five", [P, NH])
            xq, xqt = both(sb, "xq", [P, KC, D]), both(sb, "xqt", [P, T])
            sl, h, hq = both(sb, "silu", [P, KC, NI]), both(sb, "h", [P, NH]), both(sb, "hq", [P, KC, NIP])
            hqt = both(sb, "hqt", [P, NCH, T])
            bank = [ps[0:4], ps[4:8]]
            tail = [Tail(self, c, "f3", s, KC, bank[s][2][:, 0:T], None, last=True) for s in range(S)]
            loaded, w_t, w_kept, zeros = sem("weights_loaded"), sem("weightsT_ready"), sem("weightsT_kept"), sem("zeros")
            abs_done, v_done, u_done, q_done = (both(sem, "abs_done"), both(sem, "scaled_done"), both(sem, "upper_done"),
                                               both(sem, "quantised"))
            pch = both(sem, "pool_chain")
            xqt_ps, xqt_kept, gu_ps, silu_done, h_done = (both(sem, "xqT_ready"), both(sem, "xqT_kept"), both(sem, "gate_up_ready"),
                                                         both(sem, "silu_done"), both(sem, "h_done"))
            hqt_ps, hqt_kept = both(sem, "hqT_ready"), both(sem, "hqT_kept")
            chain, once = both(sem, "dve_chain"), sem("dve_once")
            block = c.enter_context(nc.Block())

            def wide(t, N):
                return t[:, 0:N // BL].unsqueeze(2).broadcast_to([P, N // BL, BL])

            def split16(t, N):
                return t[:, 0:N].rearrange("p (b k) -> p b k", k=BL)

            def quant_act(s, src, N):
                nc.scalar.activation(ab[s][:, 0:N], src, ACT.Abs)
                nc.scalar.activation(sg[s][:, 0:N], src, ACT.Sign).then_inc(abs_done[s], 1)

            def quant_dve(dve, link, s, n, N, out, view):
                v = nc.vector
                dve.wait_ge(abs_done[s], n + 1)
                link(v.tensor_reduce(am[s][:, 0:N // BL], split16(ab[s], N), AX.X, ALU.max))
                link(v.tensor_scalar(sc[s][:, 0:N // BL], am[s][:, 0:N // BL], 1.0 / 6.0, 1e-12, ALU.mult, ALU.max))
                link(v.reciprocal(rsc[s][:, 0:N // BL], sc[s][:, 0:N // BL]))
                v.tensor_tensor(split16(v_[s], N), split16(ab[s], N), wide(rsc[s], N), ALU.mult).then_inc(v_done[s], 1)
                dve.wait_ge(v_done[s], n + 1)
                link(v.tensor_scalar(t_[s][:, 0:N], v_[s][:, 0:N], 0.25, None, ALU.is_gt))
                for mid in (0.75, 1.25, 1.75):
                    link(v.scalar_tensor_tensor(t_[s][:, 0:N], v_[s][:, 0:N], mid, t_[s][:, 0:N], ALU.is_gt, ALU.add))
                dve.wait_ge(u_done[s], n + 1)
                link(v.scalar_tensor_tensor(u_[s][:, 0:N], v_[s][:, 0:N], 2.5, u_[s][:, 0:N], ALU.is_gt, ALU.add))
                link(v.scalar_tensor_tensor(t_[s][:, 0:N], u_[s][:, 0:N], 2.0, t_[s][:, 0:N], ALU.mult, ALU.add))
                v.scalar_tensor_tensor(out, view(t_[s][:, 0:N]), 0.5, view(ss_[s][:, 0:N]), ALU.mult,
                                       ALU.mult).then_inc(q_done[s], 1)

            def quant_pool(pool, s, n, N):
                g = nc.gpsimd
                pool.wait_ge(v_done[s], n + 1)
                g.tensor_tensor(split16(ss_[s], N), split16(sg[s], N), wide(sc[s], N), ALU.mult)
                g.tensor_scalar(u5[s][:, 0:N], v_[s][:, 0:N], 5.0, 2.0, ALU.is_gt, ALU.mult)
                g.tensor_scalar(u_[s][:, 0:N], v_[s][:, 0:N], 3.5, None, ALU.is_gt).then_inc(pch[s], 1)
                pool.wait_ge(pch[s], n + 1)
                g.tensor_tensor(u_[s][:, 0:N], u_[s][:, 0:N], u5[s][:, 0:N], ALU.add).then_inc(u_done[s], 1)

            @block.sync
            def _(sp):
                sp.dma_start(w_in[:], I["f3_w"]).then_inc(loaded, 16)

            @block.gpsimd
            def _(pool):
                for s in range(S):
                    quant_pool(pool, s, 0, NWQ)
                    pool.sem_inc(tail[s].x_kept, 1)
                with pool.Fori(0, B // S) as i:
                    for s in range(S):
                        quant_pool(pool, s, i * 2 + 1, NX)
                    for s in range(S):
                        quant_pool(pool, s, i * 2 + 2, NH)
                    for s in range(S):
                        tail[s].pool(pool, i, i * S + s)

            @block.scalar
            def _(act):
                a = nc.scalar
                act.wait_ge(loaded, 16)
                for s in range(S):
                    quant_act(s, w_in[:, s * NWQ:(s + 1) * NWQ], NWQ)
                act.wait_ge(w_t, 1)
                a.activation(wg[:], ps[0][:, 0:NIP], ACT.Copy)
                a.activation(wu[:], ps[1][:, 0:NIP], ACT.Copy)
                a.activation(wd[:], ps[2][:, 0:NIP].rearrange("p (c d) -> p c d", c=NCH), ACT.Copy).then_inc(w_kept, 1)
                with act.Fori(0, B // S) as i:
                    for s in range(S):
                        act.wait_ge(tail[s].done, i + 1)
                        act.wait_ge(q_done[s], i * 2 + 1)
                        quant_act(s, self.X[:, bass.ds((i * S + s) * KC, KC), :].rearrange("p c d -> p (c d)"), NX)
                    for s in range(S):
                        act.wait_ge(xqt_ps[s], i + 1)
                        a.activation(xqt[s][:], bank[s][0][:, 0:T], ACT.Copy).then_inc(xqt_kept[s], 1)
                    for s in range(S):
                        act.wait_ge(gu_ps[s], i + 1)
                        for t in range(KC):
                            m = a.activation(sl[s][:, t, :], bank[s][t][:, 0:NI], ACT.Silu)
                        m.then_inc(silu_done[s], 1)
                    for s in range(S):
                        act.wait_ge(h_done[s], i + 1)
                        quant_act(s, h[s][:], NH)
                    for s in range(S):
                        act.wait_ge(hqt_ps[s], i + 1)
                        a.activation(hqt[s][:, 0:2, :], bank[s][0][:].rearrange("p (c t) -> p c t", c=2), ACT.Copy)
                        a.activation(hqt[s][:, 2, :], bank[s][1][:, 0:T], ACT.Copy).then_inc(hqt_kept[s], 1)

            @block.tensor
            def _(pe):
                for s in range(S):
                    pe.wait_ge(q_done[s], 1)
                for k in range(3):
                    for j in range(NCH):
                        col = slice((k * NCH + j) * P, (k * NCH + j + 1) * P)
                        m = nc.tensor.transpose(ps[k][:, j * P:(j + 1) * P], wq[:, col], self.idF[:])
                m.then_inc(w_t, 1)
                pe.wait_ge(w_kept, 1)
                pe.wait_ge(zeros, S)
                with pe.Fori(0, B // S) as i:
                    for s in range(S):
                        pe.wait_ge(tail[s].done, i + 1)
                        pe.wait_ge(q_done[s], i * 2 + 2)
                        for t in range(KC):
                            m = nc.tensor.transpose(bank[s][0][:, t * P:(t + 1) * P], xq[s][:, t, :], self.idF[:])
                        m.then_inc(xqt_ps[s], 1)
                    for s in range(S):
                        pe.wait_ge(xqt_kept[s], i + 1)
                        for t in range(KC):
                            nc.tensor.matmul(bank[s][t][:, 0:NI], xqt[s][:, t * P:(t + 1) * P], wg[:, 0:NI], start=True, stop=True)
                            m = nc.tensor.matmul(bank[s][2 + t][:, 0:NI], xqt[s][:, t * P:(t + 1) * P], wu[:, 0:NI],
                                                 start=True, stop=True)
                        m.then_inc(gu_ps[s], 1)
                    for s in range(S):
                        pe.wait_ge(q_done[s], i * 2 + 3)
                        for k in range(NCH):
                            for t in range(KC):
                                o_ = bank[s][k // 2][:, (k % 2) * T + t * P:(k % 2) * T + (t + 1) * P]
                                m = nc.tensor.transpose(o_, hq[s][:, t, k * P:(k + 1) * P], self.idF[:])
                        m.then_inc(hqt_ps[s], 1)
                    for s in range(S):
                        pe.wait_ge(hqt_kept[s], i + 1)
                        for t in range(KC):
                            for k in range(NCH):
                                m = nc.tensor.matmul(bank[s][2][:, t * P:(t + 1) * P], hqt[s][:, k, t * P:(t + 1) * P],
                                                     wd[:, k, :], start=(k == 0), stop=(k == NCH - 1))
                        m.then_inc(tail[s].y_ps, 1)

            @block.vector
            def _(dve):
                v = nc.vector
                for s in range(S):
                    v.memset(hq[s][:, :, NI:], 0.0).then_inc(zeros, 1)
                link = Chain(dve, once, 0, S * QSTEPS)
                for s in range(S):
                    quant_dve(dve, link, s, 0, NWQ, wq[:, s * NWQ:(s + 1) * NWQ], lambda x: x)
                link.close()
                with dve.Fori(0, B // S) as i:
                    links = [Chain(dve, chain[s], i, 2 * QSTEPS + 3) for s in range(S)]
                    for s in range(S):
                        quant_dve(dve, links[s], s, i * 2 + 1, NX, xq[s][:].rearrange("p c d -> p (c d)"), lambda x: x)
                    for s in range(S):
                        dve.wait_ge(silu_done[s], i + 1)
                        for t in range(KC):
                            m = v.tensor_tensor(h[s][:, t * NI:(t + 1) * NI], bank[s][2 + t][:, 0:NI], sl[s][:, t, :], ALU.mult)
                        m.then_inc(h_done[s], 1)
                    for s in range(S):
                        quant_dve(dve, links[s], s, i * 2 + 2, NH, hq[s][:, :, 0:NI],
                                  lambda x: x.rearrange("p (c n) -> p c n", c=KC))
                    for s in range(S):
                        tail[s].dve(dve, links[s], i, i * S + s)
                        links[s].close()


def _rope_table(n_t, dim):
    import numpy as np
    inv = (1.0 / (10000.0 ** (np.arange(0, dim, 2, dtype=np.float32) / np.float32(dim)))).astype(np.float32)
    f = np.arange(n_t, dtype=np.float32)[:, None] * inv[None, :]
    return np.cos(f).astype(np.float32), np.sin(f).astype(np.float32)


def layout(inp):
    import numpy as np
    a = {}
    f = {k: np.asarray(v) for k, v in inp.items()}
    x = f["L0_attn_x"].reshape(NTOK, D)
    a["x"], a["xt"] = x, np.ascontiguousarray(x.T)
    a["ident"] = np.eye(P, dtype=np.float32)
    a["one_row"] = np.ones((1, P), np.float32)
    H, DH, DL = 16, 8, 32
    swap = np.arange(D).reshape(H, 2, DH // 2)[:, ::-1, :].reshape(-1)
    wq, wd = f["L0_attn_Wq"], f["L0_attn_Wdown"]
    a["a0_w"] = np.concatenate([wq, wq[:, swap], wd], 1)
    wup = f["L0_attn_Wup"].reshape(DL, H, 2 * DH)
    wk, wv = wup[:, :, :DH].reshape(DL, D), wup[:, :, DH:].reshape(DL, D)
    a["a0_up"] = np.concatenate([wk, wk[:, swap], wv], 1)
    a["a0_wout"], a["a0_bout"] = f["L0_attn_Wout"], f["L0_attn_bout"][None]
    bup, bq = f["L0_attn_bup"].reshape(H, 2 * DH), f["L0_attn_bq"]
    bk, bvv = bup[:, :DH].reshape(-1), bup[:, DH:].reshape(-1)
    vec = np.zeros((P, 6), np.float32)
    vec[:DL, 2] = f["L0_attn_bdown"]
    for n, b in ((0, bq), (1, bq[swap]), (3, bk), (4, bk[swap]), (5, bvv)):
        vec[:, n] = b
    a["a0_vec"] = vec
    cos, sin = _rope_table(T, DH)
    i = np.arange(D) % (DH // 2)
    sign = np.where(np.arange(D) % DH < DH // 2, -1, 1).astype(np.float32)
    a["a0_cs"] = np.concatenate([cos[:, i].T, sin[:, i].T * sign[:, None]], 1)
    def second(w):
        n, h, d = w.shape
        return w.reshape(n, h // P, P, d).transpose(0, 2, 1, 3).reshape(n * P, -1)

    for tag in ("f0", "f1", "f2"):
        a[tag + "_rank"] = np.broadcast_to(np.arange(8, 0, -1).astype(np.float32), (P, 8))
        a[tag + "_ones"] = np.ones((2, P), np.float32)
    wide = np.zeros((3, P, P), np.float32)
    wide[0, :32, :8], wide[1, :, :8], wide[2, :, :8] = f["L0_ffn_wg2"], f["L1_ffn_centroids"], f["L2_ffn_gate_w"].T
    a["f0_wr"], a["f0_wg2"], a["f0_bg1"] = f["L0_ffn_wg1"], wide[0, :32], f["L0_ffn_bg1"][:, None]
    a["f0_w1"], a["f0_w2"] = f["L0_ffn_w_in"].reshape(8 * D, -1), second(f["L0_ffn_w_out"])
    cat = np.concatenate
    a["f1_wr"], a["f2_wr"] = wide[1], wide[2]
    a["f1_w1"] = cat([f["L1_ffn_W1_s"], f["L1_ffn_W1_r"]]).reshape(10 * D, -1)
    a["f1_w2"] = second(cat([f["L1_ffn_W2_s"], f["L1_ffn_W2_r"]]))
    a["f1_b1"] = cat([f["L1_ffn_b1_s"], f["L1_ffn_b1_r"]]).reshape(-1, P).T
    a["f1_b2"] = cat([f["L1_ffn_b2_s"], f["L1_ffn_b2_r"]])
    a["f1_gs"] = np.stack([f["L1_ffn_g_shared"]] * 2 + [f["L1_ffn_g_routed"]] * 8, 1)
    a["f2_w1"] = cat([f["L2_ffn_shared_w1"][None], f["L2_ffn_experts_w1"]]).transpose(0, 2, 1).reshape(9 * D, -1)
    a["f2_w2"] = second(cat([f["L2_ffn_shared_w2"][None], f["L2_ffn_experts_w2"]]).transpose(0, 2, 1))
    swap = np.arange(1024).reshape(-1, 2)[:, ::-1].reshape(-1)
    uq, uk, uv = (f[f"L1_attn_w_up_{n}"] for n in "qkv")
    a["a1_wd"] = cat([f["L1_attn_w_down_q"], f["L1_attn_w_down_kv"]]).T
    a["a1_up"] = cat([cat([uq.T, uq[swap].T, np.zeros_like(uv.T)], 1), cat([uk.T, uk[swap].T, uv.T], 1)])
    a["a1_wout"] = f["L1_attn_w_out"].T.reshape(8, P, D).transpose(1, 0, 2)
    a["a1_ln"] = np.stack([f["L1_attn_ln_scale"], f["L1_attn_ln_bias"]], 1)
    inv = 1.0 / 10000.0 ** (np.arange(0, 64, 2, dtype=np.float32) / 64)
    freqs = np.outer(np.arange(T, dtype=np.float32), inv)
    pair = np.arange(P) % 64 // 2
    tabs = [cat([g_(freqs), g_(freqs)], -1)[:, ::2][:, pair].T.astype(np.float32) for g_ in (np.cos, np.sin)]
    tabs[1] = tabs[1] * np.where(np.arange(P) % 2 == 0, -1, 1).astype(np.float32)[:, None]
    a["a1_cs"] = cat(tabs, 1)
    a["a1_sel"] = np.repeat(np.eye(32, 16, dtype=np.float32), P, 1)
    a["m2_w"] = f["L2_attn_in_proj_w"].T
    xpw = f["L2_attn_x_proj_w"].T.reshape(2, P, 40)
    xp = np.zeros((P, 2, P), np.float32)
    for k in range(2):
        xp[:, k, 0:32] = xp[:, k, 32:64] = xpw[k][:, 8:40]
        xp[:, k, 64:72] = xpw[k][:, 0:8]
    dtw = np.zeros((P, 256), np.float32)
    dtw[64:72] = f["L2_attn_dt_proj_w"].T
    sel = np.zeros((64, 32, P), np.float32)
    for n in range(32):
        sel[n, n] = sel[32 + n, n] = 1
    halves = lambda w: w.reshape(2, P, -1).transpose(1, 0, 2)
    a["m2_xp"], a["m2_dt"], a["m2_sel"] = xp, dtw, sel.reshape(64, -1)
    a["m2_out"], a["m2_cw"], a["m2_alog"] = halves(f["L2_attn_out_proj_w"].T), halves(f["L2_attn_conv_w"]), halves(f["L2_attn_A_log"])
    a["m2_cvec"] = halves(np.stack([f["L2_attn_conv_b"], f["L2_attn_dt_proj_b"], f["L2_attn_D"]], 1))
    def rows(w):
        w = cat([w, np.zeros((384 - w.shape[0], D), np.float32)])
        return w.reshape(3, P, D).transpose(1, 0, 2).reshape(P, -1)

    wd = cat([f["L3_ffn_w_down"], np.zeros((D, 384 - 352), np.float32)], 1)
    a["f3_w"] = cat([rows(f["L3_ffn_w_gate"]), rows(f["L3_ffn_w_up"]), wd], 1)
    a["a3_w"] = cat([f["L3_attn_Wq"].T, f["L3_attn_Wk"].T, f["L3_attn_Wv"].T], 1)
    a["a3_wo"], a["a3_bo"] = f["L3_attn_Wo"].T, f["L3_attn_bo"][None]
    a["a3_vec"] = np.stack([f["L3_attn_bq"], f["L3_attn_bk"], f["L3_attn_bv"]], 1)
    a["a3_heads"] = np.kron(np.eye(16, dtype=np.float32), np.ones((8, 8), np.float32))
    return {k: np.ascontiguousarray(v) for k, v in a.items()}


def kernel(**inputs):
    import numpy as np
    import concourse.bacc as bacc
    from concourse.bass_utils import run_bass_kernel_spmd as run

    nc = bacc.Bacc("TRN2", target_bir_lowering=False, num_devices=1)
    arrays = {f"in_{k}": v for k, v in layout(inputs).items()}
    ins = {k[3:]: nc.dram_tensor(k, v.shape, mybir.dt.from_np(v.dtype), kind="ExternalInput").ap()
           for k, v in arrays.items()}
    out = nc.dram_tensor("out_0", (NTOK, D), F32, kind="ExternalOutput").ap()
    Program(nc, ins, out).build()
    r = run(nc, [arrays], core_ids=[0])
    return r.results[0]["out_0"].reshape(B, T, D)
```

```python
from contextlib import ExitStack

import concourse.bass as bass
from concourse import mybir

F32, F32R, BF16 = mybir.dt.float32, mybir.dt.float32r, mybir.dt.bfloat16
U32 = mybir.dt.uint32
ALU = mybir.AluOpType
ACT = mybir.ActivationFunctionType
AX = mybir.AxisListType

P = 128
B, T, D = 16, 256, 128
NTOK = B * T
NTILE = NTOK // P
LN_EPS = 1e-5
PHASES = (0, 8)


class Chain:

    def __init__(self, eng, sem, i, per):
        self.eng, self.sem, self.base, self.per, self.k = eng, sem, i * per, per, 0

    def __call__(self, ins):
        self.k += 1
        ins.then_inc(self.sem, 1)
        self.eng.wait_ge(self.sem, self.base + self.k)

    def close(self):
        assert self.k == self.per, f"this chain has {self.k} steps a turn, not {self.per}"


def mm3(nc, out, wh, wl, xh, xl, start=True, stop=True):
    nc.tensor.matmul(out, wh, xh, start=start, stop=False)
    nc.tensor.matmul(out, wl, xh, start=False, stop=False)
    return nc.tensor.matmul(out, wh, xl, start=False, stop=stop)


class Tail:

    def __init__(self, prog, c, tag, s, n, out_ps, turn_ps, gain=1.0, last=False):
        nc = self.nc = prog.nc
        self.prog, self.n, self.out_ps, self.turn_ps, self.gain, self.last = prog, n, out_ps, turn_ps, gain, last

        def sb(name, shape):
            return c.enter_context(nc.sbuf_tensor(f"{tag}_{name}{s}", shape, F32))

        def sem(name):
            return prog.semaphore(f"{tag}_{name}{s}")

        self.y, self.xn = sb("y", [P, n, D]), sb("xn", [P, n, D])
        self.st, self.mv, self.ve, self.rs = sb("st", [P, n, 6]), sb("mv", [P, n, 2]), sb("ve", [P, n]), sb("rs", [P, n])
        self.y_ps, self.ve_done, self.rs_done, self.xn_done = (sem("out_ready"), sem("var_ready"), sem("rstd_ready"),
                                                              sem("xn_ready"))
        self.xnt_ps, self.xh_kept, self.x_kept, self.done = sem("xnT_ready"), sem("xh_kept"), sem("x_kept"), sem("turn_done")
        if last:
            self.done = self.x_kept

    def dve(self, dve, link, i, seq):
        self.dve_stats(dve, link, i, seq)
        self.dve_norm(dve, i)

    def dve_stats(self, dve, link, i, seq):
        v, n, prog = self.nc.vector, self.n, self.prog
        dve.wait_ge(self.y_ps, i + 1)
        link(v.scalar_tensor_tensor(self.y[:], prog.X[:, bass.ds(seq * n, n), :], self.gain,
                                    self.out_ps.rearrange("p (c d) -> p c d", c=n), ALU.mult, ALU.add))
        prog.norm_stats(link, self.y, self.st, self.mv, self.ve[:], n, LN_EPS).then_inc(self.ve_done, 1)

    def dve_norm(self, dve, i):
        v, n = self.nc.vector, self.n
        dve.wait_ge(self.rs_done, i + 1)
        for t in range(n):
            m = v.tensor_scalar(self.xn[:, t, :], self.y[:, t, :], self.mv[:, t, 0:1], self.rs[:, t:t + 1],
                                ALU.subtract, ALU.mult)
        m.then_inc(self.xn_done, 1)

    def dve_low(self, dve, i, seq):
        w = self.n * P
        dve.wait_ge(self.xh_kept, i + 1)
        dve.wait_ge(self.x_kept, i + 1)
        self.nc.vector.tensor_tensor(self.prog.XL[:, bass.ds(seq * w, w)], self.turn_ps,
                                     self.prog.XH[:, bass.ds(seq * w, w)].bitcast(F32),
                                     ALU.subtract).then_inc(self.done, 1)

    def pool(self, pool, i, seq):
        g, n = self.nc.gpsimd, self.n
        pool.wait_ge(self.ve_done, i + 1)
        g.tensor_tensor(self.rs[:], self.ve[:], self.prog.mhalf[:, 0:n], ALU.pow).then_inc(self.rs_done, 1)
        pool.wait_ge(self.xn_done, i + 1)
        g.tensor_copy(self.prog.X[:, bass.ds(seq * n, n), :], self.xn[:]).then_inc(self.x_kept, 1)

    def act(self, act, i, seq):
        w = self.n * P
        act.wait_ge(self.xnt_ps, i + 1)
        self.nc.scalar.activation(self.prog.XH[:, bass.ds(seq * w, w)], self.turn_ps, ACT.Copy).then_inc(self.xh_kept, 1)

    def pe(self, pe, i):
        pe.wait_ge(self.xn_done, i + 1)
        for t in range(self.n):
            m = self.nc.tensor.transpose(self.turn_ps[:, t * P:(t + 1) * P], self.xn[:, t, :], self.prog.idF[:])
        m.then_inc(self.xnt_ps, 1)


class Program:
    def __init__(self, nc, ins, out):
        self.nc, self.ins, self.out = nc, ins, out
        self.ctx, self.phase_sems = ExitStack(), []

    def build(self):
        nc = self.nc
        with self.ctx:
            c = self.ctx
            self.X = c.enter_context(nc.sbuf_tensor("X", [P, NTILE, D], F32))
            self.XH = c.enter_context(nc.sbuf_tensor("XH", [P, NTOK], F32R))
            self.XL = c.enter_context(nc.sbuf_tensor("XL", [P, NTOK], F32R))
            self.idF = c.enter_context(nc.sbuf_tensor("idF", [P, P], F32))
            self.idB = c.enter_context(nc.sbuf_tensor("idB", [P, P], BF16))
            self.mhalf = c.enter_context(nc.sbuf_tensor("mhalf", [P, 8], F32))
            self.pad = c.enter_context(nc.sbuf_tensor("pad", [P, 1], F32))
            self.ps = [c.enter_context(nc.psum_tensor(f"bank{i}", [P, 512], F32)) for i in range(8)]
            self.load_x()
            self.clear_semaphores()
            phases = [self.head_attention,
                      lambda: self.mixture("f0", "mlp", ACT.Gelu, 0, 2),
                      self.latent_attention,
                      lambda: self.mixture("f1", "sigmoid", ACT.Gelu, 2, 4, rms=True, biases=True),
                      self.selective_scan,
                      lambda: self.mixture("f2", "logits", ACT.Silu, 1, 4),
                      self.window_attention,
                      self.fp4_mlp]
            for f in phases[PHASES[0]:PHASES[1]]:
                f()
                self.clear_semaphores()
            self.store_x()

    def semaphore(self, name):
        self.phase_sems.append(self.nc.alloc_semaphore(name=name))
        return self.phase_sems[-1]

    def clear_semaphores(self):
        self.nc.clear_and_free_semaphores(self.phase_sems)
        self.nc.all_engine_barrier()
        self.phase_sems = []

    def load_x(self):
        nc = self.nc
        x_in, xh_done, const_in, fin0 = (self.semaphore(n) for n in ("x_in", "xh_done", "const_in", "x_low_done"))
        with nc.sbuf_tensor("xt_in", [P, NTOK], F32) as xt_in, nc.Block() as block:
            CH = NTOK // 4

            @block.sync
            def _(sp):
                for k in range(4):
                    sp.dma_start(xt_in[:, k * CH:(k + 1) * CH], self.ins["xt"][:, k * CH:(k + 1) * CH]).then_inc(x_in, 16)
                    sp.wait_ge(x_in, 16 * (k + 1))
                sp.dma_start(self.X[:], self.ins["x"].rearrange("(n p) d -> p n d", p=P)).then_inc(const_in, 16)
                sp.dma_start(self.idF[:], self.ins["ident"]).then_inc(const_in, 16)
                sp.wait_ge(const_in, 32)

            @block.scalar
            def _(act):
                for k in range(4):
                    act.wait_ge(x_in, 16 * (k + 1))
                    act.activation(self.XH[:, k * CH:(k + 1) * CH], xt_in[:, k * CH:(k + 1) * CH],
                                   ACT.Copy).then_inc(xh_done, 1)

            @block.vector
            def _(dve):
                dve.memset(self.mhalf[:], -0.5).then_inc(fin0, 1)
                for k in range(4):
                    dve.wait_ge(xh_done, k + 1)
                    s = slice(k * CH, (k + 1) * CH)
                    dve.tensor_tensor(self.XL[:, s], xt_in[:, s], self.XH[:, s].bitcast(F32), ALU.subtract).then_inc(fin0, 1)
                dve.wait_ge(const_in, 32)
                dve.tensor_copy(self.idB[:], self.idF[:]).then_inc(fin0, 1)
                dve.wait_ge(fin0, 6)

    def store_x(self):
        nc = self.nc
        out_done = self.semaphore("out_done")
        with nc.Block() as block:
            @block.sync
            def _(sp):
                sp.dma_start(self.out.rearrange("(n p) d -> p n d", p=P), self.X[:]).then_inc(out_done, 16)
                sp.wait_ge(out_done, 16)

    def norm_stats(self, link, y, st, mv, ve, n, eps):
        v = self.nc.vector
        for t in range(n):
            ins = v.bn_stats(st[:, t, :], y[:, t, :])
            if t == n - 1:
                link(ins)
        v.memset(self.pad[:], 0.0)
        for t in range(n):
            ins = v.bn_aggr(mv[:, t, :], st[:, t, :])
            if t == n - 1:
                link(ins)
        return v.tensor_scalar(ve, mv[:, :, 1], eps, None, ALU.add)

    def head_attention(self):
        nc, I, ps = self.nc, self.ins, self.ps
        H, DH, DL = 16, 8, 32
        SCALE = 1.0 / float(DH) ** 0.5
        KC = T // P
        S = 2
        PER_DVE = 17
        with ExitStack() as c:
            def sb(name, shape, dt=F32):
                return c.enter_context(nc.sbuf_tensor("a0_" + name, shape, dt))

            def sem(name):
                return self.semaphore("a0_" + name)

            def both(make, name, *a):
                return [make(f"{name}{s}", *a) for s in range(S)]

            NW = 2 * D + DL
            NU = 3 * D
            w_in, up_in = sb("w_in", [P, NW]), sb("up_in", [DL, NU])
            wh, wl = sb("wh", [P, NW], F32R), sb("wl", [P, NW], F32R)
            uh, ul = sb("uh", [DL, NU], F32R), sb("ul", [DL, NU], F32R)
            wout, bout, one_row = sb("wout", [P, D]), sb("bout", [1, D]), sb("one_row", [1, P])
            vec, cs = sb("vec", [P, 6]), sb("cs", [P, 2 * T])
            lat_h, lat_l = both(sb, "lat_h", [DL, T], F32R), both(sb, "lat_l", [DL, T], F32R)
            rope_t, qkv, tok = both(sb, "rope_t", [P, 4, T]), both(sb, "qkv", [P, 3, T]), both(sb, "tok", [P, KC, 3, H, DH])
            prod, prod2 = both(sb, "prod", [P, KC, H * H * DH]), both(sb, "prod2", [P, KC, H * DH * H])
            s_, mx, pe_ = both(sb, "s", [P, KC, H, H]), both(sb, "mx", [P, KC, H]), both(sb, "p", [P, KC, H, H])
            den, rec = both(sb, "den", [P, KC, H]), both(sb, "rec", [P, KC, H])
            o, on, ot = both(sb, "o", [P, KC, H, DH]), both(sb, "on", [P, KC, H, DH]), both(sb, "ot", [P, T])
            bA, bB, bC, bD = ([ps[4 * s + n] for s in range(S)] for n in range(4))
            tail = [Tail(self, c, "a0", s, KC, bD[s][:, 0:T], bD[s][:, T:2 * T]) for s in range(S)]

            loaded, split, low_split = sem("weights_loaded"), sem("weights_split"), sem("low_parts_ready")
            q_ps, lat_ps, k_ps, v_ps = both(sem, "q_ready"), both(sem, "latent_ready"), both(sem, "k_ready"), both(sem, "v_projected")
            lat_split, lat_half, qkv_done = both(sem, "latent_split"), both(sem, "latent_high"), both(sem, "qkv_ready")
            tok_ps, tok_kept, v_done = both(sem, "token_major_ready"), both(sem, "token_major_kept"), both(sem, "v_ready")
            shifted, exp_done, prod2_done = both(sem, "scores_shifted"), both(sem, "exp_done"), both(sem, "pv_products_ready")
            on_done, ont_ps, ont_kept = both(sem, "normalised"), both(sem, "outT_ready"), both(sem, "outT_kept")
            dchain = both(sem, "dve_chain")
            block = c.enter_context(nc.Block())
            loads = ((w_in, "a0_w"), (up_in, "a0_up"), (wout, "a0_wout"), (bout, "a0_bout"), (vec, "a0_vec"),
                     (cs, "a0_cs"), (one_row, "one_row"))

            @block.sync
            def _(sp):
                for dst, src in loads:
                    sp.dma_start(dst[:], I[src]).then_inc(loaded, 16)

            @block.gpsimd
            def _(pool):
                with pool.Fori(0, B // S) as i:
                    for s in range(S):
                        for t in range(KC):
                            pool.wait_ge(exp_done[s], i * KC + t + 1)
                            nc.gpsimd.tensor_tensor(prod2[s][:, t, :].rearrange("p (h d g) -> p h d g", h=H, d=DH),
                                                    pe_[s][:, t, :, :].unsqueeze(2).broadcast_to([P, H, DH, H]),
                                                    tok[s][:, t, 2, :, :].rearrange("p g d -> p d g").unsqueeze(1)
                                                    .broadcast_to([P, H, DH, H]), ALU.mult).then_inc(prod2_done[s], 1)
                    for s in range(S):
                        tail[s].pool(pool, i, i * S + s)

            @block.scalar
            def _(act):
                act.wait_ge(loaded, 16 * len(loads))
                act.activation(wh[:], w_in[:], ACT.Copy).then_inc(split, 1)
                act.activation(uh[:], up_in[:], ACT.Copy).then_inc(split, 1)
                with act.Fori(0, B // S) as i:
                    for s in range(S):
                        act.wait_ge(lat_ps[s], i + 1)
                        act.activation(lat_h[s][:], bB[s][0:DL, 0:T], ACT.Identity, bias=vec[0:DL, 2:3]).then_inc(lat_half[s], 1)
                    for s in range(S):
                        act.wait_ge(v_ps[s], i + 1)
                        act.activation(qkv[s][:, 2, :], bB[s][:, T:2 * T], ACT.Identity, bias=vec[:, 5:6]).then_inc(v_done[s], 1)
                    for s in range(S):
                        for t in range(KC):
                            act.wait_ge(tok_ps[s], i * KC + t + 1)
                            act.activation(tok[s][:, t, :, :, :].rearrange("p k h d -> p (k h d)"),
                                           (bA, bC)[t][s][:, 0:3 * D], ACT.Copy).then_inc(tok_kept[s], 1)
                    for s in range(S):
                        for t in range(KC):
                            act.wait_ge(shifted[s], i * KC + t + 1)
                            act.activation(pe_[s][:, t, :, :], s_[s][:, t, :, :], ACT.Exp, scale=SCALE).then_inc(exp_done[s], 1)
                    for s in range(S):
                        act.wait_ge(ont_ps[s], i + 1)
                        act.activation(ot[s][:], bB[s][:, 0:T], ACT.Copy).then_inc(ont_kept[s], 1)
                    for s in range(S):
                        tail[s].act(act, i, i * S + s)

            @block.tensor
            def _(pe):
                pe.wait_ge(split, 2)
                pe.wait_ge(low_split, 2)
                with pe.Fori(0, B // S) as i:
                    for s in range(S):
                        seq = i * S + s
                        pe.wait_ge(tail[s].done, i + 1)
                        xh, xl = self.XH[:, bass.ds(seq * T, T)], self.XL[:, bass.ds(seq * T, T)]
                        mm3(nc, bA[s][:, 0:T], wh[:, 0:D], wl[:, 0:D], xh, xl)
                        mm3(nc, bA[s][:, T:2 * T], wh[:, D:2 * D], wl[:, D:2 * D], xh, xl).then_inc(q_ps[s], 1)
                        mm3(nc, bB[s][0:DL, 0:T], wh[:, 2 * D:NW], wl[:, 2 * D:NW], xh, xl).then_inc(lat_ps[s], 1)
                    for s in range(S):
                        pe.wait_ge(lat_split[s], i + 1)
                        for r, o_ in enumerate((bC[s][:, 0:T], bC[s][:, T:2 * T], bB[s][:, T:2 * T])):
                            m = mm3(nc, o_, uh[:, r * D:(r + 1) * D], ul[:, r * D:(r + 1) * D], lat_h[s][:], lat_l[s][:])
                            if r:
                                m.then_inc((None, k_ps, v_ps)[r][s], 1)
                    for s in range(S):
                        pe.wait_ge(qkv_done[s], i + 1)
                        pe.wait_ge(v_done[s], i + 1)
                        for t in range(KC):
                            for k in range(3):
                                m = nc.tensor.transpose((bA, bC)[t][s][:, k * D:(k + 1) * D], qkv[s][:, k, t * P:(t + 1) * P],
                                                        self.idF[:])
                            m.then_inc(tok_ps[s], 1)
                    for s in range(S):
                        pe.wait_ge(on_done[s], i * KC + KC)
                        for t in range(KC):
                            m = nc.tensor.transpose(bB[s][:, t * P:(t + 1) * P],
                                                    on[s][:, t, :, :].rearrange("p h d -> p (h d)"), self.idF[:])
                        m.then_inc(ont_ps[s], 1)
                        pe.wait_ge(ont_kept[s], i + 1)
                        for t in range(KC):
                            o_ = bD[s][:, t * P:(t + 1) * P]
                            nc.tensor.matmul(o_, ot[s][:, t * P:(t + 1) * P], wout[:], start=True, stop=False)
                            m = nc.tensor.matmul(o_, one_row[:], bout[:], start=False, stop=True)
                        m.then_inc(tail[s].y_ps, 1)
                    for s in range(S):
                        tail[s].pe(pe, i)

            @block.vector
            def _(dve):
                v = nc.vector
                dve.wait_ge(split, 2)
                v.tensor_tensor(wl[:], w_in[:], wh[:].bitcast(F32), ALU.subtract).then_inc(low_split, 1)
                v.tensor_tensor(ul[:], up_in[:], uh[:].bitcast(F32), ALU.subtract).then_inc(low_split, 1)
                for s in range(S):
                    dve.sem_inc(tail[s].done, 1)
                with dve.Fori(0, B // S) as i:
                    links = [Chain(dve, dchain[s], i, PER_DVE) for s in range(S)]
                    cos, sin = cs[:, 0:T], cs[:, T:2 * T]

                    def low(s):
                        dve.wait_ge(lat_half[s], i + 1)
                        v.scalar_tensor_tensor(lat_l[s][:], bB[s][0:DL, 0:T], vec[0:DL, 2:3], lat_h[s][:].bitcast(F32),
                                               ALU.add, ALU.subtract).then_inc(lat_split[s], 1)

                    for s in range(S):
                        low(s)
                    for s in range(S):
                        dve.wait_ge(q_ps[s], i + 1)
                        v.scalar_tensor_tensor(rope_t[s][:, 0, :], bA[s][:, 0:T], vec[:, 0:1], cos, ALU.add, ALU.mult)
                        links[s](v.scalar_tensor_tensor(rope_t[s][:, 1, :], bA[s][:, T:2 * T], vec[:, 1:2], sin, ALU.add, ALU.mult))
                        v.tensor_tensor(qkv[s][:, 0, :], rope_t[s][:, 0, :], rope_t[s][:, 1, :], ALU.add)
                    for s in range(S):
                        dve.wait_ge(k_ps[s], i + 1)
                        v.scalar_tensor_tensor(rope_t[s][:, 2, :], bC[s][:, 0:T], vec[:, 3:4], cos, ALU.add, ALU.mult)
                        links[s](v.scalar_tensor_tensor(rope_t[s][:, 3, :], bC[s][:, T:2 * T], vec[:, 4:5], sin, ALU.add, ALU.mult))
                        v.tensor_tensor(qkv[s][:, 1, :], rope_t[s][:, 2, :], rope_t[s][:, 3, :], ALU.add).then_inc(qkv_done[s], 1)
                    for s in range(S):
                        for t in range(KC):
                            dve.wait_ge(tok_kept[s], i * KC + t + 1)
                            hgd = prod[s][:, t, :].rearrange("p (h g d) -> p h g d", h=H, g=H)
                            links[s](v.tensor_tensor(hgd, tok[s][:, t, 0, :, :].unsqueeze(2).broadcast_to([P, H, H, DH]),
                                                     tok[s][:, t, 1, :, :].unsqueeze(1).broadcast_to([P, H, H, DH]), ALU.mult))
                            links[s](v.tensor_reduce(s_[s][:, t, :, :], hgd, AX.X, ALU.add))
                            links[s](v.tensor_reduce(mx[s][:, t, :], s_[s][:, t, :, :], AX.X, ALU.max))
                            v.tensor_tensor(s_[s][:, t, :, :], s_[s][:, t, :, :],
                                            mx[s][:, t, :].unsqueeze(2).broadcast_to([P, H, H]), ALU.subtract).then_inc(shifted[s], 1)
                    for s in range(S):
                        for t in range(KC):
                            dve.wait_ge(exp_done[s], i * KC + t + 1)
                            links[s](v.tensor_reduce(den[s][:, t, :], pe_[s][:, t, :, :], AX.X, ALU.add))
                            links[s](v.reciprocal(rec[s][:, t, :], den[s][:, t, :]))
                            dve.wait_ge(prod2_done[s], i * KC + t + 1)
                            links[s](v.tensor_reduce(o[s][:, t, :, :],
                                                     prod2[s][:, t, :].rearrange("p (h d g) -> p h d g", h=H, d=DH), AX.X, ALU.add))
                            v.tensor_tensor(on[s][:, t, :, :], o[s][:, t, :, :],
                                            rec[s][:, t, :].unsqueeze(2).broadcast_to([P, H, DH]), ALU.mult).then_inc(on_done[s], 1)
                    for s in range(S):
                        tail[s].dve_stats(dve, links[s], i, i * S + s)
                    for s in range(S):
                        tail[s].dve_norm(dve, i)
                    for s in range(S):
                        tail[s].dve_low(dve, i, i * S + s)
                        links[s].close()

    def mixture(self, tag, router, act_fn, n_shared, ht, rms=False, biases=False):
        nc, I, ps = self.nc, self.ins, self.ps
        NR = 8
        NE = n_shared + NR
        H = ht * P
        NB = 512
        NBLK = NTOK // NB
        TB = NB // P
        R = 32 if router == "mlp" else P
        HP, HR = 3, 4
        LAG = 2
        scaled = rms
        GR = 1 if rms else 2
        AHEAD = 4
        gates_dram = nc.dram_tensor(tag + "_gates", (2, NE, NTOK), F32).ap()
        with ExitStack() as c:
            def sb(name, shape, dt=F32):
                return c.enter_context(nc.sbuf_tensor(f"{tag}_{name}", shape, dt))

            def sem(name):
                return self.semaphore(f"{tag}_{name}")

            acc = sb("acc", [P, NTOK])
            if rms:
                RH, RL = sb("RH", [P, NTOK], F32R), sb("RL", [P, NTOK], F32R)
            else:
                RH, RL = self.XH, self.XL
            wr_in = sb("wr_in", [P, R])
            wrh, wrl = sb("wrh", [P, R], F32R), sb("wrl", [P, R], F32R)
            wg2, bg1 = sb("wg2", [32, P]), sb("bg1", [32, 1])
            rank = sb("rank", [P, NR])
            hid_r, lt = sb("hid_r", [32, NB]), sb("lt", [P, NB])
            V = sb("V", [P, NTILE, NR])
            ta, tb_, s1, s2 = (sb(n, [P, NTILE, NR]) for n in ("ta", "tb", "s1", "s2"))
            m1, m2 = sb("m1", [P, NTILE]), sb("m2", [P, NTILE])
            G = sb("G", [P, NTILE, NE])
            gt = sb("gt", [NE, NB])
            gth, gtl = sb("gth", [NE, 2, NB], F32R), sb("gtl", [NE, 2, NB], F32R)
            b2, b1 = sb("b2", [NE, P]), sb("b1", [P, NE * ht])
            b1e, b1_kept = sb("b1e", [P, 2, ht]), sem("biases_kept")
            gs = sb("gs", [P, NE])
            ones_in, ones2 = sb("ones_in", [2, P]), sb("ones2", [2, P], F32R)
            w1_in, w2_in = sb("w1_in", [P, H]), sb("w2_in", [P, H])
            w1h, w1l, w2h, w2l = (sb(n, [P, 2, H], F32R) for n in ("w1h", "w1l", "w2h", "w2l"))
            grow = sb("grow", [2, GR * NTOK], F32R)
            gsb, tmp = sb("gsb", [P, 2, NB]), sb("tmp", [P, 2, NB])
            hf = sb("hf", [P, 3, NB])
            hh, hl = sb("hh", [P, HR, NB], F32R), sb("hl", [P, HR, NB], F32R)
            gpad = sb("gpad", [P, 1])
            SC = 2
            yt = [hf[:, s, :] for s in range(SC)]
            st2, mv2, ve2, rs2 = ([sb(f"{n}{s}", sh) for s in range(SC)] for n, sh in
                                  (("stc", [P, TB, 6]), ("mvc", [P, TB, 2]), ("vec_", [P, TB]), ("rsc", [P, TB])))
            xn2 = [tmp[:, s, :].rearrange("p (t d) -> p t d", t=TB) for s in range(SC)]
            st, mv, ve, rs = sb("st", [P, TB, 6]), sb("mv", [P, TB, 2]), sb("ve", [P, TB]), sb("rs", [P, TB])
            xn = sb("xn", [P, TB, D])
            sq, ss = sb("sq", [P, TB, D]), sb("ss", [P, TB])

            loaded, split_h, split_l, idle = sem("weights_loaded"), sem("router_high"), sem("router_low"), sem("ready")
            hid_ps, hid_kept, lt_ps, lt_kept = sem("router_hidden"), sem("router_hidden_kept"), sem("logitsT"), sem("logitsT_kept")
            v_ps, v_kept = sem("logits_ready"), sem("logits_kept")
            acc_done, acc_half = sem("acc_done"), sem("acc_started")
            ss_done, sse, rrs, rn_done, rnt_ps, rh_kept, rl_kept = (sem("squares"), sem("squares_eps"), sem("rms_rstd"),
                sem("rms_ready"), sem("rmsT_ready"), sem("rms_high"), sem("rms_low"))
            once, act_once, g_done, gt_ps, gt_kept, gth_done, gtl_done = (sem("dve_once"), sem("act_once"), sem("gates_ready"),
                sem("gatesT_ready"), sem("gatesT_kept"), sem("gates_high"), sem("gates_low"))
            bias_ps, bias_added, g_stored = sem("gate_bias_ready"), sem("gate_bias_added"), sem("gates_stored")
            w_in, grow_in, w_high, w_low = sem("expert_loaded"), sem("gate_rows_loaded"), sem("expert_high"), sem("expert_low")
            gbc_ps, gbc_kept = sem("gate_broadcast"), sem("gate_kept")
            h_ps, h_act, h_high, h_split, o_step, o_ps, o_read = (sem("hidden_ready"), sem("hidden_activated"), sem("hidden_high"),
                sem("hidden_split"), sem("out_step"), sem("out_ready"), sem("out_gated"))
            yt_kept, y_ps, ve_done, rs_done, xn_done, xnt_ps, xh_kept, xl_kept, x_kept, dchain2 = (
                [sem(f"{n}{s}") for s in range(SC)] for n in ("sumT_kept", "sum_ready", "var_ready", "rstd_ready", "xn_ready",
                                                             "xnT_ready", "xh_kept", "xl_kept", "x_kept", "dve_chain"))
            block = c.enter_context(nc.Block())
            loads = [(wr_in, "wr"), (rank, "rank"), (ones_in, "ones")]
            if router == "mlp":
                loads += [(wg2, "wg2"), (bg1, "bg1")]
            if biases:
                loads += [(b1, "b1"), (b2, "b2"), (gs, "gs")]
            NLOAD = len(loads)

            @block.sync
            def _(sp):
                for dst, src in loads:
                    sp.dma_start(dst[:], I[f"{tag}_{src}"]).then_inc(loaded, 16)
                sp.dma_start(w1_in[:], I[f"{tag}_w1"][0:P, :]).then_inc(w_in, 16)
                sp.dma_start(w2_in[:], I[f"{tag}_w2"][0:P, :]).then_inc(w_in, 16)
                for b in range(NBLK):
                    sp.wait_ge(gth_done, b + 1)
                    sp.wait_ge(gtl_done, b + 1)
                    sp.dma_start(gates_dram[0, :, b * NB:(b + 1) * NB], gth[:, b % 2, :].bitcast(F32)).then_inc(g_stored, 16)
                    sp.dma_start(gates_dram[1, :, b * NB:(b + 1) * NB], gtl[:, b % 2, :].bitcast(F32)).then_inc(g_stored, 16)
                    sp.wait_ge(g_stored, 32 * (b + 1))
                sp.dma_start(grow[:, 0:NTOK].bitcast(F32), gates_dram[:, 0, :]).then_inc(grow_in, 16)
                with sp.Fori(1, NE) as e:
                    sp.wait_ge(w_high, e * 2)
                    sp.wait_ge(w_low, e * 2)
                    sp.dma_start(w1_in[:], I[f"{tag}_w1"][bass.ds(e * P, P), :]).then_inc(w_in, 16)
                    sp.dma_start(w2_in[:], I[f"{tag}_w2"][bass.ds(e * P, P), :]).then_inc(w_in, 16)
                    sp.wait_ge(grow_in, e * 16)
                    sp.wait_ge(gbc_ps, e * NBLK - (GR - 1) * NBLK + 1)
                    sp.dma_start(grow[:, bass.ds((e % GR) * NTOK, NTOK)].bitcast(F32),
                                 gates_dram[:, bass.ds(e, 1), :].rearrange("a b n -> a (b n)")).then_inc(grow_in, 16)
                if NE % 2 == 0:
                    sp.wait_ge(w_high, NE * 2)
                    sp.wait_ge(w_low, NE * 2)
                    sp.dma_start(w1_in[:], I[f"{tag}_w1"][0:P, :]).then_inc(w_in, 16)
                    sp.dma_start(w2_in[:], I[f"{tag}_w2"][0:P, :]).then_inc(w_in, 16)
                    sp.wait_ge(w_in, NE * 32 + 32)

            @block.gpsimd
            def _(pool):
                g = nc.gpsimd
                with pool.Fori(0, NBLK) as b:
                    blk = bass.ds(b * NB, NB)
                    if rms:
                        g.tensor_tensor(acc[:, blk], self.XH[:, blk].bitcast(F32), self.XL[:, blk].bitcast(F32),
                                        ALU.add).then_inc(acc_half, 1)
                        pool.wait_ge(acc_half, b + 1)
                        g.tensor_tensor(gpad[:], self.mhalf[:, 0:1], self.mhalf[:, 0:1], ALU.mult)
                        g.tensor_tensor(acc[:, blk], acc[:, blk], acc[:, blk], ALU.add).then_inc(acc_done, 1)
                        pool.wait_ge(sse, b + 1)
                        g.tensor_tensor(rs[:], ve[:], self.mhalf[:, 0:TB], ALU.pow).then_inc(rrs, 1)
                    else:
                        g.tensor_tensor(acc[:, blk], self.XH[:, blk].bitcast(F32), self.XL[:, blk].bitcast(F32),
                                        ALU.add).then_inc(acc_done, 1)
                if biases:
                    pool.wait_ge(bias_added, NBLK)
                with pool.Fori(0, NE) as e:
                    for b in range(NBLK):
                        n = e * NBLK + b
                        pool.wait_ge(o_read, n + 1)
                        pool.wait_ge(acc_done, n + 1)
                        g.tensor_tensor(acc[:, b * NB:(b + 1) * NB], acc[:, b * NB:(b + 1) * NB], tmp[:, b % 2, :],
                                        ALU.add).then_inc(acc_done, 1)
                with pool.Fori(0, NBLK // SC) as i:
                    for s in range(SC):
                        pool.wait_ge(ve_done[s], i + 1)
                        g.tensor_tensor(rs2[s][:], ve2[s][:], self.mhalf[:, 0:TB], ALU.pow).then_inc(rs_done[s], 1)
                    for s in range(SC):
                        pool.wait_ge(xn_done[s], i + 1)
                        g.tensor_copy(self.X[:, bass.ds((i * SC + s) * TB, TB), :], xn2[s]).then_inc(x_kept[s], 1)

            @block.scalar
            def _(act):
                a = nc.scalar
                act.wait_ge(loaded, 16 * NLOAD)
                a.activation(wrh[:], wr_in[:], ACT.Copy).then_inc(split_h, 1)
                a.activation(ones2[:], ones_in[:], ACT.Copy).then_inc(split_h, 1)
                with act.Fori(0, NBLK) as b:
                    if rms:
                        act.wait_ge(idle, b + 1)
                        for t in range(TB):
                            a.activation(sq[:, t, :], self.X[:, bass.ds(b * TB + t, 1), :].rearrange("p a d -> p (a d)"),
                                             ACT.Square, accum_out=ss[:, t:t + 1]).then_inc(ss_done, 1)
                    if router == "mlp":
                        act.wait_ge(hid_ps, b + 1)
                        a.activation(hid_r[:], ps[0][0:32, :], ACT.Gelu, bias=bg1[:, 0:1]).then_inc(hid_kept, 1)
                    act.wait_ge(lt_ps, b + 1)
                    a.activation(lt[:], ps[1][:], ACT.Copy).then_inc(lt_kept, 1)
                    if rms:
                        act.wait_ge(rnt_ps, b + 1)
                        a.activation(RH[:, bass.ds(b * NB, NB)], ps[3][:], ACT.Copy).then_inc(rh_kept, 1)
                if router == "sigmoid":
                    act.wait_ge(v_kept, NBLK)
                    a.activation(V[:], V[:], ACT.Sigmoid).then_inc(act_once, 1)
                else:
                    act.wait_ge(once, {"mlp": 2, "logits": 8}[router])
                    a.activation(ta[:], ta[:], ACT.Exp).then_inc(act_once, 1)
                for b in range(NBLK):
                    act.wait_ge(gt_ps, b + 1)
                    if b:
                        act.wait_ge(gtl_done, b)
                        if biases:
                            act.wait_ge(bias_ps, b)
                    a.activation(gt[:], ps[4 + b % 2][0:NE, :], ACT.Copy).then_inc(gt_kept, 1)
                    act.wait_ge(gt_kept, b + 1)
                    if b >= 2:
                        act.wait_ge(g_stored, 32 * (b - 1))
                    a.activation(gth[:, b % 2, :], gt[:], ACT.Copy).then_inc(gth_done, 1)

                def split(e, w):
                    act.wait_ge(w_in, e * 32 + 32)
                    a.activation(w2h[:, w, :], w2_in[:], ACT.Copy).then_inc(w_high, 1)
                    if scaled:
                        a.activation(w1h[:, w, :], w1_in[:], ACT.Copy, scale=gs[:, bass.ds(e % NE, 1)]).then_inc(w_high, 1)
                    else:
                        a.activation(w1h[:, w, :], w1_in[:], ACT.Copy).then_inc(w_high, 1)
                    if biases:
                        a.activation(b1e[:, w, :], b1[:, bass.ds((e % NE) * ht, ht)], ACT.Copy).then_inc(b1_kept, 1)

                def turn(e0, nu):
                    for b in range(nu * NBLK):
                        n = e0 * NBLK + b
                        u = b // NBLK
                        if biases and b % NBLK == 0:
                            act.wait_ge(b1_kept, e0 + u + 1)
                        for j in range(ht):
                            q = n * ht + j
                            k = b * ht + j
                            act.wait_ge(h_ps, q + 1)
                            if k >= 3:
                                act.wait_ge(h_split, q - 2)
                            a.activation(hf[:, k % 3, :], ps[k % HP][:], act_fn,
                                         bias=b1e[:, u % 2, j:j + 1] if biases else 0.0).then_inc(h_act, 1)
                        act.wait_ge(gbc_ps, n + 2)
                        if b >= 2:
                            act.wait_ge(o_read, n - 1)
                        a.activation(gsb[:, b % 2, :], ps[5 + b % 2][:], ACT.Copy).then_inc(gbc_kept, 1)
                        if b % NBLK == AHEAD and nu > 1:
                            act.wait_ge(o_read, (e0 + u) * NBLK + 1)
                            split(e0 + u + 1, (u + 1) % 2)

                split(0, 0)
                with act.Fori(0, NE // 2) as i:
                    turn(i * 2, 2)
                if NE % 2:
                    turn(NE - 1, 1)
                act.wait_ge(acc_done, NBLK * NE + NBLK)
                with act.Fori(0, NBLK // SC) as i:
                    for s in range(SC):
                        act.wait_ge(xl_kept[s], i + 1)
                        a.activation(yt[s], acc[:, bass.ds((i * SC + s) * NB, NB)], ACT.Copy).then_inc(yt_kept[s], 1)
                    for s in range(SC):
                        act.wait_ge(xnt_ps[s], i + 1)
                        a.activation(self.XH[:, bass.ds((i * SC + s) * NB, NB)], ps[2 + s][:], ACT.Copy).then_inc(xh_kept[s], 1)

            @block.tensor
            def _(pe):
                pe.wait_ge(split_h, 2)
                pe.wait_ge(split_l, 1)
                with pe.Fori(0, NBLK) as b:
                    pe.wait_ge(idle, b + 1)
                    xh, xl = self.XH[:, bass.ds(b * NB, NB)], self.XL[:, bass.ds(b * NB, NB)]
                    if router == "mlp":
                        mm3(nc, ps[0][0:32, :], wrh[:], wrl[:], xh, xl).then_inc(hid_ps, 1)
                        pe.wait_ge(hid_kept, b + 1)
                        nc.tensor.matmul(ps[1][:], wg2[:], hid_r[:], start=True, stop=True).then_inc(lt_ps, 1)
                    else:
                        mm3(nc, ps[1][:], wrh[:], wrl[:], xh, xl).then_inc(lt_ps, 1)
                    pe.wait_ge(lt_kept, b + 1)
                    for t in range(TB):
                        m = nc.tensor.transpose(ps[2][:, t * P:(t + 1) * P], lt[:, t * P:(t + 1) * P], self.idF[:])
                    m.then_inc(v_ps, 1)
                    if rms:
                        pe.wait_ge(rn_done, b + 1)
                        for t in range(TB):
                            m = nc.tensor.transpose(ps[3][:, t * P:(t + 1) * P], xn[:, t, :], self.idF[:])
                        m.then_inc(rnt_ps, 1)
                pe.wait_ge(g_done, 1)
                for b in range(NBLK):
                    if b >= 2:
                        pe.wait_ge(gt_kept, b - 1)
                    for t in range(TB):
                        m = nc.tensor.transpose(ps[4 + b % 2][0:NE, t * P:(t + 1) * P], G[:, b * TB + t, :], self.idF[:])
                    m.then_inc(gt_ps, 1)
                    if biases:
                        pe.wait_ge(gt_kept, b + 1)
                        if b:
                            pe.wait_ge(bias_added, b)
                        nc.tensor.matmul(ps[6][:], b2[:], gt[:], start=True, stop=True).then_inc(bias_ps, 1)
                pe.wait_ge(gt_kept, NBLK)
                if biases:
                    pe.wait_ge(bias_added, NBLK)
                pe.sem_inc(gbc_ps, 1)
                pe.sem_inc(o_ps, 1)

                def turn(e0, nu):
                    pe.wait_ge(acc_done, e0 * NBLK + NBLK)

                    def gate(b):
                        if b % NBLK == 0:
                            pe.wait_ge(grow_in, (e0 + b // NBLK) * 16 + 16)
                        if b >= 2:
                            pe.wait_ge(gbc_kept, e0 * NBLK + b - 1)
                        row = ((e0 + b // NBLK) % GR) * NTOK + (b % NBLK) * NB
                        nc.tensor.matmul(ps[5 + b % 2][:], ones2[:], grow[:, bass.ds(row, NB)], start=True,
                                         stop=True).then_inc(gbc_ps, 1)

                    def hidden(k):
                        b, j = divmod(k, ht)
                        u, w = b // NBLK, b // NBLK % 2
                        if k % (NBLK * ht) == 0:
                            pe.wait_ge(w_high, (e0 + u) * 2 + 2)
                            pe.wait_ge(w_low, (e0 + u) * 2 + 2)
                        if k >= HP:
                            pe.wait_ge(h_act, (e0 * NBLK) * ht + k - HP + 1)
                        s = slice(j * P, (j + 1) * P)
                        blk = slice(b % NBLK * NB, (b % NBLK + 1) * NB)
                        mm3(nc, ps[k % HP][:], w1h[:, w, s], w1l[:, w, s], RH[:, blk], RL[:, blk]).then_inc(h_ps, 1)

                    def outward(k):
                        b, j = divmod(k, ht)
                        w = b // NBLK % 2
                        pe.wait_ge(h_split, (e0 * NBLK) * ht + k + 1)
                        if j == 0 and b >= 2:
                            pe.wait_ge(o_read, e0 * NBLK + b - 1)
                        s = slice(j * P, (j + 1) * P)
                        m = mm3(nc, ps[3 + b % 2][:], w2h[:, w, s], w2l[:, w, s], hh[:, k % HR, :], hl[:, k % HR, :],
                                start=(j == 0), stop=(j == ht - 1))
                        m.then_inc(o_ps if j == ht - 1 else o_step, 1)

                    for k in range(nu * NBLK * ht + LAG):
                        if k < nu * NBLK * ht:
                            if k % ht == 0:
                                gate(k // ht)
                            hidden(k)
                        if k >= LAG:
                            outward(k - LAG)

                with pe.Fori(0, NE // 2) as i:
                    turn(i * 2, 2)
                if NE % 2:
                    turn(NE - 1, 1)
                pe.wait_ge(o_read, NE * NBLK)
                with pe.Fori(0, NBLK // SC) as i:
                    for s in range(SC):
                        pe.wait_ge(yt_kept[s], i + 1)
                        for t in range(TB):
                            m = nc.tensor.transpose(ps[s][:, t * P:(t + 1) * P], yt[s][:, t * P:(t + 1) * P], self.idF[:])
                        m.then_inc(y_ps[s], 1)
                    for s in range(SC):
                        pe.wait_ge(xn_done[s], i + 1)
                        for t in range(TB):
                            m = nc.tensor.transpose(ps[2 + s][:, t * P:(t + 1) * P], xn2[s][:, t, :], self.idF[:])
                        m.then_inc(xnt_ps[s], 1)

            @block.vector
            def _(dve):
                v = nc.vector
                dve.wait_ge(split_h, 1)
                v.tensor_tensor(wrl[:], wr_in[:], wrh[:].bitcast(F32), ALU.subtract).then_inc(split_l, 1)
                dve.sem_inc(idle, 1)
                with dve.Fori(0, NBLK) as b:
                    if rms:
                        dve.wait_ge(ss_done, b * TB + TB)
                        v.tensor_scalar(ve[:], ss[:], 1.0 / D, 1.1920929e-07, ALU.mult, ALU.add).then_inc(sse, 1)
                        dve.wait_ge(rrs, b + 1)
                        for t in range(TB):
                            m = v.tensor_scalar(xn[:, t, :], self.X[:, bass.ds(b * TB + t, 1), :].rearrange("p a d -> p (a d)"),
                                                rs[:, t:t + 1], None, ALU.mult)
                        m.then_inc(rn_done, 1)
                    dve.wait_ge(v_ps, b + 1)
                    v.tensor_copy(V[:, bass.ds(b * TB, TB), :], ps[2][:].rearrange("p (t r) -> p t r", t=TB)[:, :, 0:NR]).then_inc(v_kept if rms else idle, 1)
                    if rms:
                        dve.wait_ge(rh_kept, b + 1)
                        v.tensor_tensor(RL[:, bass.ds(b * NB, NB)], ps[3][:], RH[:, bass.ds(b * NB, NB)].bitcast(F32),
                                        ALU.subtract).then_inc(idle, 1)
                dve.wait_ge(*((v_kept, NBLK) if rms else (idle, NBLK + 1)))
                cnt = [0]

                def step(ins):
                    cnt[0] += 1
                    ins.then_inc(once, 1)
                    dve.wait_ge(once, cnt[0])

                def wide(m):
                    return m[:].unsqueeze(2).broadcast_to([P, NTILE, NR])

                if router == "mlp":
                    step(v.tensor_reduce(m1[:], V[:], AX.X, ALU.max))
                    step(v.tensor_tensor(ta[:], V[:], wide(m1), ALU.subtract))
                    dve.wait_ge(act_once, 1)
                    step(v.tensor_reduce(m1[:], ta[:], AX.X, ALU.add))
                    step(v.reciprocal(m2[:], m1[:]))
                    step(v.tensor_tensor(V[:], ta[:], wide(m2), ALU.mult))
                if router == "sigmoid":
                    dve.wait_ge(act_once, 1)

                def choose(vals, out):
                    step(v.tensor_reduce(m1[:], vals[:], AX.X, ALU.max))
                    step(v.tensor_tensor(tb_[:], vals[:], wide(m1), ALU.is_equal))
                    step(v.tensor_tensor(tb_[:], tb_[:], rank[:].unsqueeze(1).broadcast_to([P, NTILE, NR]), ALU.mult))
                    step(v.tensor_reduce(m2[:], tb_[:], AX.X, ALU.max))
                    step(v.tensor_tensor(out[:], tb_[:], wide(m2), ALU.is_equal))

                choose(V, s1)
                if router == "logits":
                    step(v.tensor_tensor(ta[:], V[:], wide(m1), ALU.subtract))
                    step(v.tensor_copy(m2[:], m1[:]))
                    step(v.tensor_copy(m2[:], m1[:]))
                    dve.wait_ge(act_once, 1)
                    step(v.tensor_copy(G[:, :, n_shared:], ta[:]))
                step(v.scalar_tensor_tensor(ta[:].rearrange("p t r -> p (t r)"), s1[:].rearrange("p t r -> p (t r)"), -3e38,
                                            V[:].rearrange("p t r -> p (t r)"), ALU.mult, ALU.add))
                choose(ta, s2)
                step(v.tensor_tensor(s1[:], s1[:], s2[:], ALU.add))
                if router == "mlp":
                    step(v.tensor_tensor(G[:, :, n_shared:], V[:], s1[:], ALU.mult))
                elif router == "sigmoid":
                    step(v.tensor_reduce(m1[:], V[:], AX.X, ALU.add))
                    step(v.reciprocal(m2[:], m1[:]))
                    step(v.tensor_tensor(s1[:], V[:], s1[:], ALU.mult))
                    step(v.tensor_tensor(G[:, :, n_shared:], s1[:], wide(m2), ALU.mult))
                else:
                    step(v.tensor_tensor(ta[:], G[:, :, n_shared:], s1[:], ALU.mult))
                    step(v.tensor_reduce(m1[:], ta[:], AX.X, ALU.add))
                    step(v.reciprocal(m2[:], m1[:]))
                    step(v.tensor_tensor(G[:, :, n_shared:], ta[:], wide(m2), ALU.mult))
                if n_shared:
                    step(v.memset(G[:, :, 0:n_shared], 1.0))
                v.memset(self.pad[:], 0.0).then_inc(g_done, 1)
                for b in range(NBLK):
                    s = slice(b * NB, (b + 1) * NB)
                    dve.wait_ge(gth_done, b + 1)
                    if b >= 2:
                        dve.wait_ge(g_stored, 32 * (b - 1))
                    v.tensor_tensor(gtl[:, b % 2, :], gt[:], gth[:, b % 2, :].bitcast(F32), ALU.subtract).then_inc(gtl_done, 1)
                    if biases:
                        dve.wait_ge(bias_ps, b + 1)
                        dve.wait_ge(acc_done, NBLK)
                        v.tensor_tensor(acc[:, s], ps[6][:], acc[:, s], ALU.add).then_inc(bias_added, 1)

                def split(e, w):
                    dve.wait_ge(w_high, e * 2 + 1)
                    v.tensor_tensor(w2l[:, w, :], w2_in[:], w2h[:, w, :].bitcast(F32), ALU.subtract).then_inc(w_low, 1)
                    dve.wait_ge(w_high, e * 2 + 2)
                    if scaled:
                        v.scalar_tensor_tensor(w1l[:, w, :], w1_in[:], gs[:, bass.ds(e % NE, 1)], w1h[:, w, :].bitcast(F32),
                                               ALU.mult, ALU.subtract).then_inc(w_low, 1)
                    else:
                        v.tensor_tensor(w1l[:, w, :], w1_in[:], w1h[:, w, :].bitcast(F32), ALU.subtract).then_inc(w_low, 1)

                def turn(e0, nu):
                    def gated(b):
                        n = e0 * NBLK + b
                        dve.wait_ge(gbc_kept, n + 1)
                        dve.wait_ge(o_ps, n + 2)
                        dve.wait_ge(acc_done, n + NBLK - 1)
                        v.tensor_tensor(tmp[:, b % 2, :], ps[3 + b % 2][:], gsb[:, b % 2, :], ALU.mult).then_inc(o_read, 1)

                    for k in range(nu * NBLK * ht):
                        q = e0 * (NBLK * ht) + k
                        dve.wait_ge(h_act, q + 1)
                        if k >= HR:
                            fb, fj = divmod(k - HR, ht)
                            if fj == ht - 1:
                                dve.wait_ge(o_ps, e0 * NBLK + fb + 2)
                            else:
                                dve.wait_ge(o_step, e0 * (NBLK * (ht - 1)) + fb * (ht - 1) + fj + 1)
                        v.tensor_copy(hh[:, k % HR, :], hf[:, k % 3, :]).then_inc(h_high, 1)
                        dve.wait_ge(h_high, q + 1)
                        v.tensor_tensor(hl[:, k % HR, :], hf[:, k % 3, :], hh[:, k % HR, :].bitcast(F32),
                                        ALU.subtract).then_inc(h_split, 1)
                        if k >= LAG and (k - LAG) % ht == ht - 1:
                            gated((k - LAG) // ht)
                        if k % (NBLK * ht) == (AHEAD + 1) * ht and nu > 1:
                            split(e0 + k // (NBLK * ht) + 1, (k // (NBLK * ht) + 1) % 2)
                    gated(nu * NBLK - 1)

                split(0, 0)
                with dve.Fori(0, NE // 2) as i:
                    turn(i * 2, 2)
                if NE % 2:
                    turn(NE - 1, 1)
                for s in range(SC):
                    dve.sem_inc(xl_kept[s], 1)
                with dve.Fori(0, NBLK // SC) as i:
                    links = [Chain(dve, dchain2[s], i, 2) for s in range(SC)]
                    for s in range(SC):
                        dve.wait_ge(y_ps[s], i + 1)
                        y = ps[s][:].rearrange("p (t d) -> p t d", t=TB)
                        self.norm_stats(links[s], y, st2[s], mv2[s], ve2[s][:], TB, LN_EPS).then_inc(ve_done[s], 1)
                        links[s].close()
                    for s in range(SC):
                        y = ps[s][:].rearrange("p (t d) -> p t d", t=TB)
                        dve.wait_ge(rs_done[s], i + 1)
                        for t in range(TB):
                            m = v.tensor_scalar(xn2[s][:, t, :], y[:, t, :], mv2[s][:, t, 0:1], rs2[s][:, t:t + 1],
                                                ALU.subtract, ALU.mult)
                        m.then_inc(xn_done[s], 1)
                    for s in range(SC):
                        blk = bass.ds((i * SC + s) * NB, NB)
                        dve.wait_ge(xh_kept[s], i + 1)
                        dve.wait_ge(x_kept[s], i + 1)
                        v.tensor_tensor(self.XL[:, blk], ps[2 + s][:], self.XH[:, blk].bitcast(F32),
                                        ALU.subtract).then_inc(xl_kept[s], 1)


    def latent_attention(self):
        nc, I, ps = self.nc, self.ins, self.ps
        H, DH, KC = 16, 64, T // P
        SCALE = 1.0 / float(DH) ** 0.5
        NC_ = H * DH // P
        HPC = P // DH
        WU = H * DH
        NU = 5
        with ExitStack() as c_:
            def sb(name, shape, dt=F32):
                return c_.enter_context(nc.sbuf_tensor("a1_" + name, shape, dt))

            def sem(name):
                return self.semaphore("a1_" + name)

            wd_in, up_in = sb("wd_in", [P, P]), sb("up_in", [P, WU])
            wdh, wdl = sb("wdh", [P, P], F32R), sb("wdl", [P, P], F32R)
            uh, ul = sb("uh", [P, NU, WU], F32R), sb("ul", [P, NU, WU], F32R)
            wout, ln, cs = sb("wout", [P, NC_, D]), sb("ln", [P, 2]), sb("cs", [P, 2 * T])
            sel = sb("sel", [P, H * P], BF16)
            st, mv, ve, rs, xn = sb("st_", [P, KC, 6]), sb("mv_", [P, KC, 2]), sb("ve_", [P, KC]), sb("rs_", [P, KC]), sb("xn_", [P, KC, D])
            hf, hh, hl = sb("hf", [P, T]), sb("hh", [P, T], F32R), sb("hl", [P, T], F32R)
            ch, cl = sb("ch", [P, T], F32R), sb("cl", [P, T], F32R)
            rt = sb("rt", [P, 4, 2 * T])
            q, qb = sb("q", [P, NC_, T]), sb("qb", [P, NC_, T], BF16)
            kt = sb("kt", [P, 2, T])
            kz, kb = sb("kz", [P, NC_, HPC, T]), sb("kb", [P, NC_, HPC, T], BF16)
            va = sb("va", [P, KC, H, P])
            negm, nmt = sb("negm", [P, KC, P]), sb("nmt", [P, T], BF16)
            pt = sb("pt", [P, 3, 2 * T])
            den, rec, ot = sb("den", [P, 2, T]), sb("rec", [P, 2, T]), sb("ot", [P, NC_, T])
            bM, bV, bNM, bPRE, bST, bPV = (4, 5), (4, 5), 6, 7, (0, 1, 2, 3), (4, 5)
            tail = Tail(self, c_, "a1", 0, KC, ps[6][:, 0:T], ps[7][:, 0:T], gain=2.0)

            loaded, w_high, w_low, up_loaded, zeros = sem("weights_loaded"), sem("weights_high"), sem("weights_low"), sem("up_loaded"), sem("constants_set")
            ve_done, rs_done, xn_done, hnt_ps, hf_done, hh_done, hl_done = (sem("pre_var"), sem("pre_rstd"), sem("pre_xn"),
                sem("normedT_ready"), sem("normed_scaled"), sem("normed_high"), sem("normed_low"))
            c_ps, ch_done, cl_done = sem("latents_ready"), sem("latents_high"), sem("latents_low")
            qk_ps, rt_done, add_done, qkb_done = sem("qk_ready"), sem("rope_products"), sem("rope_done"), sem("bf16_qk_ready")
            v_ps, v_kept = sem("v_ready"), sem("v_kept")
            s_ps, max_done, nm_ps, nm_kept = sem("scores_ready"), sem("max_done"), sem("maxT_ready"), sem("maxT_kept")
            st_ps, exp_done, pv_done, on_done = sem("scoresT_ready"), sem("exp_done"), sem("pv_done"), sem("normalised")
            den_kept, rec_done, chain, tchain, ochain = (sem("sums_kept"), sem("sums_inverted"), sem("dve_chain"), sem("dve_tail_chain"),
                                                       sem("dve_once"))
            block = c_.enter_context(nc.Block())
            loads = ((wd_in, "a1_wd"), (wout, "a1_wout"), (ln, "a1_ln"), (cs, "a1_cs"))

            @block.sync
            def _(sp):
                for dst, src in loads:
                    sp.dma_start(dst[:], I[src]).then_inc(loaded, 16)
                for n in range(NU + 2):
                    if n:
                        sp.wait_ge(w_high, 1 + n)
                        sp.wait_ge(w_low, 1 + min(n, NU))
                    src = I["a1_up"][:, n * WU:(n + 1) * WU] if n < NU else I["a1_sel"][:, (n - NU) * WU:(n - NU + 1) * WU]
                    sp.dma_start(up_in[:], src).then_inc(up_loaded, 16)

            @block.gpsimd
            def _(pool):
                g = nc.gpsimd

                def pre(i):
                    pool.wait_ge(ve_done, i + 1)
                    g.tensor_tensor(rs[:], ve[:], self.mhalf[:, 0:KC], ALU.pow).then_inc(rs_done, 1)

                def turn(i, prev):
                    for j in range(NC_):
                        for r in range(2):
                            m = 2 * j + r
                            pool.wait_ge(rt_done, i * 2 * NC_ + m + 1)
                            if r == 0:
                                g.tensor_tensor(q[:, j, :], rt[:, m % 4, 0:T], rt[:, m % 4, T:2 * T], ALU.add).then_inc(add_done, 1)
                            else:
                                if j >= 2:
                                    pool.wait_ge(qkb_done, i * NC_ + j - 1)
                                g.tensor_tensor(kt[:, j % 2, :], rt[:, m % 4, 0:T], rt[:, m % 4, T:2 * T], ALU.add).then_inc(add_done, 1)
                        if j == 1 and prev is not None:
                            tail.pool(pool, prev, prev)
                    pre(i + 1)

                pre(0)
                turn(0, None)
                with pool.Fori(1, B) as i:
                    turn(i, i - 1)
                tail.pool(pool, B - 1, B - 1)

            @block.scalar
            def _(act):
                a = nc.scalar
                act.wait_ge(loaded, 16 * len(loads))
                act.wait_ge(zeros, 4)
                a.activation(wdh[:], wd_in[:], ACT.Copy).then_inc(w_high, 1)
                for n in range(NU):
                    act.wait_ge(up_loaded, 16 * (n + 1))
                    a.activation(uh[:, n, :], up_in[:], ACT.Copy).then_inc(w_high, 1)
                for n in range(2):
                    act.wait_ge(up_loaded, 16 * (NU + n + 1))
                    a.activation(sel[:, n * WU:(n + 1) * WU], up_in[:], ACT.Copy).then_inc(w_high, 1)

                def pre_high(i):
                    act.wait_ge(hf_done, i + 1)
                    a.activation(hh[:], hf[:], ACT.Copy).then_inc(hh_done, 1)

                def latents(i):
                    act.wait_ge(c_ps, i + 1)
                    a.activation(ch[:], ps[bPRE][:, T:2 * T], ACT.Copy).then_inc(ch_done, 1)

                def turn(i, prev):
                    for j in range(NC_):
                        if j < 4:
                            k, half = divmod(j, 2)
                            act.wait_ge(v_ps, i * 4 + j + 1)
                            for u in range(HPC):
                                m = a.activation(va[:, k, half * 8 + u:half * 8 + 8:HPC, u * DH:(u + 1) * DH],
                                                 ps[bV[j % 2]][:].rearrange("p (g u d) -> p g u d", u=HPC, d=DH)[:, :, u, :], ACT.Copy)
                            m.then_inc(v_kept, 1)
                        act.wait_ge(add_done, i * 2 * NC_ + 2 * j + 2)
                        a.activation(qb[:, j, :], q[:, j, :], ACT.Copy)
                        for u in range(HPC):
                            rows = slice(u * DH, (u + 1) * DH)
                            a.activation(kb[rows, j, u, :], kt[rows, j % 2, :], ACT.Copy)
                            m = a.activation(kz[rows, j, u, :], kt[rows, j % 2, :], ACT.Copy)
                        m.then_inc(qkb_done, 1)
                        if j == 3 and prev is not None:
                            tail.act(act, prev, prev)
                    act.wait_ge(nm_ps, i + 1)
                    a.activation(nmt[:], ps[bNM][:, 0:T], ACT.Copy).then_inc(nm_kept, 1)

                    def keep_sums(g):
                        act.wait_ge(pv_done, i * H + HPC * g + HPC)
                        if g >= 2:
                            act.wait_ge(rec_done, i * NC_ + g - 1)
                        for u in range(HPC):
                            m = a.activation(den[u * DH:(u + 1) * DH, g % 2, :],
                                             ps[bPV[g % 2]][(1 - u) * DH:(2 - u) * DH, u * T:(u + 1) * T], ACT.Copy)
                        m.then_inc(den_kept, 1)

                    for h in range(H):
                        act.wait_ge(st_ps, i * H + h + 1)
                        if h >= 3:
                            act.wait_ge(pv_done, i * H + h - 2)
                        a.activation(pt[:, h % 3, :], ps[bST[h % 4]][:], ACT.Exp, scale=SCALE).then_inc(exp_done, 1)
                        if h == 2:
                            pre_high(i + 1)
                        if h == 6:
                            latents(i + 1)
                        if h >= 3 and h % 2 == 1:
                            keep_sums(h // 2 - 1)
                    keep_sums(NC_ - 1)

                pre_high(0)
                latents(0)
                turn(0, None)
                with act.Fori(1, B) as i:
                    turn(i, i - 1)
                tail.act(act, B - 1, B - 1)

            @block.tensor
            def _(pe):
                pe.wait_ge(w_high, 3 + NU)
                pe.wait_ge(w_low, 1 + NU)
                pe.wait_ge(zeros, 4)
                pe.wait_ge(loaded, 16 * len(loads))

                def pre_turn(i):
                    pe.wait_ge(xn_done, i + 1)
                    for t in range(KC):
                        m = nc.tensor.transpose(ps[bPRE][:, t * P:(t + 1) * P], xn[:, t, :], self.idF[:])
                    m.then_inc(hnt_ps, 1)

                def pre_down(i):
                    pe.wait_ge(hl_done, i + 1)
                    mm3(nc, ps[bPRE][:, T:2 * T], wdh[:], wdl[:], hh[:], hl[:]).then_inc(c_ps, 1)

                def turn(i, prev):
                    pe.wait_ge(ch_done, i + 1)
                    pe.wait_ge(cl_done, i + 1)

                    def project(j):
                        if j >= 2:
                            pe.wait_ge(rt_done, i * 2 * NC_ + 2 * j - 2)
                        elif prev is not None:
                            pe.wait_ge(exp_done, i * H)
                        for r in range(2):
                            for sw in range(2):
                                col = slice(j * P, (j + 1) * P)
                                m = mm3(nc, ps[2 * (j % 2) + r][:, sw * T:(sw + 1) * T], uh[:, 2 * r + sw, col],
                                        ul[:, 2 * r + sw, col], ch[:], cl[:])
                            m.then_inc(qk_ps, 1)

                    def values(n):
                        if n >= 2:
                            pe.wait_ge(v_kept, i * 4 + n - 1)
                        k, half = divmod(n, 2)
                        col = slice(half * 512, (half + 1) * 512)
                        t = slice(k * P, (k + 1) * P)
                        mm3(nc, ps[bV[n % 2]][:], ch[:, t], cl[:, t], uh[:, 4, col], ul[:, 4, col]).then_inc(v_ps, 1)

                    def maxima(j):
                        pe.wait_ge(qkb_done, i * NC_ + j + 1)
                        for u in range(HPC):
                            h = HPC * j + u
                            if h >= 2:
                                pe.wait_ge(max_done, i * H + h - 1)
                            elif u == 0:
                                pe.wait_ge(v_kept, i * 4 + 4)
                            for t in range(KC):
                                m = nc.tensor.matmul(ps[bM[h % 2]][:, t * T:(t + 1) * T], qb[:, j, t * P:(t + 1) * P],
                                                     kb[:, j, u, :], start=True, stop=True)
                            m.then_inc(s_ps, 1)

                    for j in range(NC_):
                        project(j)
                        if j < 4:
                            values(j)
                        if j == 3 and prev is not None:
                            tail.pe(pe, prev)
                        if j >= 4:
                            maxima(j - 4)
                    for j in range(NC_ - 4, NC_):
                        maxima(j)
                    pre_turn(i + 1)
                    pe.wait_ge(max_done, i * H + H)
                    for t in range(KC):
                        m = nc.tensor.transpose(ps[bNM][:, t * P:(t + 1) * P], negm[:, t, :], self.idF[:])
                    m.then_inc(nm_ps, 1)
                    pe.wait_ge(nm_kept, i + 1)

                    def scores_t(h):
                        if h >= 4:
                            pe.wait_ge(exp_done, i * H + h - 3)
                        j, u = divmod(h, HPC)
                        out = ps[bST[h % 4]]
                        for k in range(KC):
                            nc.tensor.matmul(out[:, k * T:(k + 1) * T], kz[:, j, u, k * P:(k + 1) * P], q[:, j, :],
                                             start=True, stop=False)
                            m = nc.tensor.matmul(out[:, k * T:(k + 1) * T], sel[:, h * P:(h + 1) * P], nmt[:], start=False,
                                                 stop=True)
                        m.then_inc(st_ps, 1)

                    def pv(h):
                        g, u = divmod(h, HPC)
                        pe.wait_ge(exp_done, i * H + h + 1)
                        if u == 0 and g >= 2:
                            pe.wait_ge(on_done, i * NC_ + g - 1)
                        for k in range(KC):
                            m = nc.tensor.matmul(ps[bPV[g % 2]][:, u * T:(u + 1) * T], va[:, k, h, :],
                                                 pt[:, h % 3, k * T:(k + 1) * T], start=(k == 0), stop=(k == KC - 1))
                        m.then_inc(pv_done, 1)

                    LAG = 2
                    for h in range(H + LAG):
                        if h < H:
                            scores_t(h)
                        if h >= LAG:
                            pv(h - LAG)
                        if h == 5:
                            pre_down(i + 1)
                    pe.wait_ge(on_done, i * NC_ + NC_)
                    for t in range(KC):
                        for j in range(NC_):
                            m = nc.tensor.matmul(ps[6][:, t * P:(t + 1) * P], ot[:, j, t * P:(t + 1) * P], wout[:, j, :],
                                                 start=(j == 0), stop=(j == NC_ - 1))
                    m.then_inc(tail.y_ps, 1)

                pre_turn(0)
                pre_down(0)
                turn(0, None)
                with pe.Fori(1, B) as i:
                    turn(i, i - 1)
                tail.pe(pe, B - 1)

            @block.vector
            def _(dve):
                v = nc.vector
                v.memset(negm[:], 0.0).then_inc(zeros, 1)
                v.memset(kb[:], 0.0).then_inc(zeros, 1)
                v.memset(va[:], 1.0).then_inc(zeros, 1)
                v.memset(kz[:], 0.0).then_inc(zeros, 1)
                dve.wait_ge(w_high, 1)
                v.tensor_tensor(wdl[:], wd_in[:], wdh[:].bitcast(F32), ALU.subtract).then_inc(w_low, 1)
                for n in range(NU):
                    dve.wait_ge(w_high, 2 + n)
                    v.tensor_tensor(ul[:, n, :], up_in[:], uh[:, n, :].bitcast(F32), ALU.subtract).then_inc(w_low, 1)
                dve.wait_ge(zeros, 4)

                def pre_stats(i, link):
                    self.norm_stats(link, self.X[:, bass.ds((i % B) * KC, KC), :], st, mv, ve[:], KC, LN_EPS).then_inc(ve_done, 1)

                def pre_norm(i):
                    dve.wait_ge(rs_done, i + 1)
                    for t in range(KC):
                        m = v.tensor_scalar(xn[:, t, :], self.X[:, bass.ds((i % B) * KC + t, 1), :].rearrange("p a d -> p (a d)"),
                                            mv[:, t, 0:1], rs[:, t:t + 1], ALU.subtract, ALU.mult)
                    m.then_inc(xn_done, 1)

                def pre_scale(i):
                    dve.wait_ge(hnt_ps, i + 1)
                    v.tensor_scalar(hf[:], ps[bPRE][:, 0:T], ln[:, 0:1], ln[:, 1:2], ALU.mult, ALU.add).then_inc(hf_done, 1)

                def pre_low(i):
                    dve.wait_ge(hh_done, i + 1)
                    v.tensor_tensor(hl[:], hf[:], hh[:].bitcast(F32), ALU.subtract).then_inc(hl_done, 1)

                def latents_low(i):
                    dve.wait_ge(ch_done, i + 1)
                    v.tensor_tensor(cl[:], ps[bPRE][:, T:2 * T], ch[:].bitcast(F32), ALU.subtract).then_inc(cl_done, 1)

                def turn(i, prev):
                    link = Chain(dve, chain, i, 2)
                    tlink = None if prev is None else Chain(dve, tchain, prev, 3)

                    def maxes(j):
                        for u in range(HPC):
                            h = HPC * j + u
                            dve.wait_ge(s_ps, i * H + h + 1)
                            v.tensor_reduce(negm[:, :, h:h + 1], ps[bM[h % 2]][:].rearrange("p (t k) -> p t k", t=KC), AX.X,
                                            ALU.max, negate=True).then_inc(max_done, 1)

                    for j in range(NC_):
                        for r in range(2):
                            m = 2 * j + r
                            dve.wait_ge(qk_ps, i * 2 * NC_ + m + 1)
                            if m >= 4:
                                dve.wait_ge(add_done, i * 2 * NC_ + m - 3)
                            v.tensor_tensor(rt[:, m % 4, :], ps[2 * (j % 2) + r][:], cs[:], ALU.mult).then_inc(rt_done, 1)
                        if prev is not None:
                            if j == 0:
                                tail.dve_stats(dve, tlink, prev, prev)
                            if j == 2:
                                tail.dve_norm(dve, prev)
                                tlink.close()
                            if j == 4:
                                tail.dve_low(dve, prev, prev)
                        if j >= 4:
                            maxes(j - 4)
                    pre_stats(i + 1, link)
                    for j in range(NC_ - 4, NC_ - 1):
                        maxes(j)
                    pre_norm(i + 1)
                    maxes(NC_ - 1)
                    pre_scale(i + 1)
                    for g in range(NC_):
                        dve.wait_ge(den_kept, i * NC_ + g + 1)
                        v.reciprocal(rec[:, g % 2, :], den[:, g % 2, :]).then_inc(rec_done, 1)
                        dve.wait_ge(rec_done, i * NC_ + g + 1)
                        for u in range(HPC):
                            rows = slice(u * DH, (u + 1) * DH)
                            m = v.tensor_tensor(ot[rows, g, :], ps[bPV[g % 2]][rows, u * T:(u + 1) * T], rec[rows, g % 2, :], ALU.mult)
                        m.then_inc(on_done, 1)
                        if g == 0:
                            pre_low(i + 1)
                        if g == 3:
                            latents_low(i + 1)
                    link.close()

                once = Chain(dve, ochain, 0, 5)
                pre_stats(0, once)
                pre_norm(0)
                pre_scale(0)
                pre_low(0)
                latents_low(0)
                turn(0, None)
                with dve.Fori(1, B) as i:
                    turn(i, i - 1)
                tail.dve_stats(dve, once, B - 1, B - 1)
                tail.dve_norm(dve, B - 1)
                tail.dve_low(dve, B - 1, B - 1)
                once.close()

    def selective_scan(self):
        nc, I, ps = self.nc, self.ins, self.ps
        NST, KCONV, NCH, NS = 16, 4, 2, 2
        NB = NS * T
        TB = NB // P
        NBLK = NTOK // NB
        NQ = NST * NCH
        with ExitStack() as c_:
            def sb(name, shape, dt=F32):
                return c_.enter_context(nc.sbuf_tensor("m2_" + name, shape, dt))

            def sem(name):
                return self.semaphore("m2_" + name)

            w_in, wh, wl = sb("w_in", [P, 4 * P]), sb("wh", [P, 4 * P], F32R), sb("wl", [P, 4 * P], F32R)
            xp_w, dt_w, out_w = sb("xp_w", [P, NCH, P]), sb("dt_w", [P, NCH * P]), sb("out_w", [P, NCH, D])
            sel_in, sel = sb("sel_in", [64, 2 * NST * P]), sb("sel", [64, 2 * NST * P], F32R)
            cw, cvec, a_log, am = sb("cw", [P, NCH, KCONV]), sb("cvec", [P, NCH, 3]), sb("a_log", [P, NCH, NST]), sb("a", [P, NCH, NST])
            xp = sb("xp", [P, NCH, NS, KCONV - 1 + T])
            sz, cv, xt = sb("sz", [P, NCH, NB]), sb("cv", [P, NCH, NB]), sb("xt", [P, NCH, NB])
            st, st_hi, dbl = sb("st", [64, NB], F32R), sb("st_hi", [64, NB], F32R), sb("dbl", [P, NB])
            p_, en, w1, lw, delta, dx = (sb(n, [P, NCH, NB]) for n in ("p", "en", "w1", "lw", "delta", "dx"))
            dA, dbu, h, hc, cs = sb("dA", [P, 3, NB]), sb("dbu", [P, 2, NB]), sb("h", [P, 3, NB]), sb("hc", [P, 2, NB]), sb("cs", [P, 2, NB])
            y = sb("y_", [P, NCH, NB])
            tail = Tail(self, c_, "m2", 0, TB, ps[7][:], ps[4][:])
            bXZ, bDBL, bDP, bB, bC, bY = (0, 1, 2, 3), 4, (5, 6), (0, 1), (2, 3), (5, 6)

            loaded, w_high, w_low, zeros = sem("weights_loaded"), sem("weights_high"), sem("weights_low"), sem("zeros")
            a_exp, a_neg = sem("a_exp"), sem("a_negated")
            xz_ps, xp_kept, sz_done, conv_done, xt_done = sem("xz_ready"), sem("x_padded"), sem("z_silu"), sem("conv_done"), sem("x_silu")
            dbl_ps, dbl_kept, st_low, dp_ps, p_done = sem("bcdt_ready"), sem("bcdt_kept"), sem("bc_low"), sem("dt_ready"), sem("dt_biased")
            en_done, w1_done, lw_done, dx_done = sem("exp_done"), sem("one_plus"), sem("ln_done"), sem("delta_ready")
            b_ps, c_ps, c_kept = sem("b_broadcast"), sem("c_broadcast"), sem("c_kept")
            dA_done, dbu_done, h_done, hc_done, sum_done = (sem("decay_ready"), sem("input_ready"), sem("state_ready"),
                                                           sem("readout_ready"), sem("readout_summed"))
            y_done, chain = sem("gated"), sem("dve_chain")
            block = c_.enter_context(nc.Block())
            loads = ((w_in, "m2_w"), (xp_w, "m2_xp"), (dt_w, "m2_dt"), (out_w, "m2_out"), (sel_in, "m2_sel"),
                     (cw, "m2_cw"), (cvec, "m2_cvec"), (a_log, "m2_alog"))

            @block.sync
            def _(sp):
                for dst, src in loads:
                    sp.dma_start(dst[:], I[src]).then_inc(loaded, 16)

            @block.gpsimd
            def _(pool):
                g = nc.gpsimd
                with pool.Fori(0, NBLK) as i:
                    for q in range(NQ):
                        n, c = divmod(q, NCH)
                        pool.wait_ge(h_done, i * NQ + q + 1)
                        pool.wait_ge(c_kept, i * NST + n + 1)
                        if q >= 2:
                            pool.wait_ge(sum_done, i * NQ + q - 1)
                        g.tensor_tensor(hc[:, q % 2, :], h[:, q % 3, :], cs[:, n % 2, :], ALU.mult).then_inc(hc_done, 1)
                    tail.pool(pool, i, i)

            @block.scalar
            def _(act):
                a = nc.scalar
                act.wait_ge(loaded, 16 * len(loads))
                a.activation(wh[:], w_in[:], ACT.Copy).then_inc(w_high, 1)
                a.activation(sel[:], sel_in[:], ACT.Copy).then_inc(w_high, 1)
                a.activation(am[:], a_log[:], ACT.Exp).then_inc(a_exp, 1)
                act.wait_ge(a_neg, 1)
                with act.Fori(0, NBLK) as i:
                    for c in range(NCH):
                        act.wait_ge(xz_ps, i * 4 + c + 1)
                        a.activation(xp[:, c, :, KCONV - 1:], ps[bXZ[c]][:].rearrange("p (s t) -> p s t", s=NS), ACT.Copy).then_inc(xp_kept, 1)
                    for c in range(NCH):
                        act.wait_ge(conv_done, i * NCH + c + 1)
                        a.activation(xt[:, c, :], cv[:, c, :], ACT.Silu, bias=cvec[:, c, 0:1]).then_inc(xt_done, 1)
                    act.wait_ge(xz_ps, i * 4 + 4)
                    a.activation(sz[:, 0, :], ps[bXZ[2]][:], ACT.Silu)
                    a.activation(sz[:, 1, :], ps[bXZ[3]][:], ACT.Silu).then_inc(sz_done, 1)
                    act.wait_ge(dbl_ps, i + 1)
                    a.activation(dbl[:], ps[bDBL][:], ACT.Copy)
                    a.activation(st[0:32, :], ps[bDBL][0:32, :], ACT.Copy)
                    a.activation(st_hi[32:64, :], ps[bDBL][32:64, :], ACT.Copy).then_inc(dbl_kept, 1)
                    act.wait_ge(p_done, i + 1)
                    a.activation(en[:], en[:], ACT.Exp, scale=-1.0).then_inc(en_done, 1)
                    act.wait_ge(w1_done, i + 1)
                    a.activation(lw[:], w1[:], ACT.Ln).then_inc(lw_done, 1)
                    act.wait_ge(dx_done, i + 1)

                    def keep_c(n):
                        act.wait_ge(c_ps, i * NST + n + 1)
                        if n >= 2:
                            act.wait_ge(hc_done, i * NQ + 2 * n - 2)
                        a.activation(cs[:, n % 2, :], ps[bC[n % 2]][:], ACT.Copy).then_inc(c_kept, 1)

                    for q in range(NQ):
                        n, c = divmod(q, NCH)
                        if q >= 3:
                            act.wait_ge(h_done, i * NQ + q - 2)
                        a.activation(dA[:, q % 3, :], delta[:, c, :], ACT.Exp, scale=am[:, c, n:n + 1]).then_inc(dA_done, 1)
                        if c == 0:
                            keep_c(n)
                    tail.act(act, i, i)

            @block.tensor
            def _(pe):
                pe.wait_ge(w_high, 2)
                pe.wait_ge(w_low, 1)
                with pe.Fori(0, NBLK) as i:
                    pe.wait_ge(tail.done, i + 1)
                    xh, xl = self.XH[:, bass.ds(i * NB, NB)], self.XL[:, bass.ds(i * NB, NB)]
                    for k in range(4):
                        s = slice(k * P, (k + 1) * P)
                        mm3(nc, ps[bXZ[k]][:], wh[:, s], wl[:, s], xh, xl).then_inc(xz_ps, 1)
                    for c in range(NCH):
                        pe.wait_ge(xt_done, i * NCH + c + 1)
                        m = nc.tensor.matmul(ps[bDBL][:], xp_w[:, c, :], xt[:, c, :], start=(c == 0), stop=(c == NCH - 1))
                    m.then_inc(dbl_ps, 1)
                    pe.wait_ge(dbl_kept, i + 1)
                    for c in range(NCH):
                        m = nc.tensor.matmul(ps[bDP[c]][:], dt_w[:, c * P:(c + 1) * P], dbl[:], start=True, stop=True)
                    m.then_inc(dp_ps, 1)
                    pe.wait_ge(st_low, i + 1)
                    pe.wait_ge(sz_done, i + 1)

                    def broadcast(n):
                        if n >= 2:
                            pe.wait_ge(dbu_done, i * NQ + 2 * n - 2)
                        nc.tensor.matmul(ps[bB[n % 2]][:], sel[:, n * P:(n + 1) * P], st[:], start=True, stop=True).then_inc(b_ps, 1)
                        if n >= 2:
                            pe.wait_ge(c_kept, i * NST + n - 1)
                        nc.tensor.matmul(ps[bC[n % 2]][:], sel[:, (NST + n) * P:(NST + n + 1) * P], st[:], start=True,
                                         stop=True).then_inc(c_ps, 1)

                    broadcast(0)
                    broadcast(1)
                    pe.wait_ge(p_done, i + 1)
                    for q in range(NQ):
                        n, c = divmod(q, NCH)
                        pe.wait_ge(hc_done, i * NQ + q + 1)
                        nc.tensor.matmul(ps[bY[c]][:], self.idF[:], hc[:, q % 2, :], start=(n == 0),
                                         stop=(n == NST - 1)).then_inc(sum_done, 1)
                        if c == NCH - 1 and n + 2 < NST:
                            broadcast(n + 2)
                    pe.wait_ge(y_done, i + 1)
                    for t in range(TB):
                        for c in range(NCH):
                            m = nc.tensor.matmul(ps[7][:, t * P:(t + 1) * P], y[:, c, t * P:(t + 1) * P], out_w[:, c, :],
                                                 start=(c == 0), stop=(c == NCH - 1))
                    m.then_inc(tail.y_ps, 1)
                    tail.pe(pe, i)

            @block.vector
            def _(dve):
                v = nc.vector
                v.memset(xp[:, :, :, 0:KCONV - 1], 0.0).then_inc(zeros, 1)
                dve.wait_ge(w_high, 1)
                v.tensor_tensor(wl[:], w_in[:], wh[:].bitcast(F32), ALU.subtract).then_inc(w_low, 1)
                dve.wait_ge(a_exp, 1)
                v.tensor_scalar(am[:], am[:], -1.0, None, ALU.mult).then_inc(a_neg, 1)
                dve.wait_ge(zeros, 1)
                dve.sem_inc(tail.done, 1)
                with dve.Fori(0, NBLK) as i:
                    link = Chain(dve, chain, i, 15)
                    def conv(c, k):
                        src = xp[:, c, :, k:k + T]
                        dst = cv[:, c, :].rearrange("p (s t) -> p s t", s=NS)
                        if k == 0:
                            return v.tensor_scalar(dst, src, cw[:, c, 0:1], None, ALU.mult)
                        return v.scalar_tensor_tensor(dst, src, cw[:, c, k:k + 1], dst, ALU.mult, ALU.add)

                    for c in range(NCH):
                        dve.wait_ge(xp_kept, i * NCH + c + 1)
                        for k in range(KCONV - 1):
                            link(conv(c, k))
                        conv(c, KCONV - 1).then_inc(conv_done, 1)
                    dve.wait_ge(dbl_kept, i + 1)
                    v.tensor_tensor(st[32:64, :], ps[bDBL][32:64, :], st_hi[32:64, :].bitcast(F32), ALU.subtract).then_inc(st_low, 1)
                    dve.wait_ge(dp_ps, i + 1)
                    for c in range(NCH):
                        m = v.tensor_scalar(p_[:, c, :], ps[bDP[c]][:], cvec[:, c, 1:2], None, ALU.add)
                    link(m)
                    v.tensor_scalar(w1[:], p_[:], -1.0, None, ALU.mult)
                    link(v.tensor_scalar(delta[:], p_[:], 0.0, None, ALU.max))
                    v.tensor_tensor(en[:], p_[:], w1[:], ALU.max).then_inc(p_done, 1)
                    dve.wait_ge(en_done, i + 1)
                    v.tensor_scalar(w1[:], en[:], 1.0, None, ALU.add).then_inc(w1_done, 1)
                    dve.wait_ge(w1_done, i + 1)
                    link(v.scalar_tensor_tensor(en[:], w1[:], 1.0, en[:], ALU.subtract, ALU.subtract))
                    link(v.tensor_tensor(delta[:], delta[:], en[:], ALU.subtract))
                    dve.wait_ge(lw_done, i + 1)
                    link(v.tensor_tensor(delta[:], delta[:], lw[:], ALU.add))
                    v.tensor_tensor(dx[:], delta[:], xt[:], ALU.mult).then_inc(dx_done, 1)
                    dve.wait_ge(dx_done, i + 1)
                    for q in range(NQ):
                        n, c = divmod(q, NCH)
                        dve.wait_ge(b_ps, i * NST + n + 1)
                        v.tensor_tensor(dbu[:, q % 2, :], dx[:, c, :], ps[bB[n % 2]][:], ALU.mult).then_inc(dbu_done, 1)
                        dve.wait_ge(dbu_done, i * NQ + q + 1)
                        dve.wait_ge(dA_done, i * NQ + q + 1)
                        if q >= 3:
                            dve.wait_ge(hc_done, i * NQ + q - 2)
                        for s in range(NS):
                            r = slice(s * T, (s + 1) * T)
                            m = v.tensor_tensor_scan(h[:, q % 3, r], dA[:, q % 3, r], dbu[:, q % 2, r], 0.0, ALU.mult, ALU.add)
                        m.then_inc(h_done, 1)
                    dve.wait_ge(sum_done, i * NQ + NQ)
                    for c in range(NCH):
                        m = v.scalar_tensor_tensor(y[:, c, :], xt[:, c, :], cvec[:, c, 2:3], ps[bY[c]][:], ALU.mult, ALU.add)
                    link(m)
                    v.tensor_tensor(y[:], y[:], sz[:], ALU.mult).then_inc(y_done, 1)
                    tail.dve(dve, link, i, i)
                    tail.dve_low(dve, i, i)
                    link.close()

    def window_attention(self):
        nc, I, ps = self.nc, self.ins, self.ps
        W, S, KC = 3, 2, T // P
        SCALE = 1.0 / 8.0 ** 0.5
        PAST = -1e30
        with ExitStack() as c:
            def sb(name, shape, dt=F32):
                return c.enter_context(nc.sbuf_tensor("a3_" + name, shape, dt))

            def sem(name):
                return self.semaphore("a3_" + name)

            def both(make, name, *a):
                return [make(f"{name}{s}", *a) for s in range(S)]

            w_in = sb("w_in", [P, 3 * D])
            wh, wl = sb("wh", [P, 3 * D], F32R), sb("wl", [P, 3 * D], F32R)
            wo, bo, one_row = sb("wo", [P, D]), sb("bo", [1, D]), sb("one_row", [1, P])
            vec, heads = sb("vec", [P, 3]), sb("heads", [P, P])
            q, kp, vp = both(sb, "q", [P, T]), both(sb, "kp", [P, W - 1 + T]), both(sb, "vp", [P, W - 1 + T])
            prod, e, pv = both(sb, "prod", [P, W, T]), both(sb, "e", [P, W, T]), both(sb, "pv", [P, W, T])
            m, den, rec, o, on = (both(sb, n, [P, T]) for n in ("m", "den", "rec", "o", "on"))
            bA, bB, bC = [ps[0], ps[4]], [ps[1], ps[5]], [ps[2], ps[6]]
            tail = [Tail(self, c, "a3", s, KC, bB[s][:, T:2 * T], bB[s][:, 0:T]) for s in range(S)]
            loaded, w_high, w_low = sem("weights_loaded"), sem("weights_high"), sem("weights_low")
            qk_ps, v_ps, qk_kept, v_kept = both(sem, "qk_ready"), both(sem, "v_ready"), both(sem, "qk_kept"), both(sem, "v_kept")
            prod_done, prod2_done, s_ps, shifted = (both(sem, "products"), both(sem, "products2"), both(sem, "scores_ready"),
                                                    both(sem, "shifted"))
            exp_done, pv_done, on_done = both(sem, "exp_done"), both(sem, "pv_products"), both(sem, "normalised")
            chain = both(sem, "dve_chain")
            block = c.enter_context(nc.Block())
            loads = ((w_in, "a3_w"), (wo, "a3_wo"), (bo, "a3_bo"), (vec, "a3_vec"), (heads, "a3_heads"), (one_row, "one_row"))

            @block.sync
            def _(sp):
                for dst, src in loads:
                    sp.dma_start(dst[:], I[src]).then_inc(loaded, 16)

            @block.gpsimd
            def _(pool):
                g = nc.gpsimd
                with pool.Fori(0, B // S) as i:
                    for s in range(S):
                        pool.wait_ge(qk_kept[s], i + 1)
                        g.tensor_tensor(prod[s][:, 2, :], q[s][:], kp[s][:, 0:T], ALU.mult).then_inc(prod2_done[s], 1)
                    for s in range(S):
                        pool.wait_ge(exp_done[s], i + 1)
                        pool.wait_ge(v_kept[s], i + 1)
                        g.tensor_tensor(pv[s][:, 2, :], e[s][:, 2, :], vp[s][:, 0:T], ALU.mult)
                        g.tensor_tensor(pv[s][:, 1, :], e[s][:, 1, :], vp[s][:, 1:T + 1], ALU.mult).then_inc(pv_done[s], 1)
                    for s in range(S):
                        tail[s].pool(pool, i, i * S + s)

            @block.scalar
            def _(act):
                a = nc.scalar
                act.wait_ge(loaded, 16 * len(loads))
                a.activation(wh[:], w_in[:], ACT.Copy).then_inc(w_high, 1)
                with act.Fori(0, B // S) as i:
                    for s in range(S):
                        act.wait_ge(qk_ps[s], i + 1)
                        a.activation(q[s][:], bA[s][:, 0:T], ACT.Identity, bias=vec[:, 0:1])
                        a.activation(kp[s][:, W - 1:], bA[s][:, T:2 * T], ACT.Identity, bias=vec[:, 1:2]).then_inc(qk_kept[s], 1)
                        act.wait_ge(v_ps[s], i + 1)
                        a.activation(vp[s][:, W - 1:], bB[s][:, 0:T], ACT.Identity, bias=vec[:, 2:3]).then_inc(v_kept[s], 1)
                    for s in range(S):
                        act.wait_ge(shifted[s], i + 1)
                        a.activation(e[s][:], e[s][:], ACT.Exp, scale=SCALE).then_inc(exp_done[s], 1)
                    for s in range(S):
                        tail[s].act(act, i, i * S + s)

            @block.tensor
            def _(pe):
                pe.wait_ge(w_high, 1)
                pe.wait_ge(w_low, 1 + 2 * S)
                with pe.Fori(0, B // S) as i:
                    for s in range(S):
                        seq = i * S + s
                        pe.wait_ge(tail[s].done, i + 1)
                        xh, xl = self.XH[:, bass.ds(seq * T, T)], self.XL[:, bass.ds(seq * T, T)]
                        mm3(nc, bA[s][:, 0:T], wh[:, 0:D], wl[:, 0:D], xh, xl)
                        mm3(nc, bA[s][:, T:2 * T], wh[:, D:2 * D], wl[:, D:2 * D], xh, xl).then_inc(qk_ps[s], 1)
                        mm3(nc, bB[s][:, 0:T], wh[:, 2 * D:], wl[:, 2 * D:], xh, xl).then_inc(v_ps[s], 1)
                    for s in range(S):
                        pe.wait_ge(prod_done[s], i + 1)
                        nc.tensor.matmul(bC[s][:], heads[:], prod[s][:, 0:2, :].rearrange("p j t -> p (j t)"), start=True, stop=True)
                        pe.wait_ge(prod2_done[s], i + 1)
                        nc.tensor.matmul(bA[s][:, 0:T], heads[:], prod[s][:, 2, :], start=True, stop=True).then_inc(s_ps[s], 1)
                    for s in range(S):
                        pe.wait_ge(on_done[s], i + 1)
                        for t in range(KC):
                            out = bB[s][:, T + t * P:T + (t + 1) * P]
                            nc.tensor.matmul(out, on[s][:, t * P:(t + 1) * P], wo[:], start=True, stop=False)
                            mm = nc.tensor.matmul(out, one_row[:], bo[:], start=False, stop=True)
                        mm.then_inc(tail[s].y_ps, 1)
                    for s in range(S):
                        tail[s].pe(pe, i)

            @block.vector
            def _(dve):
                v = nc.vector
                for s in range(S):
                    v.memset(kp[s][:, 0:W - 1], 0.0).then_inc(w_low, 1)
                    v.memset(vp[s][:, 0:W - 1], 0.0).then_inc(w_low, 1)
                dve.wait_ge(w_high, 1)
                v.tensor_tensor(wl[:], w_in[:], wh[:].bitcast(F32), ALU.subtract).then_inc(w_low, 1)
                for s in range(S):
                    dve.sem_inc(tail[s].done, 1)
                with dve.Fori(0, B // S) as i:
                    link = [Chain(dve, chain[s], i, 9) for s in range(S)]
                    for s in range(S):
                        dve.wait_ge(qk_kept[s], i + 1)
                        v.tensor_tensor(prod[s][:, 0, :], q[s][:], kp[s][:, 2:T + 2], ALU.mult)
                        v.tensor_tensor(prod[s][:, 1, :], q[s][:], kp[s][:, 1:T + 1], ALU.mult).then_inc(prod_done[s], 1)
                    for s in range(S):
                        dve.wait_ge(s_ps[s], i + 1)
                        v.memset(bC[s][:, T:T + 1], PAST)
                        link[s](v.memset(bA[s][:, 0:2], PAST))
                        link[s](v.tensor_reduce(m[s][:], bC[s][:].rearrange("p (j t) -> p t j", j=2), AX.X, ALU.max))
                        link[s](v.tensor_tensor(m[s][:], m[s][:], bA[s][:, 0:T], ALU.max))
                        v.tensor_tensor(e[s][:, 0:2, :], bC[s][:].rearrange("p (j t) -> p j t", j=2),
                                        m[s][:].unsqueeze(1).broadcast_to([P, 2, T]), ALU.subtract)
                        v.tensor_tensor(e[s][:, 2, :], bA[s][:, 0:T], m[s][:], ALU.subtract).then_inc(shifted[s], 1)
                    for s in range(S):
                        dve.wait_ge(exp_done[s], i + 1)
                        link[s](v.tensor_reduce(den[s][:], e[s][:].rearrange("p j t -> p t j"), AX.X, ALU.add))
                        v.reciprocal(rec[s][:], den[s][:])
                        dve.wait_ge(v_kept[s], i + 1)
                        link[s](v.tensor_tensor(pv[s][:, 0, :], e[s][:, 0, :], vp[s][:, 2:T + 2], ALU.mult))
                        dve.wait_ge(pv_done[s], i + 1)
                        link[s](v.tensor_reduce(o[s][:], pv[s][:].rearrange("p j t -> p t j"), AX.X, ALU.add))
                        v.tensor_tensor(on[s][:], o[s][:], rec[s][:], ALU.mult).then_inc(on_done[s], 1)
                    for s in range(S):
                        tail[s].dve_stats(dve, link[s], i, i * S + s)
                    for s in range(S):
                        tail[s].dve_norm(dve, i)
                    for s in range(S):
                        tail[s].dve_low(dve, i, i * S + s)
                        link[s].close()

    def fp4_mlp(self):
        nc, I, ps = self.nc, self.ins, self.ps
        S, KC, BL = 2, T // P, 16
        NI = 352
        NCH = (NI + P - 1) // P
        NIP = NCH * P
        NH = KC * NI
        NX = KC * D
        NWQ = 3 * NIP // S
        assert NWQ <= NH and NI % BL == 0
        QSTEPS = 9
        with ExitStack() as c:
            def sb(name, shape, dt=F32):
                return c.enter_context(nc.sbuf_tensor("f3_" + name, shape, dt))

            def sem(name):
                return self.semaphore("f3_" + name)

            def both(make, name, *a):
                return [make(f"{name}{s}", *a) for s in range(S)]

            w_in, wq = sb("w_in", [P, 3 * NIP]), sb("wq", [P, 3 * NIP])
            wg, wu, wd = sb("wg", [P, NIP]), sb("wu", [P, NIP]), sb("wd", [P, NCH, D])
            ab, sg, v_, t_, u_, ss_ = (both(sb, n, [P, NH]) for n in ("abs", "sign", "scaled", "code", "upper", "signscale"))
            am, sc = both(sb, "absmax", [P, NH // BL]), both(sb, "scale", [P, NH // BL])
            rsc = both(sb, "rscale", [P, NH // BL])
            u5 = both(sb, "five", [P, NH])
            xq, xqt = both(sb, "xq", [P, KC, D]), both(sb, "xqt", [P, T])
            sl, h, hq = both(sb, "silu", [P, KC, NI]), both(sb, "h", [P, NH]), both(sb, "hq", [P, KC, NIP])
            hqt = both(sb, "hqt", [P, NCH, T])
            bank = [ps[0:4], ps[4:8]]
            tail = [Tail(self, c, "f3", s, KC, bank[s][2][:, 0:T], None, last=True) for s in range(S)]
            loaded, w_t, w_kept, zeros = sem("weights_loaded"), sem("weightsT_ready"), sem("weightsT_kept"), sem("zeros")
            abs_done, v_done, u_done, q_done = (both(sem, "abs_done"), both(sem, "scaled_done"), both(sem, "upper_done"),
                                               both(sem, "quantised"))
            pch = both(sem, "pool_chain")
            xqt_ps, xqt_kept, gu_ps, silu_done, h_done = (both(sem, "xqT_ready"), both(sem, "xqT_kept"), both(sem, "gate_up_ready"),
                                                         both(sem, "silu_done"), both(sem, "h_done"))
            hqt_ps, hqt_kept = both(sem, "hqT_ready"), both(sem, "hqT_kept")
            chain, once = both(sem, "dve_chain"), sem("dve_once")
            block = c.enter_context(nc.Block())

            def wide(t, N):
                return t[:, 0:N // BL].unsqueeze(2).broadcast_to([P, N // BL, BL])

            def split16(t, N):
                return t[:, 0:N].rearrange("p (b k) -> p b k", k=BL)

            def quant_act(s, src, N):
                nc.scalar.activation(ab[s][:, 0:N], src, ACT.Abs)
                nc.scalar.activation(sg[s][:, 0:N], src, ACT.Sign).then_inc(abs_done[s], 1)

            def quant_dve(dve, link, s, n, N):
                v = nc.vector
                dve.wait_ge(abs_done[s], n + 1)
                link(v.tensor_reduce(am[s][:, 0:N // BL], split16(ab[s], N), AX.X, ALU.max))
                link(v.tensor_scalar(sc[s][:, 0:N // BL], am[s][:, 0:N // BL], 1.0 / 6.0, 1e-12, ALU.mult, ALU.max))
                link(v.reciprocal(rsc[s][:, 0:N // BL], sc[s][:, 0:N // BL]))
                v.tensor_tensor(split16(v_[s], N), split16(ab[s], N), wide(rsc[s], N), ALU.mult).then_inc(v_done[s], 1)
                dve.wait_ge(v_done[s], n + 1)
                link(v.tensor_scalar(t_[s][:, 0:N], v_[s][:, 0:N], 0.25, None, ALU.is_gt))
                for mid in (0.75, 1.25, 1.75):
                    link(v.scalar_tensor_tensor(t_[s][:, 0:N], v_[s][:, 0:N], mid, t_[s][:, 0:N], ALU.is_gt, ALU.add))

            def quant_dve_end(dve, link, s, n, N, out, view):
                v = nc.vector
                dve.wait_ge(u_done[s], n + 1)
                link(v.scalar_tensor_tensor(u_[s][:, 0:N], v_[s][:, 0:N], 2.5, u_[s][:, 0:N], ALU.is_gt, ALU.add))
                link(v.scalar_tensor_tensor(t_[s][:, 0:N], u_[s][:, 0:N], 2.0, t_[s][:, 0:N], ALU.mult, ALU.add))
                v.scalar_tensor_tensor(out, view(t_[s][:, 0:N]), 0.5, view(ss_[s][:, 0:N]), ALU.mult,
                                       ALU.mult).then_inc(q_done[s], 1)

            def quant_pool(pool, s, n, N):
                g = nc.gpsimd
                pool.wait_ge(v_done[s], n + 1)
                g.tensor_tensor(split16(ss_[s], N), split16(sg[s], N), wide(sc[s], N), ALU.mult)
                g.tensor_scalar(u5[s][:, 0:N], v_[s][:, 0:N], 5.0, 2.0, ALU.is_gt, ALU.mult)
                g.tensor_scalar(u_[s][:, 0:N], v_[s][:, 0:N], 3.5, None, ALU.is_gt).then_inc(pch[s], 1)
                pool.wait_ge(pch[s], n + 1)
                g.tensor_tensor(u_[s][:, 0:N], u_[s][:, 0:N], u5[s][:, 0:N], ALU.add).then_inc(u_done[s], 1)

            @block.sync
            def _(sp):
                sp.dma_start(w_in[:], I["f3_w"]).then_inc(loaded, 16)

            @block.gpsimd
            def _(pool):
                for s in range(S):
                    quant_pool(pool, s, 0, NWQ)
                    pool.sem_inc(tail[s].x_kept, 1)
                for s in range(S):
                    quant_pool(pool, s, 1, NX)
                with pool.Fori(0, B // S) as i:
                    for s in range(S):
                        quant_pool(pool, s, i * 2 + 2, NH)
                    for s in range(S):
                        quant_pool(pool, s, i * 2 + 3, NX)
                    for s in range(S):
                        tail[s].pool(pool, i, i * S + s)

            @block.scalar
            def _(act):
                a = nc.scalar
                act.wait_ge(loaded, 16)
                for s in range(S):
                    quant_act(s, w_in[:, s * NWQ:(s + 1) * NWQ], NWQ)
                act.wait_ge(w_t, 1)
                a.activation(wg[:], ps[0][:, 0:NIP], ACT.Copy)
                a.activation(wu[:], ps[1][:, 0:NIP], ACT.Copy)
                a.activation(wd[:], ps[2][:, 0:NIP].rearrange("p (c d) -> p c d", c=NCH), ACT.Copy).then_inc(w_kept, 1)

                def quant_x(i):
                    for s in range(S):
                        act.wait_ge(tail[s].done, i)
                        act.wait_ge(q_done[s], i * 2 + 1)
                        quant_act(s, self.X[:, bass.ds(((i * S + s) % B) * KC, KC), :].rearrange("p c d -> p (c d)"), NX)

                for s in range(S):
                    act.wait_ge(q_done[s], 1)
                    quant_act(s, self.X[:, s * KC:(s + 1) * KC, :].rearrange("p c d -> p (c d)"), NX)
                with act.Fori(0, B // S) as i:
                    for s in range(S):
                        act.wait_ge(xqt_ps[s], i + 1)
                        a.activation(xqt[s][:], bank[s][0][:, 0:T], ACT.Copy).then_inc(xqt_kept[s], 1)
                    for s in range(S):
                        act.wait_ge(gu_ps[s], i + 1)
                        for t in range(KC):
                            m = a.activation(sl[s][:, t, :], bank[s][t][:, 0:NI], ACT.Silu)
                        m.then_inc(silu_done[s], 1)
                    for s in range(S):
                        act.wait_ge(h_done[s], i + 1)
                        quant_act(s, h[s][:], NH)
                    quant_x(i + 1)
                    for s in range(S):
                        act.wait_ge(hqt_ps[s], i + 1)
                        a.activation(hqt[s][:, 0:2, :], bank[s][0][:].rearrange("p (c t) -> p c t", c=2), ACT.Copy)
                        a.activation(hqt[s][:, 2, :], bank[s][1][:, 0:T], ACT.Copy).then_inc(hqt_kept[s], 1)

            @block.tensor
            def _(pe):
                for s in range(S):
                    pe.wait_ge(q_done[s], 1)
                for k in range(3):
                    for j in range(NCH):
                        col = slice((k * NCH + j) * P, (k * NCH + j + 1) * P)
                        m = nc.tensor.transpose(ps[k][:, j * P:(j + 1) * P], wq[:, col], self.idF[:])
                m.then_inc(w_t, 1)
                pe.wait_ge(w_kept, 1)
                pe.wait_ge(zeros, S)
                with pe.Fori(0, B // S) as i:
                    for s in range(S):
                        pe.wait_ge(tail[s].done, i + 1)
                        pe.wait_ge(q_done[s], i * 2 + 2)
                        for t in range(KC):
                            m = nc.tensor.transpose(bank[s][0][:, t * P:(t + 1) * P], xq[s][:, t, :], self.idF[:])
                        m.then_inc(xqt_ps[s], 1)
                    for s in range(S):
                        pe.wait_ge(xqt_kept[s], i + 1)
                        for t in range(KC):
                            nc.tensor.matmul(bank[s][t][:, 0:NI], xqt[s][:, t * P:(t + 1) * P], wg[:, 0:NI], start=True, stop=True)
                            m = nc.tensor.matmul(bank[s][2 + t][:, 0:NI], xqt[s][:, t * P:(t + 1) * P], wu[:, 0:NI],
                                                 start=True, stop=True)
                        m.then_inc(gu_ps[s], 1)
                    for s in range(S):
                        pe.wait_ge(q_done[s], i * 2 + 3)
                        for k in range(NCH):
                            for t in range(KC):
                                o_ = bank[s][k // 2][:, (k % 2) * T + t * P:(k % 2) * T + (t + 1) * P]
                                m = nc.tensor.transpose(o_, hq[s][:, t, k * P:(k + 1) * P], self.idF[:])
                        m.then_inc(hqt_ps[s], 1)
                    for s in range(S):
                        pe.wait_ge(hqt_kept[s], i + 1)
                        for t in range(KC):
                            for k in range(NCH):
                                m = nc.tensor.matmul(bank[s][2][:, t * P:(t + 1) * P], hqt[s][:, k, t * P:(t + 1) * P],
                                                     wd[:, k, :], start=(k == 0), stop=(k == NCH - 1))
                        m.then_inc(tail[s].y_ps, 1)

            @block.vector
            def _(dve):
                v = nc.vector
                for s in range(S):
                    v.memset(hq[s][:, :, NI:], 0.0).then_inc(zeros, 1)
                link = Chain(dve, once, 0, 2 * S * QSTEPS)
                for s in range(S):
                    quant_dve(dve, link, s, 0, NWQ)
                for s in range(S):
                    quant_dve_end(dve, link, s, 0, NWQ, wq[:, s * NWQ:(s + 1) * NWQ], lambda x: x)

                def quant_x(links, i):
                    for s in range(S):
                        quant_dve(dve, links[s], s, i * 2 + 1, NX)
                    for s in range(S):
                        quant_dve_end(dve, links[s], s, i * 2 + 1, NX, xq[s][:].rearrange("p c d -> p (c d)"), lambda x: x)

                quant_x([link] * S, 0)
                link.close()
                with dve.Fori(0, B // S) as i:
                    links = [Chain(dve, chain[s], i, 2 * QSTEPS + 3) for s in range(S)]
                    for s in range(S):
                        dve.wait_ge(silu_done[s], i + 1)
                        for t in range(KC):
                            m = v.tensor_tensor(h[s][:, t * NI:(t + 1) * NI], bank[s][2 + t][:, 0:NI], sl[s][:, t, :], ALU.mult)
                        m.then_inc(h_done[s], 1)
                    for s in range(S):
                        quant_dve(dve, links[s], s, i * 2 + 2, NH)
                    for s in range(S):
                        quant_dve_end(dve, links[s], s, i * 2 + 2, NH, hq[s][:, :, 0:NI],
                                      lambda x: x.rearrange("p (c n) -> p c n", c=KC))
                    quant_x(links, i + 1)
                    for s in range(S):
                        tail[s].dve_stats(dve, links[s], i, i * S + s)
                        links[s].close()
                    for s in range(S):
                        tail[s].dve_norm(dve, i)


def _rope_table(n_t, dim):
    import numpy as np
    inv = (1.0 / (10000.0 ** (np.arange(0, dim, 2, dtype=np.float32) / np.float32(dim)))).astype(np.float32)
    f = np.arange(n_t, dtype=np.float32)[:, None] * inv[None, :]
    return np.cos(f).astype(np.float32), np.sin(f).astype(np.float32)


def layout(inp):
    import numpy as np
    a = {}
    f = {k: np.asarray(v) for k, v in inp.items()}
    x = f["L0_attn_x"].reshape(NTOK, D)
    a["x"], a["xt"] = x, np.ascontiguousarray(x.T)
    a["ident"] = np.eye(P, dtype=np.float32)
    a["one_row"] = np.ones((1, P), np.float32)
    H, DH, DL = 16, 8, 32
    swap = np.arange(D).reshape(H, 2, DH // 2)[:, ::-1, :].reshape(-1)
    wq, wd = f["L0_attn_Wq"], f["L0_attn_Wdown"]
    a["a0_w"] = np.concatenate([wq, wq[:, swap], wd], 1)
    wup = f["L0_attn_Wup"].reshape(DL, H, 2 * DH)
    wk, wv = wup[:, :, :DH].reshape(DL, D), wup[:, :, DH:].reshape(DL, D)
    a["a0_up"] = np.concatenate([wk, wk[:, swap], wv], 1)
    a["a0_wout"], a["a0_bout"] = f["L0_attn_Wout"], f["L0_attn_bout"][None]
    bup, bq = f["L0_attn_bup"].reshape(H, 2 * DH), f["L0_attn_bq"]
    bk, bvv = bup[:, :DH].reshape(-1), bup[:, DH:].reshape(-1)
    vec = np.zeros((P, 6), np.float32)
    vec[:DL, 2] = f["L0_attn_bdown"]
    for n, b in ((0, bq), (1, bq[swap]), (3, bk), (4, bk[swap]), (5, bvv)):
        vec[:, n] = b
    a["a0_vec"] = vec
    cos, sin = _rope_table(T, DH)
    i = np.arange(D) % (DH // 2)
    sign = np.where(np.arange(D) % DH < DH // 2, -1, 1).astype(np.float32)
    a["a0_cs"] = np.concatenate([cos[:, i].T, sin[:, i].T * sign[:, None]], 1)
    def second(w):
        n, h, d = w.shape
        return w.reshape(n, h // P, P, d).transpose(0, 2, 1, 3).reshape(n * P, -1)

    for tag in ("f0", "f1", "f2"):
        a[tag + "_rank"] = np.broadcast_to(np.arange(8, 0, -1).astype(np.float32), (P, 8))
        a[tag + "_ones"] = np.ones((2, P), np.float32)
    wide = np.zeros((3, P, P), np.float32)
    wide[0, :32, :8], wide[1, :, :8], wide[2, :, :8] = f["L0_ffn_wg2"], f["L1_ffn_centroids"], f["L2_ffn_gate_w"].T
    a["f0_wr"], a["f0_wg2"], a["f0_bg1"] = f["L0_ffn_wg1"], wide[0, :32], f["L0_ffn_bg1"][:, None]
    a["f0_w1"], a["f0_w2"] = f["L0_ffn_w_in"].reshape(8 * D, -1), second(f["L0_ffn_w_out"])
    cat = np.concatenate
    a["f1_wr"], a["f2_wr"] = wide[1], wide[2]
    a["f1_w1"] = cat([f["L1_ffn_W1_s"], f["L1_ffn_W1_r"]]).reshape(10 * D, -1)
    a["f1_w2"] = second(cat([f["L1_ffn_W2_s"], f["L1_ffn_W2_r"]]))
    a["f1_b1"] = cat([f["L1_ffn_b1_s"], f["L1_ffn_b1_r"]]).reshape(-1, P).T
    a["f1_b2"] = cat([f["L1_ffn_b2_s"], f["L1_ffn_b2_r"]])
    a["f1_gs"] = np.stack([f["L1_ffn_g_shared"]] * 2 + [f["L1_ffn_g_routed"]] * 8, 1)
    a["f2_w1"] = cat([f["L2_ffn_shared_w1"][None], f["L2_ffn_experts_w1"]]).transpose(0, 2, 1).reshape(9 * D, -1)
    a["f2_w2"] = second(cat([f["L2_ffn_shared_w2"][None], f["L2_ffn_experts_w2"]]).transpose(0, 2, 1))
    swap = np.arange(1024).reshape(-1, 2)[:, ::-1].reshape(-1)
    uq, uk, uv = (f[f"L1_attn_w_up_{n}"] for n in "qkv")
    a["a1_wd"] = cat([f["L1_attn_w_down_q"], f["L1_attn_w_down_kv"]]).T
    a["a1_up"] = cat([cat([uq.T, uq[swap].T, np.zeros((64, 3072), np.float32)], 1),
                      cat([np.zeros((64, 2048), np.float32), uk.T, uk[swap].T, uv.T], 1)])
    a["a1_wout"] = f["L1_attn_w_out"].T.reshape(8, P, D).transpose(1, 0, 2)
    a["a1_ln"] = np.stack([f["L1_attn_ln_scale"], f["L1_attn_ln_bias"]], 1)
    inv = 1.0 / 10000.0 ** (np.arange(0, 64, 2, dtype=np.float32) / 64)
    freqs = np.outer(np.arange(T, dtype=np.float32), inv)
    pair = np.arange(P) % 64 // 2
    tabs = [cat([g_(freqs), g_(freqs)], -1)[:, ::2][:, pair].T.astype(np.float32) for g_ in (np.cos, np.sin)]
    tabs[1] = tabs[1] * np.where(np.arange(P) % 2 == 0, -1, 1).astype(np.float32)[:, None]
    a["a1_cs"] = cat(tabs, 1)
    a["a1_sel"] = np.repeat(np.eye(P, 16, dtype=np.float32), P, 1)
    a["m2_w"] = f["L2_attn_in_proj_w"].T
    xpw = f["L2_attn_x_proj_w"].T.reshape(2, P, 40)
    xp = np.zeros((P, 2, P), np.float32)
    for k in range(2):
        xp[:, k, 0:32] = xp[:, k, 32:64] = xpw[k][:, 8:40]
        xp[:, k, 64:72] = xpw[k][:, 0:8]
    dtw = np.zeros((P, 256), np.float32)
    dtw[64:72] = f["L2_attn_dt_proj_w"].T
    sel = np.zeros((64, 32, P), np.float32)
    for n in range(32):
        sel[n, n] = sel[32 + n, n] = 1
    halves = lambda w: w.reshape(2, P, -1).transpose(1, 0, 2)
    a["m2_xp"], a["m2_dt"], a["m2_sel"] = xp, dtw, sel.reshape(64, -1)
    a["m2_out"], a["m2_cw"], a["m2_alog"] = halves(f["L2_attn_out_proj_w"].T), halves(f["L2_attn_conv_w"]), halves(f["L2_attn_A_log"])
    a["m2_cvec"] = halves(np.stack([f["L2_attn_conv_b"], f["L2_attn_dt_proj_b"], f["L2_attn_D"]], 1))
    def rows(w):
        w = cat([w, np.zeros((384 - w.shape[0], D), np.float32)])
        return w.reshape(3, P, D).transpose(1, 0, 2).reshape(P, -1)

    wd = cat([f["L3_ffn_w_down"], np.zeros((D, 384 - 352), np.float32)], 1)
    a["f3_w"] = cat([rows(f["L3_ffn_w_gate"]), rows(f["L3_ffn_w_up"]), wd], 1)
    a["a3_w"] = cat([f["L3_attn_Wq"].T, f["L3_attn_Wk"].T, f["L3_attn_Wv"].T], 1)
    a["a3_wo"], a["a3_bo"] = f["L3_attn_Wo"].T, f["L3_attn_bo"][None]
    a["a3_vec"] = np.stack([f["L3_attn_bq"], f["L3_attn_bk"], f["L3_attn_bv"]], 1)
    a["a3_heads"] = np.kron(np.eye(16, dtype=np.float32), np.ones((8, 8), np.float32))
    return {k: np.ascontiguousarray(v) for k, v in a.items()}


def kernel(**inputs):
    import numpy as np
    import concourse.bacc as bacc
    from concourse.bass_utils import run_bass_kernel_spmd as run

    nc = bacc.Bacc("TRN2", target_bir_lowering=False, num_devices=1)
    arrays = {f"in_{k}": v for k, v in layout(inputs).items()}
    ins = {k[3:]: nc.dram_tensor(k, v.shape, mybir.dt.from_np(v.dtype), kind="ExternalInput").ap()
           for k, v in arrays.items()}
    out = nc.dram_tensor("out_0", (NTOK, D), F32, kind="ExternalOutput").ap()
    Program(nc, ins, out).build()
    r = run(nc, [arrays], core_ids=[0])
    return r.results[0]["out_0"].reshape(B, T, D)
```
